# Optimizing a Trainium2 kernel written in Bass

```python
import numpy as np
import jax
import jax.numpy as jnp

def _softmax(x, axis=-1):
    return jax.nn.softmax(x, axis=axis)

def _gelu(x):
    return jax.nn.gelu(x, approximate=True)

def _silu(x):
    return jax.nn.silu(x)

def _sigmoid(x):
    return jax.nn.sigmoid(x)

def _layernorm(x, axis=-1, eps=1e-05):
    m = jnp.mean(x, axis=axis, keepdims=True)
    v = jnp.var(x, axis=axis, keepdims=True)
    return (x - m) / jnp.sqrt(v + eps)

def _scatter_add(tgt, idx, src, axis=0):
    return tgt.at[idx].add(src)

def _segment_sum(src, seg, n):
    return jax.ops.segment_sum(src, seg, n)
kernel_name = 'mk_metaformer_d1_conv_nchw512_r2_175e06'

def setup_inputs(seed: int=0):
    np.random.seed(seed)
    _w = jnp.asarray

    def _rec_inputs():
        import jax
        import jax.numpy as jnp
        _gk = jax.random.key(seed)
        x = -0.0002928 + 1 * jax.random.normal(jax.random.fold_in(_gk, 1), (2, 256, 32, 32), jnp.float32)
        return x
    x = _rec_inputs()

    def _L0_conv_setup():
        import jax, jax.numpy as jnp
        import numpy as np
        B, C, H, W = (2, 256, 32, 32)
        TC = 128

        def _w(k, o, i):
            return jax.random.normal(k, (o, i), jnp.float32) * (1.0 / np.sqrt(i))

        def _proj(x, w, g, b):
            y = jnp.einsum('oc,bcn->bon', w, x)
            return jax.nn.relu(y * g[None, :, None] + b[None, :, None])
        key = jax.random.key(seed)
        ks = jax.random.split(key, 8)
        ones = lambda n: jnp.ones((n,), jnp.float32)
        zeros = lambda n: jnp.zeros((n,), jnp.float32)
        return {'x': jax.random.normal(ks[0], (B, C, H, W), jnp.float32), 'q_w1': _w(ks[1], TC, C), 'q_g1': ones(TC), 'q_b1': zeros(TC), 'q_w2': _w(ks[2], TC, TC), 'q_g2': ones(TC), 'q_b2': zeros(TC), 'k_w1': _w(ks[3], TC, 2 * C), 'k_g1': ones(TC), 'k_b1': zeros(TC), 'k_w2': _w(ks[4], TC, TC), 'k_g2': ones(TC), 'k_b2': zeros(TC), 'v_w': _w(ks[5], TC, 2 * C), 'v_g': ones(TC), 'v_b': zeros(TC), 'o_w': _w(ks[6], C, TC), 'o_g': ones(C), 'o_b': zeros(C)}
    _L0_conv_all = _L0_conv_setup()
    _L0_conv_in = {k: v for k, v in _L0_conv_all.items() if k in ('q_w1', 'q_g1', 'q_b1', 'q_w2', 'q_g2', 'q_b2', 'k_w1', 'k_g1', 'k_b1', 'k_w2', 'k_g2', 'k_b2', 'v_w', 'v_g', 'v_b', 'o_w', 'o_g', 'o_b')}
    del _L0_conv_all

    def _L0_ffn_setup():
        import jax, jax.numpy as jnp
        import numpy as np
        B, L, D, H, E, K = (8, 4096, 256, 1024, 8, 2)
        SCALE = 0.02
        key = jax.random.key(seed)
        ks = jax.random.split(key, 6)
        return {'x': jax.random.normal(ks[0], (B, L, D), dtype=jnp.float32), 'Wg': jax.random.normal(ks[1], (D, E), dtype=jnp.float32) * SCALE, 'W1': jax.random.normal(ks[2], (E, D, H), dtype=jnp.float32) * SCALE, 'b1': jax.random.normal(ks[3], (E, H), dtype=jnp.float32) * SCALE, 'W2': jax.random.normal(ks[4], (E, H, D), dtype=jnp.float32) * SCALE, 'b2': jax.random.normal(ks[5], (E, D), dtype=jnp.float32) * SCALE}
    _L0_ffn_all = _L0_ffn_setup()
    _L0_ffn_in = {k: v for k, v in _L0_ffn_all.items() if k in ('Wg', 'W1', 'b1', 'W2', 'b2')}
    del _L0_ffn_all
    return {'x': x, 'L0_conv_q_w1': _L0_conv_in['q_w1'], 'L0_conv_q_g1': _L0_conv_in['q_g1'], 'L0_conv_q_b1': _L0_conv_in['q_b1'], 'L0_conv_q_w2': _L0_conv_in['q_w2'], 'L0_conv_q_g2': _L0_conv_in['q_g2'], 'L0_conv_q_b2': _L0_conv_in['q_b2'], 'L0_conv_k_w1': _L0_conv_in['k_w1'], 'L0_conv_k_g1': _L0_conv_in['k_g1'], 'L0_conv_k_b1': _L0_conv_in['k_b1'], 'L0_conv_k_w2': _L0_conv_in['k_w2'], 'L0_conv_k_g2': _L0_conv_in['k_g2'], 'L0_conv_k_b2': _L0_conv_in['k_b2'], 'L0_conv_v_w': _L0_conv_in['v_w'], 'L0_conv_v_g': _L0_conv_in['v_g'], 'L0_conv_v_b': _L0_conv_in['v_b'], 'L0_conv_o_w': _L0_conv_in['o_w'], 'L0_conv_o_g': _L0_conv_in['o_g'], 'L0_conv_o_b': _L0_conv_in['o_b'], 'L0_ffn_Wg': _L0_ffn_in['Wg'], 'L0_ffn_W1': _L0_ffn_in['W1'], 'L0_ffn_b1': _L0_ffn_in['b1'], 'L0_ffn_W2': _L0_ffn_in['W2'], 'L0_ffn_b2': _L0_ffn_in['b2']}

def reference(x, L0_conv_q_w1, L0_conv_q_g1, L0_conv_q_b1, L0_conv_q_w2, L0_conv_q_g2, L0_conv_q_b2, L0_conv_k_w1, L0_conv_k_g1, L0_conv_k_b1, L0_conv_k_w2, L0_conv_k_g2, L0_conv_k_b2, L0_conv_v_w, L0_conv_v_g, L0_conv_v_b, L0_conv_o_w, L0_conv_o_g, L0_conv_o_b, L0_ffn_Wg, L0_ffn_W1, L0_ffn_b1, L0_ffn_W2, L0_ffn_b2):
    import jax
    import jax.numpy as jnp

    def _L0_conv_ref(x, q_w1, q_g1, q_b1, q_w2, q_g2, q_b2, k_w1, k_g1, k_b1, k_w2, k_g2, k_b2, v_w, v_g, v_b, o_w, o_g, o_b):
        import jax, jax.numpy as jnp
        import numpy as np
        B, C, H, W = (2, 256, 32, 32)
        TC = 128

        def _w(k, o, i):
            return jax.random.normal(k, (o, i), jnp.float32) * (1.0 / np.sqrt(i))

        def _proj(x, w, g, b):
            y = jnp.einsum('oc,bcn->bon', w, x)
            return jax.nn.relu(y * g[None, :, None] + b[None, :, None])
        b, c, h, w = x.shape
        n = h * w
        xf = x.reshape(b, c, n)
        g_vec = jnp.mean(jax.nn.softmax(xf, axis=2) * xf, axis=2)
        g_map = jnp.broadcast_to(g_vec[:, :, None], (b, c, n))
        kv_in = jnp.concatenate([g_map, xf], axis=1)
        q = _proj(_proj(xf, q_w1, q_g1, q_b1), q_w2, q_g2, q_b2)
        k = _proj(_proj(kv_in, k_w1, k_g1, k_b1), k_w2, k_g2, k_b2)
        v = _proj(kv_in, v_w, v_g, v_b)
        tc = q.shape[1]
        sim = jnp.einsum('bcn,bcm->bnm', q, k) * tc ** (-0.5)
        attn = jax.nn.softmax(sim, axis=-1)
        ctx = jnp.einsum('bnm,bcm->bcn', attn, v)
        out = _proj(ctx, o_w, o_g, o_b)
        return out.reshape(b, -1, h, w)

    def _L0_ffn_ref(x, Wg, W1, b1, W2, b2):
        import jax, jax.numpy as jnp
        import numpy as np
        B, L, D, H, E, K = (8, 4096, 256, 1024, 8, 2)
        SCALE = 0.02
        b, l, d = x.shape
        xt = x.reshape(-1, d)
        T = xt.shape[0]
        gate = jax.nn.softmax(xt @ Wg, axis=-1)
        topv, topi = jax.lax.top_k(gate, K)
        topv = topv / (jnp.sum(topv, axis=-1, keepdims=True) + 1e-06)
        scores = jnp.zeros((T, E), dtype=xt.dtype).at[jnp.arange(T)[:, None], topi].set(topv)
        out = jnp.zeros_like(xt)
        for e in range(E):
            h = jax.nn.gelu(xt @ W1[e] + b1[e], approximate=False)
            ye = h @ W2[e] + b2[e]
            out = out + ye * scores[:, e:e + 1]
        return out.reshape(b, l, d)

    def _gn(v, G=32, eps=1e-05):
        B_, C_, H_, W_ = v.shape
        g = v.reshape(B_, G, C_ // G, H_, W_)
        m = jnp.mean(g, axis=(2, 3, 4), keepdims=True)
        s = jnp.var(g, axis=(2, 3, 4), keepdims=True)
        return ((g - m) / jnp.sqrt(s + eps)).reshape(v.shape)

    def _ln_c(v, eps=1e-06):
        m = jnp.mean(v, axis=1, keepdims=True)
        s = jnp.var(v, axis=1, keepdims=True)
        return (v - m) / jnp.sqrt(s + eps)

    def _ln_t(v, eps=1e-05):
        m = jnp.mean(v, axis=-1, keepdims=True)
        s = jnp.var(v, axis=-1, keepdims=True)
        return (v - m) / jnp.sqrt(s + eps)

    def _to_tokens(v):
        B_, C_, H_, W_ = v.shape
        return v.reshape(B_, C_, H_ * W_).transpose(0, 2, 1)

    def _from_tokens(t, like):
        B_, C_, H_, W_ = like.shape
        return t.transpose(0, 2, 1).reshape(B_, C_, H_, W_)
    x = x + _L0_conv_ref(_ln_c(x), L0_conv_q_w1, L0_conv_q_g1, L0_conv_q_b1, L0_conv_q_w2, L0_conv_q_g2, L0_conv_q_b2, L0_conv_k_w1, L0_conv_k_g1, L0_conv_k_b1, L0_conv_k_w2, L0_conv_k_g2, L0_conv_k_b2, L0_conv_v_w, L0_conv_v_g, L0_conv_v_b, L0_conv_o_w, L0_conv_o_g, L0_conv_o_b)
    t = _to_tokens(x)
    t = t + _L0_ffn_ref(_ln_t(t), L0_ffn_Wg, L0_ffn_W1, L0_ffn_b1, L0_ffn_W2, L0_ffn_b2)
    x = _from_tokens(t, x)
    return x

_drawn_inputs = setup_inputs


def setup_inputs(seed=0):
    import zlib

    import numpy as np

    out = dict(_drawn_inputs(seed))
    spreads = {'L0_conv_q_g1': (1.0, 0.6),
     'L0_conv_q_b1': (0.0, 0.8),
     'L0_conv_q_g2': (1.0, 0.6),
     'L0_conv_q_b2': (0.0, 0.8),
     'L0_conv_k_g1': (1.0, 0.6),
     'L0_conv_k_b1': (0.0, 0.8),
     'L0_conv_k_g2': (1.0, 0.6),
     'L0_conv_k_b2': (0.0, 0.8),
     'L0_conv_v_g': (1.0, 0.2),
     'L0_conv_v_b': (0.0, 0.1),
     'L0_conv_o_g': (1.0, 0.2),
     'L0_conv_o_b': (0.0, 0.1)}
    factors = {'L0_conv_q_w1': 8.0,
     'L0_conv_q_w2': 8.0,
     'L0_conv_k_w1': 8.0,
     'L0_conv_k_w2': 8.0,
     'L0_conv_v_w': 3.505,
     'L0_ffn_b1': 8.0,
     'L0_ffn_b2': 3.937}
    for name, (base, spread) in spreads.items():
        noise = np.random.default_rng([zlib.crc32(name.encode()), seed]).standard_normal(out[name].shape)
        drawn = base * np.exp(spread * noise) if base else spread * noise
        out[name] = jnp.asarray(drawn.astype(out[name].dtype))
    for name, factor in factors.items():
        out[name] = (out[name] * factor).astype(out[name].dtype)
    return out
```

```python
from contextlib import ExitStack

import concourse.bass as bass
from concourse import mybir

F32 = mybir.dt.float32
F32R = mybir.dt.float32r
I32 = mybir.dt.int32
U32 = mybir.dt.uint32
ALU = mybir.AluOpType
ACT = mybir.ActivationFunctionType
AX = mybir.AxisListType

P = 128
B, C, N = 2, 256, 1024
TC = 128
KC = C // P
TOK = B * N
NBLK = TOK // P
UNIT = 512
UNITS = TOK // UNIT
BLKU = UNIT // P
E, H = 8, 1024
HJ = H // P
TILE = 256
TMAX = TOK * 2 // TILE + 2 * E
NQ = (TMAX + 2) * TILE // P
RING = 4
WCOLS = KC * H + HJ * C
PIECE = WCOLS // HJ
SCALE = float(TC) ** -0.5
CHAN_EPS, TOK_EPS, GATE_EPS = 1e-6, 1e-5, 1e-6


def metaformer_kernel(nc, x_cn_d, x_tok_d, q1_d, q2_d, k1_d, k2_d, v_d, o_d, aff_d, og_d, ob_d,
                      wg_d, w1_d, b1_d, w2_d, b2_d, out_d):
    ctx = ExitStack()
    with ctx:
        def sb(name, shape, dt=F32, stack=ctx):
            return stack.enter_context(nc.sbuf_tensor(name, shape, dt))

        def sem(name):
            return ctx.enter_context(nc.semaphore(name))

        xs_d = nc.dram_tensor("xn_rows", (TOK, C), F32, kind="Internal").ap()

        ident = sb("ident", [P, P])
        avg = sb("avg", [P, P])
        ones = sb("ones", [P, P])
        upper = sb("upper", [P, P])
        iota_r = sb("iota_r", [P, P])
        iota_q = sb("iota_q", [P, NQ])
        iota_e = sb("iota_e", [P, E])
        iota_tile = sb("iota_tile", [P, E, HJ])
        token_id = sb("token_id", [P, NBLK])
        spare_row = sb("spare_row", [P, NQ])
        eps_c = sb("eps_c", [P, 1])
        eps_t = sb("eps_t", [P, 1])
        aff = sb("aff", [P, 10])
        w_g = sb("w_g", [P, KC, E])
        b1t = sb("b1t", [P, E * HJ])
        b2b = sb("b2b", [P, E * C])
        x1 = sb("x1", [P, NBLK, C])
        w_raw = [sb(f"w_raw{i}", [P, WCOLS]) for i in range(2)]

        with ExitStack() as s:
            x_cn = sb("x_cn", [P, KC, TOK], stack=s)
            sq = [sb(f"sq{i}", [P, KC, UNIT], stack=s) for i in range(2)]
            std = sb("std", [P, UNITS, UNIT], stack=s)
            q1r = [sb(f"q1r{i}", [P, UNIT], stack=s) for i in range(2)]
            k1r = [sb(f"k1r{i}", [P, UNIT], stack=s) for i in range(2)]
            vr = [sb(f"vr{i}", [P, UNIT], stack=s) for i in range(2)]
            q2r = [sb(f"q2r{i}", [P, UNIT], stack=s) for i in range(2)]
            k2r = [sb(f"k2r{i}", [P, UNIT], stack=s) for i in range(2)]
            w_q1 = sb("w_q1", [P, KC, TC], stack=s)
            w_q2 = sb("w_q2", [P, TC], stack=s)
            w_k1 = sb("w_k1", [P, 2 * KC, TC], stack=s)
            w_k2 = sb("w_k2", [P, TC], stack=s)
            w_v = sb("w_v", [P, 2 * KC, TC], stack=s)
            w_o = sb("w_o", [P, C], stack=s)
            og = sb("og", [P, C], stack=s)
            w_og = sb("w_og", [P, C], stack=s)
        with ExitStack() as s:
            pt_hi = [sb(f"pt_hi{i}", [P, N // P, UNIT], F32R, s) for i in range(2)]
            pt_lo = [sb(f"pt_lo{i}", [P, N // P, UNIT], F32R, s) for i in range(2)]
        s_w = ctx.enter_context(ExitStack())
        w_hi = [sb(f"w_hi{i}", [P, WCOLS], F32R, s_w) for i in range(2)]
        w_lo = [sb(f"w_lo{i}", [P, WCOLS], F32R, s_w) for i in range(2)]

        with ExitStack() as s:
            q_hi = sb("q_hi", [P, TOK], F32R, s)
            q_lo = sb("q_lo", [P, TOK], F32R, s)
            k_hi = sb("k_hi", [P, TOK], F32R, s)
            k_lo = sb("k_lo", [P, TOK], F32R, s)
            vt_hi = sb("vt_hi", [P, NBLK, TC], F32R, s)
            vt_lo = sb("vt_lo", [P, NBLK, TC], F32R, s)
            prob = [sb(f"prob{i}", [P, N], stack=s) for i in range(2)]
        with ExitStack() as s:
            xn2 = sb("xn2", [P, NBLK, C], stack=s)
            xt2 = [sb(f"xt2_{i}", [P, 2, KC, P], stack=s) for i in range(2)]
            hot_r = sb("hot_r", [P, 2 * NBLK, P], stack=s)
            hot_q = sb("hot_q", [P, 2 * NBLK, 2, NQ], stack=s)
        s_t = ctx.enter_context(ExitStack())
        h_raw = [sb(f"h_raw{i}", [P, TILE], stack=s_t) for i in range(RING)]
        h_hi = sb("h_hi", [P, HJ, TILE], F32R, s_t)
        h_lo = sb("h_lo", [P, HJ, TILE], F32R, s_t)
        x_hi = sb("x_hi", [P, KC, TILE], F32R, s_t)
        x_lo = sb("x_lo", [P, KC, TILE], F32R, s_t)
        xg = sb("xg", [P, 2, C], stack=s_t)
        y_sum = sb("y_sum", [P, 2, C], stack=s_t)
        y_out = sb("y_out", [P, 2, C], stack=s_t)
        pad = sb("pad", [P, 4 * TOK + 2 * NBLK * TC + 2 * N - (RING + 2 * HJ + 2 * KC) * TILE - 6 * C], stack=s_t)

        ctx_hi = [sb(f"ctx_hi{i}", [P, UNIT], F32R) for i in range(2)]
        ctx_lo = [sb(f"ctx_lo{i}", [P, UNIT], F32R) for i in range(2)]
        ob = sb("ob", [P, C])
        wo_hi = sb("wo_hi", [P, C], F32R)
        wo_lo = sb("wo_lo", [P, C], F32R)
        o_tmp = sb("o_tmp", [P, 2, C])
        gmax = sb("gmax", [P, B, KC])
        gsum = sb("gsum", [P, B, KC])
        gdot = sb("gdot", [P, B, KC])
        gvec = sb("gvec", [P, B, KC])
        kbias = sb("kbias", [P, B])
        vbias = sb("vbias", [P, B])
        rmax = sb("rmax", [P, NBLK])
        rneg = sb("rneg", [P, NBLK])
        rsum = sb("rsum", [P, NBLK])
        rinv = sb("rinv", [P, NBLK])
        bst = sb("bst", [P, NBLK, 6])
        mv = sb("mv", [P, NBLK, 2])
        tstd = sb("tstd", [P, NBLK])
        trstd = sb("trstd", [P, NBLK])
        lg = sb("lg", [P, NBLK, E])
        gate = sb("gate", [P, NBLK, E])
        g1 = sb("g1", [P, NBLK])
        g2 = sb("g2", [P, NBLK])
        top8 = sb("top8", [P, NBLK, E])
        idx8 = sb("idx8", [P, NBLK, E], U32)
        idxf = sb("idxf", [P, 2, NBLK])
        topg = sb("topg", [P, 2, NBLK])
        hot_e = sb("hot_e", [P, 2, NBLK, E])
        sel = sb("sel", [P, NBLK, E])
        base_a = sb("base_a", [P, NBLK, E])
        base_b = sb("base_b", [P, NBLK, E])
        count = sb("count", [P, E])
        over = sb("over", [P, E, HJ])
        tiles = sb("tiles", [P, E])
        start_a = sb("start_a", [P, E])
        start_b = sb("start_b", [P, E])
        start_i = sb("start_i", [1, E + 1], I32)
        pos3 = sb("pos3", [P, 2, NBLK, E])
        posf = sb("posf", [P, 2, NBLK])
        posi = sb("posi", [P, 2, NBLK], I32)
        qi = sb("qi", [P, 2, NBLK], I32)
        ri = sb("ri", [P, 2, NBLK], I32)
        qf = sb("qf", [P, 2, NBLK])
        rf = sb("rf", [P, 2, NBLK])
        slot_id = sb("slot_id", [P, NQ])
        slot_gate = sb("slot_gate", [P, NQ])
        row_f = sb("row_f", [P, NQ])
        empty = sb("empty", [P, NQ])
        row_in = sb("row_in", [P, NQ], U32)
        row_out = sb("row_out", [P, NQ], U32)
        idx_in = sb("idx_in", [P, 2], U32)
        idx_out = sb("idx_out", [P, 2], U32)

        banks = ctx.enter_context(nc.psum_tensor("banks", [P, 8, 512], F32))

        x_loaded = [sem(f"x_loaded{u}") for u in range(UNITS)]
        conv_loaded = sem("conv_loaded")
        xtok_loaded = sem("xtok_loaded")
        bias_loaded = sem("bias_loaded")
        w_loaded = [sem(f"w_loaded{i}") for i in range(2)]
        consts_made = sem("consts_made")
        pool_step = sem("pool_step")
        dve_step = sem("dve_step")
        act_step = sem("act_step")
        mean_ready = sem("mean_ready")
        centred = sem("centred")
        sq_ready = sem("sq_ready")
        var_ready = sem("var_ready")
        std_ready = sem("std_ready")
        normed = sem("normed")
        gmax_ready = sem("gmax_ready")
        gexp_ready = sem("gexp_ready")
        gvec_ready = sem("gvec_ready")
        gproj_ready = sem("gproj_ready")
        gbias_ready = sem("gbias_ready")
        proj_ready = sem("proj_ready")
        proj_out = sem("proj_out")
        q_split = sem("q_split")
        k_split = sem("k_split")
        vt_ready = sem("vt_ready")
        vt_hi_done = sem("vt_hi_done")
        vt_split = sem("vt_split")
        wo_split = sem("wo_split")
        s_ready = sem("s_ready")
        rmax_ready = sem("rmax_ready")
        exp_done = sem("exp_done")
        t_ready = sem("t_ready")
        pt_hi_done = sem("pt_hi_done")
        pt_split = sem("pt_split")
        pv_ready = sem("pv_ready")
        ctx_hi_done = sem("ctx_hi_done")
        ctx_split = sem("ctx_split")
        o_ready = sem("o_ready")
        o_taken = sem("o_taken")
        x1_ready = sem("x1_ready")
        var2_ready = sem("var2_ready")
        std2_ready = sem("std2_ready")
        xn2_ready = sem("xn2_ready")
        xt_ready = sem("xt_ready")
        xt_copied = sem("xt_copied")
        lg_ready = sem("lg_ready")
        shifted = sem("shifted")
        expd = sem("expd")
        sel_ready = sem("sel_ready")
        rank_ready = sem("rank_ready")
        hot_ready = sem("hot_ready")
        inv_ready = sem("inv_ready")
        starts_ready = sem("starts_ready")
        slots_ready = sem("slots_ready")
        xs_stored = sem("xs_stored")
        x1_stored = sem("x1_stored")
        x_gathered = sem("x_gathered")
        idx_in_set = sem("idx_in_set")
        idx_out_set = sem("idx_out_set")
        xg_turned = sem("xg_turned")
        xhi_done = sem("xhi_done")
        x_split = sem("x_split")
        l1_ready = sem("l1_ready")
        gelu_done = sem("gelu_done")
        h_hi_done = sem("h_hi_done")
        h_split = sem("h_split")
        l2_done = sem("l2_done")
        y_taken = sem("y_taken")
        y_ready = sem("y_ready")
        y_added = sem("y_added")
        y_free = sem("y_free")
        gathers_begun = sem("gathers_begun")
        adds_begun = sem("adds_begun")
        whi_done = sem("whi_done")
        w_split = sem("w_split")

        block = ctx.enter_context(nc.Block())

        PROJ = []
        for b in range(B):
            u, w = 2 * b, 2 * b + 1
            PROJ += [("q1", u), ("q1", w), ("q2", u), ("q2", w), ("k1", u), ("v", u), ("k1", w),
                     ("v", w), ("k2", u), ("k2", w)]
        AT = {item: n for n, item in enumerate(PROJ)}
        GROUPS = NBLK // BLKU

        def load_expert(sp, e):
            raw = w_raw[e % 2]
            sp.dma_start(raw[:, 0:KC * H].rearrange("p (k h) -> p k h", k=KC),
                         w1_d[e].rearrange("(k p) h -> p k h", p=P)).then_inc(w_loaded[e % 2], 16)
            sp.dma_start(raw[:, KC * H:].rearrange("p (j d) -> p j d", j=HJ),
                         w2_d[e].rearrange("(j p) d -> p j d", p=P)).then_inc(w_loaded[e % 2], 16)

        @block.sync
        def _(sp):
            for u in range(UNITS):
                b, h = divmod(u, 2)
                sp.dma_start(x_cn[:, :, u * UNIT:(u + 1) * UNIT],
                             x_cn_d[b, :, h * UNIT:(h + 1) * UNIT].rearrange("(k p) n -> p k n", p=P)
                             ).then_inc(x_loaded[u], 16)
            for dst, src in ((w_q1, q1_d), (w_k1, k1_d), (w_v, v_d), (w_g, wg_d)):
                sp.dma_start(dst[:, :, :], src.rearrange("(k p) o -> p k o", p=P)).then_inc(conv_loaded, 16)
            for dst, src in ((w_q2, q2_d), (w_k2, k2_d), (w_o, o_d), (aff, aff_d),
                             (og, og_d.partition_broadcast(P)), (ob, ob_d.partition_broadcast(P))):
                sp.dma_start(dst[:, :], src).then_inc(conv_loaded, 16)
            sp.dma_start(x1[:, :, :], x_tok_d.rearrange("(i p) c -> p i c", p=P)).then_inc(xtok_loaded, 16)
            sp.dma_start(b1t[:, :], b1_d).then_inc(bias_loaded, 16)
            sp.dma_start(b2b[:, :], b2_d.partition_broadcast(P)).then_inc(bias_loaded, 16)
            for e in range(2):
                load_expert(sp, e)
            sp.wait_ge(x1_ready, NBLK)
            sp.dma_start(out_d[0:TOK, :].rearrange("(i p) c -> p i c", p=P), x1[:, :, :]).then_inc(x1_stored, 16)
            sp.dma_start(out_d[TOK:TOK + TILE, :].rearrange("(i p) c -> p i c", p=P),
                         x1[:, 0:2, :]).then_inc(x1_stored, 16)
            for g in range(GROUPS):
                sp.wait_ge(xn2_ready, BLKU * (g + 1))
                sp.dma_start(xs_d[g * UNIT:(g + 1) * UNIT, :].rearrange("(i p) c -> p i c", p=P),
                             xn2[:, g * BLKU:(g + 1) * BLKU, :]).then_inc(xs_stored, 16)
            for e in range(2, E):
                sp.wait_ge(w_split, HJ * (e - 1))
                load_expert(sp, e)

        @block.gpsimd
        def _(pool):
            pool.memset(ident[:, :], 0.0).then_inc(pool_step, 1)
            pool.memset(upper[:, :], 1.0).then_inc(pool_step, 1)
            pool.memset(avg[:, :], 1.0 / C).then_inc(consts_made, 1)
            pool.memset(ones[:, :], 1.0).then_inc(consts_made, 1)
            pool.memset(eps_c[:, :], CHAN_EPS).then_inc(consts_made, 1)
            pool.memset(eps_t[:, :], TOK_EPS).then_inc(consts_made, 1)
            pool.wait_ge(pool_step, 2)
            pool.affine_select(out=ident[:, :], in_=ident[:, :], compare_op=ALU.not_equal, fill=1.0, base=0,
                               pattern=[[-1, P]], channel_multiplier=1).then_inc(consts_made, 1)
            pool.affine_select(out=upper[:, :], in_=upper[:, :], compare_op=ALU.is_gt, fill=0.0, base=0,
                               pattern=[[1, P]], channel_multiplier=-1).then_inc(consts_made, 1)
            io = dict(allow_small_or_imprecise_dtypes=True)
            pool.iota(iota_r[:, :], [[1, P]], base=0, channel_multiplier=0, **io).then_inc(consts_made, 1)
            pool.iota(iota_q[:, :], [[1, NQ]], base=0, channel_multiplier=0, **io).then_inc(consts_made, 1)
            pool.iota(iota_e[:, :], [[1, E]], base=0, channel_multiplier=0, **io).then_inc(consts_made, 1)
            pool.iota(iota_tile[:, :, :], [[0, E], [TILE, HJ]], base=0, channel_multiplier=0, **io
                      ).then_inc(consts_made, 1)
            pool.iota(token_id[:, :], [[P, NBLK]], base=1, channel_multiplier=1, **io).then_inc(consts_made, 1)
            pool.iota(spare_row[:, :], [[0, NQ // 2], [P, 2]], base=TOK + 1, channel_multiplier=1, **io
                      ).then_inc(consts_made, 1)
            pool.wait_ge(pv_ready, GROUPS)
            pool.wait_ge(w_loaded[0], 32)
            for k in range(HJ):
                c = slice(k * PIECE, (k + 1) * PIECE)
                pool.tensor_copy(w_hi[0][:, c], w_raw[0][:, c]).then_inc(whi_done, 1)
                pool.wait_ge(whi_done, k + 1)
                pool.tensor_tensor(w_lo[0][:, c], w_raw[0][:, c], w_hi[0][:, c].bitcast(F32),
                                   ALU.subtract).then_inc(w_split, 1)

            def gather(t, n):
                pool.tensor_copy(idx_in[:, :], row_in[:, bass.ds(t * 2, 2)]).then_inc(idx_in_set, 1)
                pool.wait_ge(idx_in_set, n + 1)
                pool.sem_inc(gathers_begun, 1)
                for i in range(2):
                    pool.indirect_dma_start(xg[:, i, :], None, xs_d,
                                            bass.IndirectOffsetOnAxis(ap=idx_in[:, i:i + 1], axis=0)
                                            ).then_inc(x_gathered, 16)

            pool.wait_ge(slots_ready, 1)
            pool.wait_ge(xs_stored, 16 * GROUPS)
            gather(0, 0)
            pool.wait_ge(xg_turned, 1)
            gather(1, 1)
            pool.wait_ge(x1_stored, 32)

            def tile(t):
                pool.wait_ge(xg_turned, t + 2)
                pool.wait_ge(x_gathered, (t + 2) * 32)
                gather(t + 2, t + 2)
                pool.tensor_copy(idx_out[:, :], row_out[:, bass.ds(t * 2, 2)]).then_inc(idx_out_set, 1)
                pool.wait_ge(idx_out_set, t + 1)
                pool.wait_ge(y_ready, t * 2 + 2)
                pool.sem_inc(adds_begun, 1)
                for i in range(2):
                    pool.indirect_dma_start(out_d, bass.IndirectOffsetOnAxis(ap=idx_out[:, i:i + 1], axis=0),
                                            y_out[:, i, :], None, compute_op=ALU.add).then_inc(y_added, 16)
                pool.wait_ge(y_added, (t + 1) * 32)
                pool.sem_inc(y_free, 1)

            pool.sem_inc(y_free, 1)
            pool.wait_ge(starts_ready, 1)
            for e in range(E):
                t0 = pool.value_load(start_i[0:1, e:e + 1], min_val=0, max_val=TMAX)
                t1 = pool.value_load(start_i[0:1, e + 1:e + 2], min_val=2, max_val=TMAX)
                with pool.Fori(t0, t1) as t:
                    tile(t)
            t1 = pool.value_load(start_i[0:1, E:E + 1], min_val=2, max_val=TMAX)
            pool.wait_ge(x_gathered, (t1 + 2) * 32)

        @block.scalar
        def _(act):
            act.wait_ge(consts_made, 12)
            act.wait_ge(conv_loaded, 16 * 10)
            for u in range(UNITS):
                act.wait_ge(centred, u + 1)
                if u >= 2:
                    act.wait_ge(var_ready, u - 1)
                act.activation(sq[u % 2][:, :, :], x_cn[:, :, u * UNIT:(u + 1) * UNIT], ACT.Square
                               ).then_inc(sq_ready, 1)
            for u in range(UNITS):
                act.wait_ge(var_ready, u + 1)
                act.activation(std[:, u, :], banks[:, 4 + u, :], ACT.Sqrt, bias=eps_c[:, :]).then_inc(std_ready, 1)

            def take(kind, u):
                n = AT[kind, u]
                b = u // 2
                act.wait_ge(proj_ready, n + 1)
                if u >= 2:
                    if kind in ("q1", "k1"):
                        act.wait_ge(proj_ready, AT[kind[0] + "2", u - 2] + 1)
                    elif kind == "v":
                        act.wait_ge(vt_ready, u - 1)
                    else:
                        act.wait_ge(q_split if kind == "q2" else k_split, u - 1)
                dst = {"q1": q1r, "q2": q2r, "k1": k1r, "k2": k2r, "v": vr}[kind][u % 2]
                g = {"q1": 0, "q2": 2, "k1": 4, "k2": 6, "v": 8}[kind]
                bias = {"k1": kbias[:, b:b + 1], "v": vbias[:, b:b + 1]}.get(kind, aff[:, g + 1:g + 2])
                act.activation(dst[:, :], banks[:, n % 4, :], ACT.Relu, bias=bias, scale=aff[:, g:g + 1]
                               ).then_inc(proj_out, 1)

            def vt(u):
                act.wait_ge(vt_ready, u + 1)
                act.activation(vt_hi[:, u * BLKU:(u + 1) * BLKU, :],
                               banks[:, 5 + u % 2, :].rearrange("p (i c) -> p i c", i=BLKU), ACT.Copy
                               ).then_inc(vt_hi_done, 1)

            for b in range(B):
                u, w = 2 * b, 2 * b + 1
                for item in (("q1", u), ("q1", w), ("q2", u), ("q2", w)):
                    take(*item)
                act.wait_ge(gmax_ready, b + 1)
                for k in range(KC):
                    if b == 0:
                        act.wait_ge(var_ready, UNITS)
                    else:
                        act.wait_ge(gvec_ready, b)
                    act.activation(sq[k][:, :, :].rearrange("p h n -> p (h n)"), x_cn[:, k, b * N:(b + 1) * N], ACT.Exp, bias=gmax[:, b, k:k + 1],
                                   accum_out=gsum[:, b, k:k + 1]).then_inc(gexp_ready, 1)
                act.wait_ge(gbias_ready, b + 1)
                for item in (("k1", u), ("v", u), ("k1", w), ("v", w)):
                    take(*item)
                vt(u)
                take("k2", u)
                vt(w)
                take("k2", w)

            def exp_row(r):
                act.wait_ge(rmax_ready, r + 1)
                if r >= 2:
                    act.wait_ge(t_ready, 2 * (r - 1))
                act.activation(prob[r % 2][:, :].rearrange("p (h m) -> p h m", h=2),
                               banks[:, 2 * (r % 2):2 * (r % 2) + 2, :], ACT.Exp, bias=rneg[:, r:r + 1], scale=SCALE,
                               accum_out=rsum[:, r:r + 1]).then_inc(exp_done, 1)

            def pt_high(r, h):
                g, i = divmod(r, BLKU)
                act.wait_ge(t_ready, 2 * r + h + 1)
                if g >= 2:
                    act.wait_ge(pv_ready, g - 1)
                act.activation(pt_hi[g % 2][:, 4 * h:4 * h + 4, i * P:(i + 1) * P],
                               banks[:, 4 + h, :].rearrange("p (m n) -> p m n", m=4), ACT.Copy
                               ).then_inc(pt_hi_done, 1)

            act.wait_ge(k_split, UNITS)
            for step in range(NBLK + 6):
                if step < NBLK:
                    exp_row(step)
                if 1 <= step <= NBLK:
                    pt_high(step - 1, 0)
                    pt_high(step - 1, 1)
                if step >= 8 and step % 4 == 0:
                    g = step // 4 - 2
                    act.wait_ge(pv_ready, g + 1)
                    if g >= 2:
                        act.wait_ge(o_ready, 2 * (g - 1))
                    act.activation(ctx_hi[g % 2][:, :], banks[:, 6, :], ACT.Copy).then_inc(ctx_hi_done, 1)

            act.wait_ge(var2_ready, 1)
            act.activation(tstd[:, :], mv[:, :, 1], ACT.Sqrt, bias=eps_t[:, :]).then_inc(std2_ready, 1)
            for i in range(NBLK // 2):
                act.wait_ge(xt_ready, i + 1)
                if i >= 2:
                    act.wait_ge(lg_ready, i - 1)
                act.activation(xt2[i % 2][:, :, :, :],
                               banks[:, i % 4, :].rearrange("p (i k n) -> p i k n", i=2, k=KC), ACT.Copy
                               ).then_inc(xt_copied, 1)
            act.wait_ge(shifted, 1)
            act.activation(gate[:, :, :], lg[:, :, :], ACT.Exp).then_inc(expd, 1)

            def x_high(n):
                act.wait_ge(xg_turned, n + 1)
                act.activation(x_hi[:, :, :], banks[:, 6, :].rearrange("p (k n) -> p k n", k=KC), ACT.Copy
                               ).then_inc(xhi_done, 1)

            def tile(t, e, split):
                for j in range(HJ):
                    act.wait_ge(l1_ready, t * HJ + (j + 1))
                    act.wait_ge(h_split, t * HJ + (j + 1))
                    act.activation(h_raw[j % RING][:, :], banks[:, j % RING, 0:TILE], ACT.Gelu,
                                   bias=b1t[:, e * HJ + j:e * HJ + j + 1]).then_inc(gelu_done, 1)
                    if split and e + 1 < E:
                        if j == 0:
                            act.wait_ge(w_loaded[(e + 1) % 2], 32 * ((e + 1) // 2 + 1))
                            act.wait_ge(l2_done, t * HJ + HJ)
                        c = slice(j * PIECE, (j + 1) * PIECE)
                        act.activation(w_hi[(e + 1) % 2][:, c], w_raw[(e + 1) % 2][:, c], ACT.Copy
                                       ).then_inc(whi_done, 1)
                x_high(t + 1)

            act.sem_inc(gelu_done, RING)
            x_high(0)
            act.wait_ge(bias_loaded, 32)
            act.wait_ge(starts_ready, 1)
            for e in range(E):
                t0 = act.value_load(start_i[0:1, e:e + 1], min_val=0, max_val=TMAX)
                t1 = act.value_load(start_i[0:1, e + 1:e + 2], min_val=2, max_val=TMAX)
                tile(t0, e, True)
                with act.Fori(t0 + 1, t1) as t:
                    tile(t, e, False)

        @block.vector
        def _(dve):
            steps = [0]

            def then(ins):
                steps[0] += 1
                ins.then_inc(dve_step, 1)
                dve.wait_ge(dve_step, steps[0])

            dve.wait_ge(conv_loaded, 16 * 10)
            dve.wait_ge(consts_made, 12)
            for u in range(UNITS):
                c = x_cn[:, :, u * UNIT:(u + 1) * UNIT]
                dve.wait_ge(mean_ready, u + 1)
                dve.tensor_tensor(c, c, banks[:, u:u + 1, :].broadcast_to([P, KC, UNIT]), ALU.subtract
                                  ).then_inc(centred, 1)

            def norm(u):
                c = x_cn[:, :, u * UNIT:(u + 1) * UNIT]
                dve.wait_ge(std_ready, u + 1)
                then(dve.reciprocal(std[:, u, :], std[:, u, :]))
                dve.tensor_tensor(c, c, std[:, u:u + 1, :].broadcast_to([P, KC, UNIT]), ALU.mult
                                  ).then_inc(normed, 1)

            def global_max(b):
                dve.wait_ge(normed, 2 * b + 2)
                then(dve.tensor_reduce(gmax[:, b, :], x_cn[:, :, b * N:(b + 1) * N], AX.X, ALU.max))
                dve.tensor_scalar(gmax[:, b, :], gmax[:, b, :], -1.0, None, ALU.mult).then_inc(gmax_ready, 1)

            def global_vector(b):
                dve.wait_ge(gexp_ready, KC * (b + 1))
                for k in range(KC):
                    then(dve.scalar_tensor_tensor(sq[k][:, :, :].rearrange("p h n -> p (h n)"), sq[k][:, :, :].rearrange("p h n -> p (h n)"), 1.0 / N, x_cn[:, k, b * N:(b + 1) * N],
                                                  ALU.mult, ALU.mult, accum_out=gdot[:, b, k:k + 1]))
                then(dve.reciprocal(gsum[:, b, :], gsum[:, b, :]))
                dve.tensor_tensor(gvec[:, b, :], gdot[:, b, :], gsum[:, b, :], ALU.mult).then_inc(gvec_ready, 1)
                dve.wait_ge(gproj_ready, b + 1)
                dve.tensor_scalar(kbias[:, b:b + 1], banks[:, 4, 2 * b:2 * b + 1], aff[:, 4:5], aff[:, 5:6],
                                  ALU.mult, ALU.add).then_inc(dve_step, 1)
                dve.tensor_scalar(vbias[:, b:b + 1], banks[:, 4, 2 * b + 1:2 * b + 2], aff[:, 8:9], aff[:, 9:10],
                                  ALU.mult, ALU.add).then_inc(gbias_ready, 1)
                steps[0] += 1

            def split(kind, u, raw, hi, lo, done):
                dve.wait_ge(proj_out, AT[kind, u] + 1)
                c = slice(u * UNIT, (u + 1) * UNIT)
                then(dve.tensor_copy(hi[:, c], raw[u % 2][:, :]))
                dve.tensor_tensor(lo[:, c], raw[u % 2][:, :], hi[:, c].bitcast(F32), ALU.subtract).then_inc(done, 1)

            def vt_low(u):
                dve.wait_ge(vt_hi_done, u + 1)
                c = slice(u * BLKU, (u + 1) * BLKU)
                dve.tensor_tensor(vt_lo[:, c, :], banks[:, 5 + u % 2, :].rearrange("p (i c) -> p i c", i=BLKU),
                                  vt_hi[:, c, :].bitcast(F32), ALU.subtract).then_inc(vt_split, 1)

            norm(0)
            norm(1)
            global_max(0)
            norm(2)
            norm(3)
            then(dve.tensor_tensor(w_og[:, :], w_o[:, :], og[:, :], ALU.mult))
            then(dve.tensor_copy(wo_hi[:, :], w_og[:, :]))
            dve.tensor_tensor(wo_lo[:, :], w_og[:, :], wo_hi[:, :].bitcast(F32), ALU.subtract).then_inc(wo_split, 1)
            for b in range(B):
                if b:
                    global_max(b)
                global_vector(b)
                for u in (2 * b, 2 * b + 1):
                    split("q2", u, q2r, q_hi, q_lo, q_split)
                for u in (2 * b, 2 * b + 1):
                    vt_low(u)
                    split("k2", u, k2r, k_hi, k_lo, k_split)

            def row_max(r):
                dve.wait_ge(s_ready, r + 1)
                then(dve.tensor_reduce(rmax[:, r:r + 1], banks[:, 2 * (r % 2):2 * (r % 2) + 2, :], AX.XY, ALU.max))
                dve.tensor_scalar(rneg[:, r:r + 1], rmax[:, r:r + 1], -SCALE, None, ALU.mult).then_inc(rmax_ready, 1)

            def pt_low(r, h):
                g, i = divmod(r, BLKU)
                dve.wait_ge(pt_hi_done, 2 * r + h + 1)
                c = pt_hi[g % 2][:, 4 * h:4 * h + 4, i * P:(i + 1) * P]
                dve.tensor_tensor(pt_lo[g % 2][:, 4 * h:4 * h + 4, i * P:(i + 1) * P],
                                  banks[:, 4 + h, :].rearrange("p (m n) -> p m n", m=4), c.bitcast(F32),
                                  ALU.subtract).then_inc(pt_split, 1)

            def out_rows(g, pair):
                if pair == 0:
                    dve.wait_ge(exp_done, BLKU * (g + 1))
                    then(dve.reciprocal(rinv[:, g * BLKU:(g + 1) * BLKU], rsum[:, g * BLKU:(g + 1) * BLKU]))
                dve.wait_ge(o_ready, 2 * g + pair + 1)
                for i in range(2):
                    k = g * BLKU + 2 * pair + i
                    ins = dve.scalar_tensor_tensor(o_tmp[:, i, :], banks[:, 7, i * C:(i + 1) * C], rinv[:, k:k + 1],
                                                   ob[:, :], ALU.mult, ALU.add)
                    if i == 0:
                        ins.then_inc(dve_step, 1)
                        steps[0] += 1
                    else:
                        ins.then_inc(o_taken, 1)
                dve.wait_ge(o_taken, 2 * g + pair + 1)
                dve.wait_ge(dve_step, steps[0])
                for i in range(2):
                    k = g * BLKU + 2 * pair + i
                    dve.scalar_tensor_tensor(x1[:, k, :], o_tmp[:, i, :], 0.0, x1[:, k, :], ALU.max, ALU.add
                                             ).then_inc(x1_ready, 1)
                for i in range(2):
                    k = g * BLKU + 2 * pair + i
                    dve.wait_ge(x1_ready, k + 1)
                    then(dve.bn_stats(bst[:, k, :], x1[:, k, :]))
                    then(dve.bn_aggr(mv[:, k, :], bst[:, k, :]))

            dve.wait_ge(xtok_loaded, 16)
            for step in range(NBLK + 7):
                if step < NBLK:
                    row_max(step)
                if 1 <= step <= NBLK:
                    pt_low(step - 1, 0)
                    pt_low(step - 1, 1)
                if step >= 8 and step % 4 == 0:
                    g = step // 4 - 2
                    dve.wait_ge(ctx_hi_done, g + 1)
                    dve.tensor_tensor(ctx_lo[g % 2][:, :], banks[:, 6, :], ctx_hi[g % 2][:, :].bitcast(F32),
                                      ALU.subtract).then_inc(ctx_split, 1)
                if step >= 9 and step % 4 in (1, 2):
                    out_rows(step // 4 - 2, step % 4 - 1)

            dve.tensor_copy(trstd[:, 0:1], mv[:, 0:1, 1]).then_inc(var2_ready, 1)
            dve.wait_ge(std2_ready, 1)
            then(dve.reciprocal(trstd[:, :], tstd[:, :]))
            for i in range(NBLK):
                dve.tensor_scalar(xn2[:, i, :], x1[:, i, :], mv[:, i, 0:1], trstd[:, i:i + 1], ALU.subtract, ALU.mult
                                  ).then_inc(xn2_ready, 1)

            dve.wait_ge(lg_ready, NBLK // 2)
            lgp = banks[:, 4, 0:NBLK * E].rearrange("p (i e) -> p i e", e=E)
            spread = [P, NBLK, E]
            then(dve.tensor_reduce(g1[:, :], lgp, AX.X, ALU.max))
            dve.tensor_tensor(lg[:, :, :], lgp, g1[:, :].unsqueeze(2).broadcast_to(spread), ALU.subtract
                              ).then_inc(shifted, 1)
            dve.wait_ge(expd, 1)
            then(dve.tensor_reduce(g2[:, :], gate[:, :, :], AX.X, ALU.add))
            then(dve.reciprocal(g2[:, :], g2[:, :]))
            then(dve.tensor_tensor(gate[:, :, :], gate[:, :, :], g2[:, :].unsqueeze(2).broadcast_to(spread), ALU.mult))
            for i in range(NBLK):
                then(dve.max(top8[:, i, :], gate[:, i, :]))
                then(dve.max_index(idx8[:, i, :], top8[:, i, :], gate[:, i, :]))
            for k in range(2):
                then(dve.tensor_copy(idxf[:, k, :], idx8[:, :, k]))
            for k in range(2):
                then(dve.tensor_tensor(hot_e[:, k, :, :], iota_e[:, :].unsqueeze(1).broadcast_to(spread),
                                       idxf[:, k, :].unsqueeze(2).broadcast_to(spread), ALU.is_equal))
            dve.tensor_tensor(sel[:, :, :], hot_e[:, 0, :, :], hot_e[:, 1, :, :], ALU.add).then_inc(sel_ready, 1)
            then(dve.tensor_tensor(g1[:, :], top8[:, :, 0], top8[:, :, 1], ALU.add))
            then(dve.tensor_scalar(g1[:, :], g1[:, :], GATE_EPS, None, ALU.add))
            then(dve.reciprocal(g1[:, :], g1[:, :]))
            for k in range(2):
                then(dve.tensor_tensor(topg[:, k, :], top8[:, :, k], g1[:, :], ALU.mult))
            dve.wait_ge(rank_ready, 1)
            total = banks[:, 6, 0:NBLK * E].rearrange("p (i e) -> p i e", e=E)
            then(dve.tensor_copy(base_a[:, :, :], total))
            src, dst = base_a, base_b
            for sh in (1, 2, 4, 8):
                then(dve.tensor_copy(dst[:, 0:sh, :], src[:, 0:sh, :]))
                then(dve.tensor_tensor(dst[:, sh:, :], src[:, sh:, :], src[:, :NBLK - sh, :], ALU.add))
                src, dst = dst, src
            then(dve.tensor_copy(count[:, :], src[:, NBLK - 1, :]))
            then(dve.tensor_tensor(over[:, :, :], count[:, :].unsqueeze(2).broadcast_to([P, E, HJ]),
                                   iota_tile[:, :, :], ALU.is_gt))
            then(dve.tensor_reduce(tiles[:, :], over[:, :, :], AX.X, ALU.add))
            then(dve.tensor_scalar(tiles[:, :], tiles[:, :], 2.0, None, ALU.max))
            then(dve.tensor_copy(start_a[:, :], tiles[:, :]))
            sa, sbf = start_a, start_b
            for sh in (1, 2, 4):
                then(dve.tensor_copy(sbf[:, 0:sh], sa[:, 0:sh]))
                then(dve.tensor_tensor(sbf[:, sh:], sa[:, sh:], sa[:, :E - sh], ALU.add))
                sa, sbf = sbf, sa
            then(dve.memset(start_i[0:1, 0:1], 0))
            dve.tensor_copy(start_i[0:1, 1:], sa[0:1, :]).then_inc(starts_ready, 1)
            then(dve.tensor_tensor(sbf[:, :], sa[:, :], tiles[:, :], ALU.subtract))
            then(dve.tensor_scalar(sbf[:, :], sbf[:, :], float(TILE), None, ALU.mult))
            then(dve.tensor_tensor(dst[:, :, :], src[:, :, :], total, ALU.subtract))
            then(dve.tensor_tensor(src[:, :, :], dst[:, :, :],
                                   banks[:, 5, 0:NBLK * E].rearrange("p (i e) -> p i e", e=E), ALU.add))
            then(dve.tensor_tensor(dst[:, :, :], src[:, :, :], sbf[:, :].unsqueeze(1).broadcast_to(spread), ALU.add))
            for k in range(2):
                then(dve.tensor_tensor(pos3[:, k, :, :], hot_e[:, k, :, :], dst[:, :, :], ALU.mult))
            then(dve.tensor_reduce(posf[:, :, :], pos3[:, :, :, :], AX.X, ALU.add))
            then(dve.tensor_copy(posi[:, :, :], posf[:, :, :]))
            then(dve.tensor_scalar(qi[:, :, :], posi[:, :, :], 7, None, ALU.logical_shift_right))
            then(dve.tensor_scalar(ri[:, :, :], posi[:, :, :], P - 1, None, ALU.bitwise_and))
            then(dve.tensor_copy(qf[:, :, :], qi[:, :, :]))
            then(dve.tensor_copy(rf[:, :, :], ri[:, :, :]))
            for k in range(2):
                for i in range(NBLK):
                    m = k * NBLK + i
                    dve.tensor_scalar(hot_r[:, m, :], iota_r[:, :], rf[:, k, i:i + 1], None, ALU.is_equal
                                      ).then_inc(hot_ready, 1)
                    dve.tensor_scalar(hot_q[:, m, 0, :], iota_q[:, :], qf[:, k, i:i + 1], token_id[:, i:i + 1],
                                      ALU.is_equal, ALU.mult).then_inc(hot_ready, 1)
                    dve.tensor_scalar(hot_q[:, m, 1, :], iota_q[:, :], qf[:, k, i:i + 1], topg[:, k, i:i + 1],
                                      ALU.is_equal, ALU.mult).then_inc(hot_ready, 1)
            dve.wait_ge(inv_ready, 1)
            then(dve.tensor_copy(slot_id[:, :], banks[:, 7, 0:NQ]))
            then(dve.tensor_copy(slot_gate[:, :], banks[:, 7, NQ:2 * NQ]))
            then(dve.tensor_scalar(row_f[:, :], slot_id[:, :], -1.0, 0.0, ALU.add, ALU.max))
            then(dve.tensor_copy(row_in[:, :], row_f[:, :]))
            then(dve.scalar_tensor_tensor(empty[:, :], slot_id[:, :], 0.0, spare_row[:, :], ALU.is_equal, ALU.mult))
            then(dve.scalar_tensor_tensor(row_f[:, :], slot_id[:, :], -1.0, empty[:, :], ALU.add, ALU.add))
            dve.tensor_copy(row_out[:, :], row_f[:, :]).then_inc(slots_ready, 1)

            def x_low(n):
                dve.wait_ge(xhi_done, n + 1)
                dve.tensor_tensor(x_lo[:, :, :], banks[:, 6, :].rearrange("p (k n) -> p k n", k=KC),
                                  x_hi[:, :, :].bitcast(F32), ALU.subtract).then_inc(x_split, 1)

            def tile(t, e, split):
                for j in range(HJ):
                    dve.wait_ge(gelu_done, t * HJ + (j + 1 + RING))
                    dve.wait_ge(l2_done, t * HJ + (j + 1))
                    dve.tensor_copy(h_hi[:, j, :], h_raw[j % RING][:, :]).then_inc(h_hi_done, 1)
                    dve.wait_ge(h_hi_done, t * HJ + (j + 1))
                    dve.tensor_tensor(h_lo[:, j, :], h_raw[j % RING][:, :], h_hi[:, j, :].bitcast(F32),
                                      ALU.subtract).then_inc(h_split, 1)
                    if split and e + 1 < E:
                        c = slice(j * PIECE, (j + 1) * PIECE)
                        dve.wait_ge(whi_done, HJ * (e + 1) + j + 1)
                        dve.tensor_tensor(w_lo[(e + 1) % 2][:, c], w_raw[(e + 1) % 2][:, c],
                                          w_hi[(e + 1) % 2][:, c].bitcast(F32), ALU.subtract).then_inc(w_split, 1)
                x_low(t + 1)
                dve.wait_ge(l2_done, t * HJ + 2 * HJ)
                for i in range(2):
                    dve.tensor_tensor(y_sum[:, i, :], banks[:, 4 + i, 0:C], b2b[:, e * C:(e + 1) * C], ALU.add
                                      ).then_inc(y_taken, 1)
                dve.wait_ge(y_free, t + 1)
                for i in range(2):
                    dve.wait_ge(y_taken, t * 2 + (2 + i + 1))
                    dve.tensor_scalar(y_out[:, i, :], y_sum[:, i, :], slot_gate[:, bass.ds(t * 2 + i, 1)], None, ALU.mult
                                      ).then_inc(y_ready, 1)

            dve.sem_inc(h_split, RING)
            dve.sem_inc(y_taken, 2)
            x_low(0)
            dve.wait_ge(bias_loaded, 32)
            for e in range(E):
                t0 = dve.value_load(start_i[0:1, e:e + 1], min_val=0, max_val=TMAX)
                t1 = dve.value_load(start_i[0:1, e + 1:e + 2], min_val=2, max_val=TMAX)
                tile(t0, e, True)
                with dve.Fori(t0 + 1, t1) as t:
                    tile(t, e, False)

        def logits(pe, i):
            pe.wait_ge(xt_copied, i + 1)
            for j in range(2):
                for k in range(KC):
                    ins = pe.matmul(banks[:, 4, (2 * i + j) * E:(2 * i + j + 1) * E], xt2[i % 2][:, j, k, :],
                                    w_g[:, k, :], start=k == 0, stop=k == KC - 1)
            ins.then_inc(lg_ready, 1)

        @block.tensor
        def _(pe):
            def product3(out, a_hi, a_lo, b_hi, b_lo, start, stop):
                pe.matmul(out, a_hi, b_hi, start=start, stop=False)
                pe.matmul(out, a_hi, b_lo, start=False, stop=False)
                return pe.matmul(out, a_lo, b_hi, start=False, stop=stop)

            pe.wait_ge(consts_made, 12)
            for u in range(UNITS):
                pe.wait_ge(x_loaded[u], 16)
                for k in range(KC):
                    ins = pe.matmul(banks[:, u, :], avg[:, :], x_cn[:, k, u * UNIT:(u + 1) * UNIT],
                                    start=k == 0, stop=k == KC - 1)
                ins.then_inc(mean_ready, 1)
            for u in range(UNITS):
                pe.wait_ge(sq_ready, u + 1)
                for k in range(KC):
                    ins = pe.matmul(banks[:, 4 + u, :], avg[:, :], sq[u % 2][:, k, :], start=k == 0, stop=k == KC - 1)
                ins.then_inc(var_ready, 1)

            pe.wait_ge(conv_loaded, 16 * 10)
            pe.wait_ge(centred, UNITS)

            def project(kind, u):
                n = AT[kind, u]
                if n >= 4:
                    pe.wait_ge(proj_out, n - 3)
                out = banks[:, n % 4, :]
                if kind in ("q2", "k2"):
                    src, w = (q1r, w_q2) if kind == "q2" else (k1r, w_k2)
                    pe.wait_ge(proj_out, AT[kind[0] + "1", u] + 1)
                    ins = pe.matmul(out, w[:, :], src[u % 2][:, :], start=True, stop=True)
                else:
                    w = {"q1": w_q1[:, :, :], "k1": w_k1[:, KC:, :], "v": w_v[:, KC:, :]}[kind]
                    pe.wait_ge(normed, u + 1)
                    for k in range(KC):
                        ins = pe.matmul(out, w[:, k, :], x_cn[:, k, u * UNIT:(u + 1) * UNIT],
                                        start=k == 0, stop=k == KC - 1)
                ins.then_inc(proj_ready, 1)

            def project_global(b):
                pe.wait_ge(gvec_ready, b + 1)
                if b:
                    pe.wait_ge(gbias_ready, b)
                else:
                    pe.wait_ge(std_ready, 1)
                for i, w in enumerate((w_k1, w_v)):
                    for k in range(KC):
                        ins = pe.matmul(banks[:, 4, 2 * b + i:2 * b + i + 1], w[:, k, :], gvec[:, b, k:k + 1],
                                        start=k == 0, stop=k == KC - 1)
                ins.then_inc(gproj_ready, 1)

            def turn_v(u):
                pe.wait_ge(proj_out, AT["v", u] + 1)
                if u >= 2:
                    pe.wait_ge(vt_split, u - 1)
                else:
                    pe.wait_ge(std_ready, UNITS)
                for i in range(BLKU):
                    ins = pe.transpose(banks[:, 5 + u % 2, i * P:(i + 1) * P], vr[u % 2][:, i * P:(i + 1) * P],
                                       ident[:, :])
                ins.then_inc(vt_ready, 1)

            for b in range(B):
                u, w = 2 * b, 2 * b + 1
                for item in (("q1", u), ("q1", w), ("q2", u), ("q2", w), ("k1", u), ("v", u)):
                    project(*item)
                project_global(b)
                project("k1", w)
                project("v", w)
                turn_v(u)
                project("k2", u)
                turn_v(w)
                project("k2", w)

            def scores(r):
                b, i = divmod(r, N // P)
                if r >= 2:
                    pe.wait_ge(exp_done, r - 1)
                if r % (N // P) == 0:
                    pe.wait_ge(q_split, 2 * b + 2)
                    pe.wait_ge(k_split, 2 * b + 2)
                qc = slice(r * P, (r + 1) * P)
                for h in range(2):
                    kc = slice(b * N + h * UNIT, b * N + (h + 1) * UNIT)
                    ins = product3(banks[:, 2 * (r % 2) + h, :], q_hi[:, qc], q_lo[:, qc], k_hi[:, kc], k_lo[:, kc],
                                   True, True)
                ins.then_inc(s_ready, 1)

            def turn(r):
                pe.wait_ge(exp_done, r + 1)
                for h in range(2):
                    if r:
                        pe.wait_ge(pt_split, 2 * (r - 1) + h + 1)
                    for m in range(4):
                        ins = pe.transpose(banks[:, 4 + h, m * P:(m + 1) * P],
                                           prob[r % 2][:, (4 * h + m) * P:(4 * h + m + 1) * P], ident[:, :])
                    ins.then_inc(t_ready, 1)

            def context(g, quarter):
                b = g // 2
                if quarter == 0:
                    pe.wait_ge(pt_split, 2 * BLKU * (g + 1))
                    if g:
                        pe.wait_ge(ctx_split, g)
                for m in (2 * quarter, 2 * quarter + 1):
                    ins = product3(banks[:, 6, :], vt_hi[:, b * 8 + m, :], vt_lo[:, b * 8 + m, :],
                                   pt_hi[g % 2][:, m, :], pt_lo[g % 2][:, m, :], m == 0, m == 7)
                if quarter == 3:
                    ins.then_inc(pv_ready, 1)

            def out_conv(g, pair):
                pe.wait_ge(ctx_split, g + 1)
                pe.wait_ge(wo_split, 1)
                if 2 * g + pair:
                    pe.wait_ge(o_taken, 2 * g + pair)
                for i in range(2):
                    c = slice((2 * pair + i) * P, (2 * pair + i + 1) * P)
                    ins = product3(banks[:, 7, i * C:(i + 1) * C], ctx_hi[g % 2][:, c], ctx_lo[g % 2][:, c],
                                   wo_hi[:, :], wo_lo[:, :], True, True)
                ins.then_inc(o_ready, 1)

            pe.wait_ge(proj_out, len(PROJ))
            pe.wait_ge(gbias_ready, B)
            pe.wait_ge(vt_split, UNITS)
            for step in range(NBLK + 7):
                if step < NBLK:
                    scores(step)
                if 1 <= step <= NBLK:
                    turn(step - 1)
                if 5 <= step < 5 + NBLK:
                    context((step - 5) // 4, (step - 5) % 4)
                if step >= 9 and step % 4 in (1, 2):
                    out_conv(step // 4 - 2, step % 4 - 1)

            for i in range(NBLK // 2):
                pe.wait_ge(xn2_ready, 2 * i + 2)
                if i >= 4:
                    pe.wait_ge(xt_copied, i - 3)
                for j in range(2):
                    for k in range(KC):
                        ins = pe.transpose(banks[:, i % 4, (KC * j + k) * P:(KC * j + k + 1) * P],
                                           xn2[:, 2 * i + j, k * P:(k + 1) * P], ident[:, :])
                ins.then_inc(xt_ready, 1)
                if i:
                    logits(pe, i - 1)
            logits(pe, NBLK // 2 - 1)
            pe.wait_ge(sel_ready, 1)
            pe.matmul(banks[:, 5, 0:NBLK * E], upper[:, :], sel[:, :, :].rearrange("p i e -> p (i e)"),
                      start=True, stop=True)
            pe.matmul(banks[:, 6, 0:NBLK * E], ones[:, :], sel[:, :, :].rearrange("p i e -> p (i e)"),
                      start=True, stop=True).then_inc(rank_ready, 1)
            for m in range(2 * NBLK):
                pe.wait_ge(hot_ready, 3 * (m + 1))
                ins = pe.matmul(banks[:, 7, 0:2 * NQ], hot_r[:, m, :], hot_q[:, m, :, :].rearrange("p v q -> p (v q)"),
                                start=m == 0, stop=m == 2 * NBLK - 1)
            ins.then_inc(inv_ready, 1)

            def turn_x(n):
                pe.wait_ge(x_gathered, (n + 1) * 32)
                for i in range(2):
                    for k in range(KC):
                        ins = pe.transpose(banks[:, 6, k * TILE + i * P:k * TILE + (i + 1) * P],
                                           xg[:, i, k * P:(k + 1) * P], ident[:, :])
                ins.then_inc(xg_turned, 1)

            def layer1(t, e, j):
                pe.wait_ge(gelu_done, t * HJ + (j + 1))
                for k in range(KC):
                    c = slice(k * H + j * P, k * H + (j + 1) * P)
                    ins = product3(banks[:, j % RING, 0:TILE], w_hi[e % 2][:, c], w_lo[e % 2][:, c], x_hi[:, k, :],
                                   x_lo[:, k, :], k == 0, k == KC - 1)
                ins.then_inc(l1_ready, 1)

            def layer2(t, e, j):
                pe.wait_ge(h_split, t * HJ + (j + 1 + RING))
                if j == 0:
                    pe.wait_ge(y_taken, t * 2 + 2)
                c = slice(KC * H + j * C, KC * H + (j + 1) * C)
                for i in range(2):
                    r = slice(i * P, (i + 1) * P)
                    ins = product3(banks[:, 4 + i, 0:C], h_hi[:, j, r], h_lo[:, j, r], w_hi[e % 2][:, c],
                                   w_lo[e % 2][:, c], j == 0, j == HJ - 1)
                ins.then_inc(l2_done, 1)

            def tile(t, e):
                pe.wait_ge(x_split, t + 1)
                for j in range(3):
                    layer1(t, e, j)
                for j in range(3, HJ):
                    layer2(t, e, j - 3)
                    layer1(t, e, j)
                layer2(t, e, HJ - 3)
                turn_x(t + 1)
                layer2(t, e, HJ - 2)
                layer2(t, e, HJ - 1)

            pe.sem_inc(l2_done, HJ)
            turn_x(0)
            for e in range(E):
                t0 = pe.value_load(start_i[0:1, e:e + 1], min_val=0, max_val=TMAX)
                t1 = pe.value_load(start_i[0:1, e + 1:e + 2], min_val=2, max_val=TMAX)
                pe.wait_ge(w_split, HJ * (e + 1))
                with pe.Fori(t0, t1) as t:
                    tile(t, e)


def kernel(**inputs):
    import numpy as np
    import concourse.bacc as bacc
    from concourse.bass_utils import run_bass_kernel_spmd

    a = {k.replace("L0_conv_", "").replace("L0_ffn_", ""): np.asarray(v) for k, v in inputs.items()}
    x = a["x"]
    shape = x.shape
    cn = np.ascontiguousarray(x.reshape(B, C, N))
    tok = np.ascontiguousarray(cn.transpose(0, 2, 1).reshape(TOK, C))
    aff = np.stack([a[n] for n in ("q_g1", "q_b1", "q_g2", "q_b2", "k_g1", "k_b1", "k_g2", "k_b2", "v_g", "v_b")],
                   axis=1)
    arrays = dict(
        x_cn=cn, x_tok=tok, q1=a["q_w1"].T, q2=a["q_w2"].T, k1=a["k_w1"].T, k2=a["k_w2"].T, v=a["v_w"].T,
        o=a["o_w"].T, aff=aff, og=a["o_g"], ob=a["o_b"], wg=a["Wg"], w1=a["W1"],
        b1=a["b1"].reshape(E, HJ, P).transpose(2, 0, 1).reshape(P, E * HJ), w2=a["W2"],
        b2=a["b2"].reshape(E * C))
    arrays = {f"in_{k}": np.ascontiguousarray(v) for k, v in arrays.items()}
    nc = bacc.Bacc("TRN2", target_bir_lowering=False, num_devices=1)
    args = [nc.dram_tensor(k, v.shape, mybir.dt.from_np(v.dtype), kind="ExternalInput").ap()
            for k, v in arrays.items()]
    out = nc.dram_tensor("out_rows", (TOK + TILE, C), F32, kind="ExternalOutput").ap()
    metaformer_kernel(nc, *args, out)
    rows = run_bass_kernel_spmd(nc, [arrays], core_ids=[0]).results[0]["out_rows"][:TOK]
    return np.ascontiguousarray(rows.reshape(B, N, C).transpose(0, 2, 1)).reshape(shape)
```

```python
from contextlib import ExitStack

import concourse.bass as bass
from concourse import mybir

F32 = mybir.dt.float32
F32R = mybir.dt.float32r
I32 = mybir.dt.int32
U32 = mybir.dt.uint32
ALU = mybir.AluOpType
ACT = mybir.ActivationFunctionType
AX = mybir.AxisListType

P = 128
B, C, N = 2, 256, 1024
TC = 128
KC = C // P
TOK = B * N
NBLK = TOK // P
UNIT = 512
UNITS = TOK // UNIT
BLKU = UNIT // P
E, H = 8, 1024
HJ = H // P
MBLK = TOK // P
LEAST = 2
BLOCKS = 2 * TOK // P + LEAST * E
TMAX = BLOCKS // 2
WIDE = 3
TILE = WIDE * P
TILES = TMAX + 3
SLOTS = TILES * WIDE
HALF = NBLK // 2
ROW = C + E
RING = 4
WCOLS = KC * H + HJ * C
PIECE = WCOLS // HJ
SCALE = float(TC) ** -0.5
CHAN_EPS, TOK_EPS, GATE_EPS = 1e-6, 1e-5, 1e-6


def metaformer_kernel(nc, x_cn_d, x_tok_d, q1_d, q2_d, k1_d, k2_d, v_d, o_d, aff_d, og_d, ob_d,
                      wg_d, w1_d, b1_d, w2_d, b2_d, out_d):
    ctx = ExitStack()
    with ctx:
        def sb(name, shape, dt=F32, stack=ctx):
            return stack.enter_context(nc.sbuf_tensor(name, shape, dt))

        def sem(name):
            return ctx.enter_context(nc.semaphore(name))

        xs_d = nc.dram_tensor("xn_rows", (TOK, ROW), F32, kind="Internal").ap()

        ident = sb("ident", [P, P])
        avg = sb("avg", [P, P])
        ones = sb("ones", [P, P])
        iota_r = sb("iota_r", [P, P])
        below = sb("below", [P, P])
        iota_e = sb("iota_e", [P, E])
        own = sb("own", [P, E])
        q_i = sb("q_i", [P, 1], I32)
        k_i = sb("k_i", [P, 2], I32)
        k_f = sb("k_f", [P, 2])
        k_one = sb("k_one", [P, 1])
        k_col = sb("k_col", [P, 1])
        k_move = sb("k_move", [P, 1])
        seg2 = sb("seg2", [P, 2, E + 1])
        seg = sb("seg", [P, E, HALF])
        token_id = sb("token_id", [P, NBLK])
        spare_row = sb("spare_row", [P, TILES, WIDE])
        eps_c = sb("eps_c", [P, 1])
        std = sb("std", [P, UNITS, BLKU])
        warm = sb("warm", [P, 1])
        aff = sb("aff", [P, 10])
        w_g = sb("w_g", [P, KC, E])
        b1t = sb("b1t", [P, E * HJ])
        x1 = sb("x1", [P, NBLK, C])
        xn2 = sb("xn2", [P, NBLK, ROW])
        w_raw0 = sb("w_raw0", [P, WCOLS])
        with ExitStack() as s:
            xt2 = sb("xt2", [P, NBLK, KC, P], stack=s)
        s_raw = ctx.enter_context(ExitStack())
        w_raw = [w_raw0, sb("w_raw1", [P, WCOLS], stack=s_raw)]

        with ExitStack() as s:
            x_cn = sb("x_cn", [P, KC, TOK], stack=s)
            sq = [sb(f"sq{i}", [P, KC, UNIT], stack=s) for i in range(2)]
            diag = [sb(f"diag{i}", [P, BLKU, P], stack=s) for i in range(2)]
            q1r = [sb(f"q1r{i}", [P, UNIT], stack=s) for i in range(2)]
            k1r = [sb(f"k1r{i}", [P, UNIT], stack=s) for i in range(2)]
            vr = [sb(f"vr{i}", [P, UNIT], stack=s) for i in range(2)]
            q2r = [sb(f"q2r{i}", [P, UNIT], stack=s) for i in range(2)]
            k2r = [sb(f"k2r{i}", [P, UNIT], stack=s) for i in range(2)]
            w_q1 = sb("w_q1", [P, KC, TC], stack=s)
            w_q2 = sb("w_q2", [P, TC], stack=s)
            w_k1 = sb("w_k1", [P, 2 * KC, TC], stack=s)
            w_k2 = sb("w_k2", [P, TC], stack=s)
            w_v = sb("w_v", [P, 2 * KC, TC], stack=s)
            w_o = sb("w_o", [P, C], stack=s)
            og = sb("og", [P, C], stack=s)
            w_og = sb("w_og", [P, C], stack=s)
        with ExitStack() as s:
            pt_hi = [sb(f"pt_hi{i}", [P, N // P, UNIT], F32R, s) for i in range(2)]
            pt_lo = [sb(f"pt_lo{i}", [P, N // P, UNIT], F32R, s) for i in range(2)]
        s_w = ctx.enter_context(ExitStack())
        w_hi = [sb(f"w_hi{i}", [P, WCOLS], F32R, s_w) for i in range(2)]
        w_lo = [sb(f"w_lo{i}", [P, WCOLS], F32R, s_w) for i in range(2)]

        with ExitStack() as s:
            qk = [[sb(f"{n}{b}", [P, N], F32R, s) for n in ("q_hi", "q_lo", "k_hi", "k_lo")] for b in range(B)]
            vt = [[sb(f"{n}{b}", [P, N // P, TC], F32R, s) for n in ("vt_hi", "vt_lo")] for b in range(B)]
            prob = [sb(f"prob{i}", [P, N], stack=s) for i in range(2)]
        with ExitStack() as s:
            hot_r = sb("hot_r", [P, 2, HALF, P], F32R, s)
            hot_q = sb("hot_q", [P, 2, HALF, P], F32R, s)
        s_t = ctx.enter_context(ExitStack())
        h_raw = [sb(f"h_raw{i}", [P, TILE], stack=s_t) for i in range(RING)]
        h_hi = sb("h_hi", [P, HJ, TILE], F32R, s_t)
        h_lo = sb("h_lo", [P, HJ, TILE], F32R, s_t)
        x_hi = sb("x_hi", [P, KC, TILE], F32R, s_t)
        x_lo = sb("x_lo", [P, KC, TILE], F32R, s_t)
        b2b = sb("b2b", [P, E * C], stack=s_t)
        pad = sb("pad", [P, 4 * TOK + 2 * NBLK * TC + 2 * N - (RING + 2 * HJ + 2 * KC) * TILE - E * C], stack=s_t)
        score_next = sb("score_next", [P, WIDE, E])
        score = sb("score", [P, WIDE, E])
        s_y = ExitStack()
        with s_y:
            ctx_hi = sb("ctx_hi", [P, UNIT], F32R, s_y)
            ctx_lo = sb("ctx_lo", [P, UNIT], F32R, s_y)
            o_tmp = sb("o_tmp", [P, 2, C], stack=s_y)
            wo_hi = sb("wo_hi", [P, C], F32R, s_y)
            wo_lo = sb("wo_lo", [P, C], F32R, s_y)
            ob = sb("ob", [P, C], stack=s_y)
        s_y2 = ctx.enter_context(ExitStack())
        y_sum = sb("y_sum", [P, WIDE, C], stack=s_y2)
        y_out = sb("y_out", [P, WIDE, C], stack=s_y2)
        xg = sb("xg", [P, WIDE, ROW], stack=s_y2)
        gmax = sb("gmax", [P, B, KC])
        gsum = sb("gsum", [P, B, KC])
        gdot = sb("gdot", [P, B, KC])
        gvec = sb("gvec", [P, B, KC])
        kbias = sb("kbias", [P, B])
        vbias = sb("vbias", [P, B])
        rmax = sb("rmax", [P, NBLK])
        rneg = sb("rneg", [P, NBLK])
        rsum = sb("rsum", [P, NBLK])
        rinv = sb("rinv", [P, NBLK])
        bst = sb("bst", [P, NBLK, 6])
        mv = sb("mv", [P, NBLK, 2])
        rv = sb("rv", [P, NBLK])
        rhv = sb("rhv", [P, NBLK])
        ri0 = sb("ri0", [P, NBLK], I32)
        rstd_i = sb("rstd_i", [P, NBLK], I32)
        rt = sb("rt", [P, NBLK])
        nmean = sb("nmean", [P, NBLK])
        nmr = sb("nmr", [P, NBLK])
        lg = sb("lg", [P, HALF, E])
        gate = sb("gate", [P, HALF, E])
        g1 = sb("g1", [P, HALF])
        top8 = sb("top8", [P, HALF, E])
        idx8 = sb("idx8", [P, HALF, E], U32)
        idxf = sb("idxf", [P, 2, HALF])
        topg = sb("topg", [P, 2, HALF])
        hot_e = sb("hot_e", [P, 2, HALF, E])
        scored = sb("scored", [P, 2, HALF, E])
        sel = sb("sel", [P, E, HALF])
        incl = sb("incl", [P, E, HALF])
        rank = sb("rank", [P, E, HALF])
        run = [sb(f"run{i}", [P, E]) for i in range(3)]
        blocks_i = sb("blocks_i", [P, 2, E], I32)
        parts_i = sb("parts_i", [P, 3, E], I32)
        parts = sb("parts", [P, 3, E + 1])
        before = sb("before", [P, 2, E + 1])
        odd_m = sb("odd_m", [P, E])
        scrap = sb("scrap", [P, 2, E])
        col_a = sb("col_a", [P, 1])
        col_z = sb("col_z", [P, 1])
        col_q = sb("col_q", [P, 1])
        place = sb("place", [P, SLOTS])
        starts = sb("starts", [1, 4, E + 1], I32)
        pos3 = sb("pos3", [P, 2, HALF, E])
        posf = sb("posf", [P, 2, HALF])
        posi = sb("posi", [P, 2, HALF], I32)
        qi = sb("qi", [P, 2, HALF], I32)
        ri = sb("ri", [P, 2, HALF], I32)
        qf = sb("qf", [P, 2, HALF])
        rf = sb("rf", [P, 2, HALF])
        slot_t = sb("slot_t", [P, P])
        empty = sb("empty", [P, TILES, WIDE])
        row_in = sb("row_in", [P, TILES, WIDE], U32)
        row_out = sb("row_out", [P, TILES, WIDE], U32)
        idx_in = sb("idx_in", [P, WIDE], U32)
        idx_out = sb("idx_out", [P, WIDE], U32)

        banks = ctx.enter_context(nc.psum_tensor("banks", [P, 8, 512], F32))

        x_loaded = [sem(f"x_loaded{u}") for u in range(UNITS)]
        conv_loaded = sem("conv_loaded")
        xtok_loaded = sem("xtok_loaded")
        bias_loaded = sem("bias_loaded")
        w_loaded = [sem(f"w_loaded{i}") for i in range(2)]
        consts_made = sem("consts_made")
        ones_made = sem("ones_made")
        pool_step = sem("pool_step")
        newton_step = sem("newton_step")
        guess_ready = sem("guess_ready")
        rq_ready = sem("rq_ready")
        dve_step = sem("dve_step")
        act_step = sem("act_step")
        mean_ready = sem("mean_ready")
        centred = sem("centred")
        sq_ready = sem("sq_ready")
        var_ready = sem("var_ready")
        std_ready = sem("std_ready")
        diag_ready = sem("diag_ready")
        rstd_ready = sem("rstd_ready")
        normed = sem("normed")
        gmax_ready = sem("gmax_ready")
        gexp_ready = sem("gexp_ready")
        gvec_ready = sem("gvec_ready")
        gproj_ready = sem("gproj_ready")
        gbias_ready = sem("gbias_ready")
        proj_ready = sem("proj_ready")
        proj_out = sem("proj_out")
        q_split = sem("q_split")
        k_split = sem("k_split")
        vt_ready = sem("vt_ready")
        vt_hi_done = sem("vt_hi_done")
        vt_split = sem("vt_split")
        wo_split = sem("wo_split")
        s_ready = sem("s_ready")
        rmax_ready = sem("rmax_ready")
        exp_done = sem("exp_done")
        t_ready = sem("t_ready")
        pt_hi_done = sem("pt_hi_done")
        pt_split = sem("pt_split")
        pv_ready = sem("pv_ready")
        ctx_hi_done = sem("ctx_hi_done")
        ctx_split = sem("ctx_split")
        o_ready = sem("o_ready")
        o_taken = sem("o_taken")
        x1_ready = sem("x1_ready")
        nmr_ready = sem("nmr_ready")
        xn2_ready = sem("xn2_ready")
        xt_ready = sem("xt_ready")
        xt_copied = sem("xt_copied")
        lg_ready = sem("lg_ready")
        shifted = sem("shifted")
        expd = sem("expd")
        scores_ready = sem("scores_ready")
        sel_ready = sem("sel_ready")
        rank_ready = sem("rank_ready")
        rank_taken = sem("rank_taken")
        hot_r_ready = sem("hot_r_ready")
        hot_q_ready = sem("hot_q_ready")
        inv_ready = sem("inv_ready")
        inv_taken = sem("inv_taken")
        place_ready = sem("place_ready")
        table_ready = sem("table_ready")
        starts_ready = sem("starts_ready")
        slots_ready = sem("slots_ready")
        xs_stored = sem("xs_stored")
        x1_stored = sem("x1_stored")
        x_gathered = sem("x_gathered")
        idx_in_set = sem("idx_in_set")
        idx_out_set = sem("idx_out_set")
        xg_turned = sem("xg_turned")
        xhi_done = sem("xhi_done")
        x_split = sem("x_split")
        l1_ready = sem("l1_ready")
        gelu_done = sem("gelu_done")
        h_split = sem("h_split")
        l2_done = sem("l2_done")
        y_taken = sem("y_taken")
        y_weighted = sem("y_weighted")
        scores_kept = sem("scores_kept")
        y_added = sem("y_added")
        gathers_begun = sem("gathers_begun")
        scores_begun = sem("scores_begun")
        scores_moved = sem("scores_moved")
        weights_begun = sem("weights_begun")
        adds_begun = sem("adds_begun")
        whi_done = sem("whi_done")
        w_split = sem("w_split")

        block = ctx.enter_context(nc.Block())

        PROJ = ([(kind, b + i) for b in (0, 2) for kind in ("q1", "q2") for i in range(2)]
                + [(kind, b + i) for b in (0, 2) for kind, i in
                   (("k1", 0), ("v", 0), ("k1", 1), ("v", 1), ("k2", 0), ("k2", 1))])
        AT = {item: n for n, item in enumerate(PROJ)}
        GROUPS = NBLK // BLKU
        CTX_BANK = [6, 6, 6, 0]
        O_BANK = [7, 7, 7, 7, 7, 1, 2, 3]
        XT_BANK = [7, 7, 7, 7, 5, 6, 0, 1]
        LG_BANK, RANK_BANK, INV_BANK, TABLE_BANK = (4, 2), (3, 5), 7, 6

        def expert_range(eng, e):
            t0 = eng.value_load(starts[0:1, 0, e:e + 1], min_val=0, max_val=TMAX)
            t1 = eng.value_load(starts[0:1, 0, e + 1:e + 2], min_val=1, max_val=TMAX)
            odd = eng.value_load(starts[0:1, 2, e:e + 1], min_val=0, max_val=1)
            more = eng.value_load(starts[0:1, 3, e:e + 1], min_val=0, max_val=1)
            return t0, t1, odd, more

        def load_expert(sp, e):
            raw = w_raw[e % 2]
            sp.dma_start(raw[:, 0:KC * H].rearrange("p (k h) -> p k h", k=KC),
                         w1_d[e].rearrange("(k p) h -> p k h", p=P)).then_inc(w_loaded[e % 2], 16)
            sp.dma_start(raw[:, KC * H:].rearrange("p (j d) -> p j d", j=HJ),
                         w2_d[e].rearrange("(j p) d -> p j d", p=P)).then_inc(w_loaded[e % 2], 16)

        @block.sync
        def _(sp):
            for u in range(UNITS):
                b, h = divmod(u, 2)
                sp.dma_start(x_cn[:, :, u * UNIT:(u + 1) * UNIT],
                             x_cn_d[b, :, h * UNIT:(h + 1) * UNIT].rearrange("(k p) n -> p k n", p=P)
                             ).then_inc(x_loaded[u], 16)
            for dst, src in ((w_q1, q1_d), (w_k1, k1_d), (w_v, v_d), (w_g, wg_d)):
                sp.dma_start(dst[:, :, :], src.rearrange("(k p) o -> p k o", p=P)).then_inc(conv_loaded, 16)
            for dst, src in ((w_q2, q2_d), (w_k2, k2_d), (w_o, o_d), (aff, aff_d),
                             (og, og_d.partition_broadcast(P)), (ob, ob_d.partition_broadcast(P))):
                sp.dma_start(dst[:, :], src).then_inc(conv_loaded, 16)
            sp.dma_start(x1[:, :, :], x_tok_d.rearrange("(i p) c -> p i c", p=P)).then_inc(xtok_loaded, 16)
            sp.dma_start(b1t[:, :], b1_d).then_inc(bias_loaded, 16)
            load_expert(sp, 0)
            sp.wait_ge(pv_ready, GROUPS)
            sp.dma_start(b2b[:, :], b2_d.partition_broadcast(P)).then_inc(bias_loaded, 16)
            def store_rows(half):
                sp.wait_ge(xn2_ready, HALF * (half + 1))
                sp.wait_ge(scores_ready, half + 1)
                sp.dma_start(xs_d[half * HALF * P:(half + 1) * HALF * P, :].rearrange("(i p) c -> p i c", p=P),
                             xn2[:, half * HALF:(half + 1) * HALF, :]).then_inc(xs_stored, 16)

            store_rows(0)
            sp.wait_ge(x1_ready, NBLK)
            sp.dma_start(out_d[0:TOK, :].rearrange("(i p) c -> p i c", p=P), x1[:, :, :]).then_inc(x1_stored, 16)
            store_rows(1)
            sp.wait_ge(lg_ready, NBLK // 2)
            load_expert(sp, 1)
            for e in range(2, E):
                sp.wait_ge(w_split, HJ * (e - 1))
                load_expert(sp, e)

        @block.gpsimd
        def _(pool):
            pool.memset(ident[:, :], 0.0).then_inc(pool_step, 1)
            pool.memset(below[:, :], -1.0).then_inc(pool_step, 1)
            pool.memset(avg[:, :], 1.0 / C).then_inc(consts_made, 1)
            pool.memset(eps_c[:, :], CHAN_EPS).then_inc(consts_made, 1)
            pool.wait_ge(pool_step, 2)
            pool.affine_select(out=ident[:, :], in_=ident[:, :], compare_op=ALU.not_equal, fill=1.0, base=0,
                               pattern=[[-1, P]], channel_multiplier=1).then_inc(consts_made, 1)
            pool.affine_select(out=below[:, :], in_=below[:, :], compare_op=ALU.is_ge, fill=0.0, base=0,
                               pattern=[[-1, P]], channel_multiplier=1).then_inc(consts_made, 1)
            io = dict(allow_small_or_imprecise_dtypes=True)
            pool.iota(iota_r[:, :], [[1, P]], base=0, channel_multiplier=0, **io).then_inc(consts_made, 1)
            pool.iota(iota_e[:, :], [[1, E]], base=0, channel_multiplier=0, **io).then_inc(consts_made, 1)
            pool.iota(q_i[:, :], [[0, 1]], base=0, channel_multiplier=1).then_inc(consts_made, 1)
            pool.memset(seg[:, :, :], 1.0).then_inc(pool_step, 1)
            pool.memset(seg2[:, :, :], 1.0).then_inc(pool_step, 1)
            pool.memset(own[:, :], 1.0).then_inc(pool_step, 1)
            pool.wait_ge(pool_step, 5)
            pool.memset(seg[:, :, 0:1], 0.0).then_inc(consts_made, 1)
            pool.memset(seg2[:, :, 0:1], 0.0).then_inc(consts_made, 1)
            pool.memset(parts[:, :, 0:1], 0.0).then_inc(consts_made, 1)
            pool.memset(starts[:, :, :], 0).then_inc(consts_made, 1)
            pool.affine_select(out=own[:, :], in_=own[:, :], compare_op=ALU.is_ge, fill=0.0, base=0,
                               pattern=[[-MBLK, E]], channel_multiplier=1).then_inc(pool_step, 1)
            pool.wait_ge(pool_step, 6)
            pool.affine_select(out=own[:, :], in_=own[:, :], compare_op=ALU.is_ge, fill=0.0, base=MBLK - 1,
                               pattern=[[MBLK, E]], channel_multiplier=-1).then_inc(consts_made, 1)
            pool.iota(run[0][:, :], [[TOK, E]], base=0, channel_multiplier=0, **io).then_inc(consts_made, 1)
            pool.iota(token_id[:, :], [[P, NBLK]], base=1, channel_multiplier=1, **io).then_inc(consts_made, 1)
            pool.iota(spare_row[:, :, :],
                      [[0, TILES], [P, WIDE]], base=TOK + 1, channel_multiplier=1, **io).then_inc(consts_made, 1)
            pool.wait_ge(xtok_loaded, 16)
            pool.dma_start(out_d[TOK:TOK + TILE, :].rearrange("(i p) c -> p i c", p=P),
                           x1[:, 0:WIDE, :]).then_inc(y_added, 16)
            steps = [0]

            def then(ins):
                steps[0] += 1
                ins.then_inc(newton_step, 1)
                pool.wait_ge(newton_step, steps[0])

            def inverse_std(g):
                c = slice(g * BLKU, (g + 1) * BLKU)
                y = rstd_i[:, c].bitcast(F32)
                pool.wait_ge(guess_ready, g + 1)
                for _ in range(3):
                    then(pool.tensor_tensor(rt[:, c], y, rhv[:, c], ALU.mult))
                    then(pool.tensor_tensor(rt[:, c], rt[:, c], y, ALU.mult))
                    then(pool.tensor_scalar(rt[:, c], rt[:, c], 1.5, None, ALU.add))
                    then(pool.tensor_tensor(y, rt[:, c], y, ALU.mult))
                pool.tensor_tensor(nmr[:, c], nmean[:, c], y, ALU.mult).then_inc(nmr_ready, 1)

            def w_low(k):
                c = slice(k * PIECE, (k + 1) * PIECE)
                pool.wait_ge(whi_done, k + 1)
                pool.tensor_tensor(w_lo[0][:, c], w_raw[0][:, c], w_hi[0][:, c].bitcast(F32),
                                   ALU.subtract).then_inc(w_split, 1)

            def row_hots(half):
                pool.wait_ge(rq_ready, half + 1)
                if half:
                    pool.wait_ge(inv_ready, half)
                for i in range(HALF):
                    pool.tensor_scalar(hot_r[:, 0, i, :], iota_r[:, :], rf[:, 0, i:i + 1], None, ALU.is_equal
                                       ).then_inc(hot_r_ready, 1)

            for g in range(GROUPS):
                inverse_std(g)
            for k in range(HJ // 2):
                w_low(k)
            row_hots(0)
            for k in range(HJ // 2, HJ):
                w_low(k)
            row_hots(1)

            def gather(n):
                pool.tensor_copy(idx_in[:, :], row_in[:, bass.ds(n, 1), :].rearrange("p a w -> p (a w)")
                                 ).then_inc(idx_in_set, 1)
                pool.wait_ge(idx_in_set, n + 1)
                pool.sem_inc(gathers_begun, 1)
                for i in range(WIDE):
                    pool.indirect_dma_start(xg[:, i, :], None, xs_d,
                                            bass.IndirectOffsetOnAxis(ap=idx_in[:, i:i + 1], axis=0)
                                            ).then_inc(x_gathered, 16)

            def keep_scores(n):
                pool.wait_ge(x_gathered, (n + 1) * (16 * WIDE))
                pool.sem_inc(scores_begun, 1)
                pool.tensor_copy(score_next[:, :, :], xg[:, :, C:]).then_inc(scores_kept, 1)

            def move_scores(n):
                pool.wait_ge(scores_kept, n + 1)
                pool.sem_inc(scores_begun, 1)
                pool.tensor_copy(score[:, :, :], score_next[:, :, :]).then_inc(scores_moved, 1)

            pool.wait_ge(slots_ready, 1)
            pool.wait_ge(xs_stored, 32)
            gather(0)
            keep_scores(0)
            move_scores(0)
            pool.wait_ge(xg_turned, 1)
            gather(1)
            pool.wait_ge(slots_ready, 2)
            pool.wait_ge(x1_stored, 16)
            pool.wait_ge(starts_ready, 1)

            def tile(t, e, block, width):
                pool.wait_ge(scores_moved, t + 1)
                keep_scores(t + 1)
                pool.wait_ge(scores_kept, t + 2)
                pool.wait_ge(xg_turned, t + 2)
                gather(t + 2)
                pool.wait_ge(y_added, block * 16 + 16)
                pool.tensor_copy(idx_out[:, :], row_out[:, bass.ds(t, 1), :].rearrange("p a w -> p (a w)")
                                 ).then_inc(idx_out_set, 1)
                pool.wait_ge(idx_out_set, t + 1)
                pool.wait_ge(y_taken, t + 2)
                pool.sem_inc(weights_begun, 1)
                for i in range(width):
                    ins = pool.tensor_scalar(y_out[:, i, :], y_sum[:, i, :], score[:, i, e:e + 1], None, ALU.mult)
                ins.then_inc(y_weighted, 1)
                pool.wait_ge(y_weighted, t + 2)
                pool.sem_inc(adds_begun, 1)
                for i in range(width):
                    pool.indirect_dma_start(out_d, bass.IndirectOffsetOnAxis(ap=idx_out[:, i:i + 1], axis=0),
                                            y_out[:, i, :], None, compute_op=ALU.add).then_inc(y_added, 16)
                move_scores(t + 1)

            pool.sem_inc(y_weighted, 1)
            for e in range(E):
                t0, t1, odd, more = expert_range(pool, e)
                odd0 = pool.value_load(starts[0:1, 1, e:e + 1], min_val=0, max_val=E)
                odd1 = pool.value_load(starts[0:1, 1, e + 1:e + 2], min_val=0, max_val=E)
                with pool.If(odd):
                    tile(t0, e, t0 * 2 + odd0, WIDE)
                with pool.Else():
                    tile(t0, e, t0 * 2 + odd0, 2)
                with pool.If(more):
                    with pool.Fori(t0 + 1, t1) as t:
                        tile(t, e, t * 2 + odd1, 2)
            odd1 = pool.value_load(starts[0:1, 1, E:E + 1], min_val=0, max_val=E)
            t1 = pool.value_load(starts[0:1, 0, E:E + 1], min_val=1, max_val=TMAX)
            pool.wait_ge(y_added, t1 * 32 + odd1 * 16 + 16)
            pool.wait_ge(x_gathered, (t1 + 2) * (16 * WIDE))

        @block.scalar
        def _(act):
            act.wait_ge(consts_made, 15)
            act.activation(warm[:, :], eps_c[:, :], ACT.Sqrt)

            def square(u):
                act.wait_ge(centred, u + 1)
                if u >= 2:
                    act.wait_ge(var_ready, u - 1)
                act.activation(sq[u % 2][:, :, :], x_cn[:, :, u * UNIT:(u + 1) * UNIT], ACT.Square
                               ).then_inc(sq_ready, 1)

            def root(u):
                act.wait_ge(var_ready, u + 1)
                act.activation(std[:, u, :], banks[:, u, 0:BLKU], ACT.Sqrt, bias=eps_c[:, :]).then_inc(std_ready, 1)

            square(0)
            square(1)
            root(0)
            square(2)
            root(1)
            square(3)
            root(2)
            root(3)
            act.wait_ge(conv_loaded, 16 * 10)

            def take(kind, u):
                n = AT[kind, u]
                b = u // 2
                act.wait_ge(proj_ready, n + 1)
                if u >= 2:
                    if kind in ("q1", "k1"):
                        act.wait_ge(proj_ready, AT[kind[0] + "2", u - 2] + 1)
                    elif kind == "v":
                        act.wait_ge(vt_ready, u - 1)
                    else:
                        act.wait_ge(q_split if kind == "q2" else k_split, u - 1)
                dst = {"q1": q1r, "q2": q2r, "k1": k1r, "k2": k2r, "v": vr}[kind][u % 2]
                g = {"q1": 0, "q2": 2, "k1": 4, "k2": 6, "v": 8}[kind]
                bias = {"k1": kbias[:, b:b + 1], "v": vbias[:, b:b + 1]}.get(kind, aff[:, g + 1:g + 2])
                act.activation(dst[:, :], banks[:, n % 4, :], ACT.Relu, bias=bias, scale=aff[:, g:g + 1]
                               ).then_inc(proj_out, 1)

            def vt_high(u):
                act.wait_ge(vt_ready, u + 1)
                act.activation(vt[u // 2][0][:, u % 2 * BLKU:(u % 2 + 1) * BLKU, :],
                               banks[:, 5 + u % 2, :].rearrange("p (i c) -> p i c", i=BLKU), ACT.Copy
                               ).then_inc(vt_hi_done, 1)

            def global_exp(b):
                act.wait_ge(gmax_ready, b + 1)
                for k in range(KC):
                    if b == 0:
                        act.wait_ge(var_ready, UNITS)
                    else:
                        act.wait_ge(gvec_ready, b)
                    act.activation(sq[k][:, :, :].rearrange("p h n -> p (h n)"), x_cn[:, k, b * N:(b + 1) * N],
                                   ACT.Exp, bias=gmax[:, b, k:k + 1], accum_out=gsum[:, b, k:k + 1]
                                   ).then_inc(gexp_ready, 1)

            for b in range(B):
                for item in (("q1", 2 * b), ("q1", 2 * b + 1), ("q2", 2 * b), ("q2", 2 * b + 1)):
                    take(*item)
                global_exp(b)
            for b in range(B):
                u, w = 2 * b, 2 * b + 1
                act.wait_ge(gbias_ready, b + 1)
                for item in (("k1", u), ("v", u), ("k1", w), ("v", w)):
                    take(*item)
                vt_high(u)
                take("k2", u)
                vt_high(w)
                take("k2", w)

            def exp_row(r):
                act.wait_ge(rmax_ready, r + 1)
                if r >= 2:
                    act.wait_ge(t_ready, 2 * (r - 1))
                act.activation(prob[r % 2][:, :].rearrange("p (h m) -> p h m", h=2),
                               banks[:, 2 * (r % 2):2 * (r % 2) + 2, :], ACT.Exp, bias=rneg[:, r:r + 1], scale=SCALE,
                               accum_out=rsum[:, r:r + 1]).then_inc(exp_done, 1)

            def pt_high(r, h):
                g, i = divmod(r, BLKU)
                act.wait_ge(t_ready, 2 * r + h + 1)
                if g >= 2:
                    act.wait_ge(pv_ready, g - 1)
                act.activation(pt_hi[g % 2][:, 4 * h:4 * h + 4, i * P:(i + 1) * P],
                               banks[:, 4 + h, :].rearrange("p (m n) -> p m n", m=4), ACT.Copy
                               ).then_inc(pt_hi_done, 1)

            act.wait_ge(k_split, UNITS)

            def ctx_high(g):
                act.wait_ge(pv_ready, g + 1)
                if g:
                    act.wait_ge(o_ready, 2 * g)
                act.activation(ctx_hi[:, :], banks[:, CTX_BANK[g], :], ACT.Copy).then_inc(ctx_hi_done, 1)

            def token_norm(g):
                act.wait_ge(nmr_ready, g + 1)
                for i in range(g * BLKU, (g + 1) * BLKU):
                    act.activation(xn2[:, i, 0:C], x1[:, i, :], ACT.Identity, bias=nmr[:, i:i + 1],
                                   scale=rstd_i[:, i:i + 1].bitcast(F32)).then_inc(xn2_ready, 1)

            def xt_copy(i):
                act.wait_ge(xt_ready, i + 1)
                act.activation(xt2[:, 2 * i:2 * i + 2, :, :],
                               banks[:, XT_BANK[i], :].rearrange("p (i k n) -> p i k n", i=2, k=KC), ACT.Copy
                               ).then_inc(xt_copied, 1)

            def gate_exp(half):
                act.wait_ge(shifted, half + 1)
                act.activation(gate[:, :, :], lg[:, :, :], ACT.Exp).then_inc(expd, 1)

            def w_high(k):
                act.wait_ge(pv_ready, GROUPS)
                act.wait_ge(w_loaded[0], 32)
                c = slice(k * PIECE, (k + 1) * PIECE)
                act.activation(w_hi[0][:, c], w_raw[0][:, c], ACT.Copy).then_inc(whi_done, 1)

            for step in range(NBLK + 1):
                if step:
                    pt_high(step - 1, 0)
                    pt_high(step - 1, 1)
                if step < NBLK:
                    exp_row(step)
                if step in (8, 12, 16):
                    ctx_high(step // 4 - 2)
                if step in (11, 15):
                    token_norm(step // 4 - 2)
                if step in (12, 16):
                    xt_copy(step // 2 - 6)
                    xt_copy(step // 2 - 5)
            ctx_high(3)
            token_norm(2)
            xt_copy(4)
            xt_copy(5)
            gate_exp(0)
            for k in range(HJ):
                w_high(k)
            token_norm(3)
            xt_copy(6)
            xt_copy(7)
            gate_exp(1)
            act.wait_ge(inv_ready, 2)
            act.activation(slot_t[:, :], banks[:, INV_BANK, 0:P], ACT.Copy).then_inc(inv_taken, 1)

            def x_high(n):
                act.wait_ge(xg_turned, n + 1)
                act.activation(x_hi[:, :, :], banks[:, 6:8, 0:TILE], ACT.Copy
                               ).then_inc(xhi_done, 1)

            def tile(t, e, width, split):
                w = width * P
                for j in range(HJ):
                    act.wait_ge(l1_ready, t * HJ + (j + 1))
                    act.wait_ge(h_split, t * HJ + (j + 1))
                    bias = b1t[:, e * HJ + j:e * HJ + j + 1]
                    act.activation(h_raw[j % RING][:, 0:w], banks[:, j % RING, 0:w], ACT.Gelu, bias=bias)
                    act.wait_ge(l2_done, t * HJ + (j + 1))
                    act.activation(h_hi[:, j, 0:w], banks[:, j % RING, 0:w], ACT.Gelu, bias=bias
                                   ).then_inc(gelu_done, 1)
                    if split and e + 1 < E:
                        if j == 0:
                            act.wait_ge(w_loaded[(e + 1) % 2], 32 * ((e + 1) // 2 + 1))
                            act.wait_ge(l2_done, t * HJ + HJ)
                        c = slice(j * PIECE, (j + 1) * PIECE)
                        act.activation(w_hi[(e + 1) % 2][:, c], w_raw[(e + 1) % 2][:, c], ACT.Copy
                                       ).then_inc(whi_done, 1)
                x_high(t + 1)

            act.sem_inc(gelu_done, RING)
            x_high(0)
            act.wait_ge(bias_loaded, 32)
            act.wait_ge(starts_ready, 1)
            for e in range(E):
                t0, t1, odd, more = expert_range(act, e)
                with act.If(odd):
                    tile(t0, e, WIDE, True)
                with act.Else():
                    tile(t0, e, 2, True)
                with act.If(more):
                    with act.Fori(t0 + 1, t1) as t:
                        tile(t, e, 2, False)

        @block.vector
        def _(dve):
            steps = [0]

            def then(ins):
                steps[0] += 1
                ins.then_inc(dve_step, 1)
                dve.wait_ge(dve_step, steps[0])

            dve.memset(ones[:, :], 1.0).then_inc(ones_made, 1)
            dve.wait_ge(consts_made, 15)
            then(dve.tensor_scalar(k_i[:, 0:1], q_i[:, :], MBLK - 1, None, ALU.bitwise_and))
            then(dve.tensor_scalar(k_i[:, 1:2], k_i[:, 0:1], 1, None, ALU.logical_shift_right))
            then(dve.tensor_copy(k_f[:, :], k_i[:, :]))
            then(dve.tensor_tensor(k_col[:, :], k_f[:, 0:1], k_f[:, 1:2], ALU.add))
            dve.tensor_scalar(k_one[:, :], k_f[:, 0:1], 1.0, None, ALU.add).then_inc(dve_step, 1)
            steps[0] += 1
            then(dve.tensor_scalar(k_move[:, :], k_col[:, :], -1.0, 2.0, ALU.mult, ALU.add))
            for u in range(UNITS):
                c = x_cn[:, :, u * UNIT:(u + 1) * UNIT]
                dve.wait_ge(mean_ready, u + 1)
                dve.tensor_tensor(c, c, banks[:, u:u + 1, :].broadcast_to([P, KC, UNIT]), ALU.subtract
                                  ).then_inc(centred, 1)

            def spread_root(u):
                dve.wait_ge(std_ready, u + 1)
                if u >= 2:
                    dve.wait_ge(rstd_ready, u - 1)
                then(dve.reciprocal(std[:, u, :], std[:, u, :]))
                dve.tensor_tensor(diag[u % 2][:, :, :], ident[:, :].unsqueeze(1).broadcast_to([P, BLKU, P]),
                                  std[:, u, :].unsqueeze(2).broadcast_to([P, BLKU, P]), ALU.mult
                                  ).then_inc(diag_ready, 1)

            def norm(u):
                c = x_cn[:, :, u * UNIT:(u + 1) * UNIT]
                dve.wait_ge(rstd_ready, u + 1)
                dve.tensor_tensor(c, c, banks[:, 4 + u:5 + u, :].broadcast_to([P, KC, UNIT]), ALU.mult
                                  ).then_inc(normed, 1)

            def global_max(b):
                dve.wait_ge(normed, 2 * b + 2)
                then(dve.tensor_reduce(gmax[:, b, :], x_cn[:, :, b * N:(b + 1) * N], AX.X, ALU.max))
                dve.tensor_scalar(gmax[:, b, :], gmax[:, b, :], -1.0, None, ALU.mult).then_inc(gmax_ready, 1)

            def global_vector(b):
                dve.wait_ge(gexp_ready, KC * (b + 1))
                for k in range(KC):
                    then(dve.scalar_tensor_tensor(sq[k][:, :, :].rearrange("p h n -> p (h n)"), sq[k][:, :, :].rearrange("p h n -> p (h n)"), 1.0 / N, x_cn[:, k, b * N:(b + 1) * N],
                                                  ALU.mult, ALU.mult, accum_out=gdot[:, b, k:k + 1]))
                then(dve.reciprocal(gsum[:, b, :], gsum[:, b, :]))
                dve.tensor_tensor(gvec[:, b, :], gdot[:, b, :], gsum[:, b, :], ALU.mult).then_inc(gvec_ready, 1)

            def global_bias(b):
                dve.wait_ge(gproj_ready, b + 1)
                dve.tensor_scalar(kbias[:, b:b + 1], banks[:, 4, 2 * b:2 * b + 1], aff[:, 4:5], aff[:, 5:6],
                                  ALU.mult, ALU.add).then_inc(dve_step, 1)
                dve.tensor_scalar(vbias[:, b:b + 1], banks[:, 4, 2 * b + 1:2 * b + 2], aff[:, 8:9], aff[:, 9:10],
                                  ALU.mult, ALU.add).then_inc(gbias_ready, 1)
                steps[0] += 1

            def split(kind, u, raw, done):
                hi, lo = qk[u // 2][0:2] if kind == "q2" else qk[u // 2][2:4]
                dve.wait_ge(proj_out, AT[kind, u] + 1)
                c = slice(u % 2 * UNIT, (u % 2 + 1) * UNIT)
                then(dve.tensor_copy(hi[:, c], raw[u % 2][:, :]))
                dve.tensor_tensor(lo[:, c], raw[u % 2][:, :], hi[:, c].bitcast(F32), ALU.subtract).then_inc(done, 1)

            def vt_low(u):
                dve.wait_ge(vt_hi_done, u + 1)
                c = slice(u % 2 * BLKU, (u % 2 + 1) * BLKU)
                hi, lo = vt[u // 2]
                dve.tensor_tensor(lo[:, c, :], banks[:, 5 + u % 2, :].rearrange("p (i c) -> p i c", i=BLKU),
                                  hi[:, c, :].bitcast(F32), ALU.subtract).then_inc(vt_split, 1)

            spread_root(0)
            spread_root(1)
            norm(0)
            norm(1)
            spread_root(2)
            spread_root(3)
            global_max(0)
            norm(2)
            norm(3)
            split("q2", 0, q2r, q_split)
            split("q2", 1, q2r, q_split)
            global_vector(0)
            global_max(1)
            split("q2", 2, q2r, q_split)
            split("q2", 3, q2r, q_split)
            global_bias(0)
            global_vector(1)
            dve.wait_ge(conv_loaded, 16 * 10)
            then(dve.tensor_tensor(w_og[:, :], w_o[:, :], og[:, :], ALU.mult))
            then(dve.tensor_copy(wo_hi[:, :], w_og[:, :]))
            dve.tensor_tensor(wo_lo[:, :], w_og[:, :], wo_hi[:, :].bitcast(F32), ALU.subtract).then_inc(wo_split, 1)
            global_bias(1)
            for b in range(B):
                for u in (2 * b, 2 * b + 1):
                    vt_low(u)
                    split("k2", u, k2r, k_split)

            def row_max(r):
                dve.wait_ge(s_ready, r + 1)
                then(dve.tensor_reduce(rmax[:, r:r + 1], banks[:, 2 * (r % 2):2 * (r % 2) + 2, :], AX.XY, ALU.max))
                dve.tensor_scalar(rneg[:, r:r + 1], rmax[:, r:r + 1], -SCALE, None, ALU.mult).then_inc(rmax_ready, 1)

            def pt_low(r, h):
                g, i = divmod(r, BLKU)
                dve.wait_ge(pt_hi_done, 2 * r + h + 1)
                c = pt_hi[g % 2][:, 4 * h:4 * h + 4, i * P:(i + 1) * P]
                dve.tensor_tensor(pt_lo[g % 2][:, 4 * h:4 * h + 4, i * P:(i + 1) * P],
                                  banks[:, 4 + h, :].rearrange("p (m n) -> p m n", m=4), c.bitcast(F32),
                                  ALU.subtract).then_inc(pt_split, 1)

            def out_rows(g, pair):
                if pair == 0:
                    dve.wait_ge(exp_done, BLKU * (g + 1))
                    then(dve.reciprocal(rinv[:, g * BLKU:(g + 1) * BLKU], rsum[:, g * BLKU:(g + 1) * BLKU]))
                dve.wait_ge(o_ready, 2 * g + pair + 1)
                for i in range(2):
                    k = g * BLKU + 2 * pair + i
                    ins = dve.scalar_tensor_tensor(o_tmp[:, i, :], banks[:, O_BANK[2 * g + pair], i * C:(i + 1) * C], rinv[:, k:k + 1],
                                                   ob[:, :], ALU.mult, ALU.add)
                    if i == 0:
                        ins.then_inc(dve_step, 1)
                        steps[0] += 1
                    else:
                        ins.then_inc(o_taken, 1)
                dve.wait_ge(o_taken, 2 * g + pair + 1)
                dve.wait_ge(dve_step, steps[0])
                for i in range(2):
                    k = g * BLKU + 2 * pair + i
                    dve.scalar_tensor_tensor(x1[:, k, :], o_tmp[:, i, :], 0.0, x1[:, k, :], ALU.max, ALU.add
                                             ).then_inc(x1_ready, 1)
                for i in range(2):
                    k = g * BLKU + 2 * pair + i
                    dve.wait_ge(x1_ready, k + 1)
                    dve.bn_stats(bst[:, k, :], x1[:, k, :]).then_inc(dve_step, 1)
                steps[0] += 2
                dve.wait_ge(dve_step, steps[0])
                for i in range(2):
                    k = g * BLKU + 2 * pair + i
                    dve.bn_aggr(mv[:, k, :], bst[:, k, :]).then_inc(dve_step, 1)
                steps[0] += 2
                dve.wait_ge(dve_step, steps[0])

            def guess_std(g):
                c = slice(g * BLKU, (g + 1) * BLKU)
                then(dve.tensor_scalar(rv[:, c], mv[:, c, 1], TOK_EPS, None, ALU.add))
                dve.tensor_scalar(rhv[:, c], rv[:, c], -0.5, None, ALU.mult).then_inc(dve_step, 1)
                dve.tensor_scalar(nmean[:, c], mv[:, c, 0], -1.0, None, ALU.mult).then_inc(dve_step, 1)
                steps[0] += 2
                then(dve.tensor_scalar(ri0[:, c], rv[:, c].bitcast(I32), 1, None, ALU.logical_shift_right))
                dve.tensor_scalar(rstd_i[:, c], ri0[:, c], -1.0, float(0x5F3759DF), ALU.mult, ALU.add
                                  ).then_inc(guess_ready, 1)

            spread = [P, HALF, E]
            spread2 = [P, 2, HALF, E]

            def route_gates(half):
                dve.wait_ge(lg_ready, HALF // 2 * (half + 1))
                lgp = banks[:, LG_BANK[half], 0:HALF * E].rearrange("p (i e) -> p i e", e=E)
                then(dve.tensor_reduce(g1[:, :], lgp, AX.X, ALU.max))
                dve.tensor_tensor(lg[:, :, :], lgp, g1[:, :].unsqueeze(2).broadcast_to(spread), ALU.subtract
                                  ).then_inc(shifted, 1)
                dve.wait_ge(expd, half + 1)
                then(dve.tensor_reduce(g1[:, :], gate[:, :, :], AX.X, ALU.add))
                then(dve.reciprocal(g1[:, :], g1[:, :]))
                then(dve.tensor_tensor(gate[:, :, :], gate[:, :, :], g1[:, :].unsqueeze(2).broadcast_to(spread),
                                       ALU.mult))
                for i in range(HALF):
                    dve.max(top8[:, i, :], gate[:, i, :]).then_inc(dve_step, 1)
                steps[0] += HALF
                dve.wait_ge(dve_step, steps[0])
                for i in range(HALF):
                    dve.max_index(idx8[:, i, :], top8[:, i, :], gate[:, i, :]).then_inc(dve_step, 1)
                steps[0] += HALF
                dve.wait_ge(dve_step, steps[0])
                then(dve.tensor_copy(idxf[:, :, :], idx8[:, :, 0:2].rearrange("p i k -> p k i")))
                then(dve.tensor_tensor(hot_e[:, :, :, :], iota_e[:, :].unsqueeze(1).unsqueeze(1).broadcast_to(spread2),
                                       idxf[:, :, :].unsqueeze(3).broadcast_to(spread2), ALU.is_equal))
                dve.tensor_tensor(sel[:, :, :].rearrange("p e i -> p i e"), hot_e[:, 0, :, :], hot_e[:, 1, :, :],
                                  ALU.add).then_inc(sel_ready, 1)
                then(dve.tensor_tensor(g1[:, :], top8[:, :, 0], top8[:, :, 1], ALU.add))
                then(dve.tensor_scalar(g1[:, :], g1[:, :], GATE_EPS, None, ALU.add))
                then(dve.reciprocal(g1[:, :], g1[:, :]))
                then(dve.tensor_tensor(topg[:, :, :], top8[:, :, 0:2].rearrange("p i k -> p k i"),
                                       g1[:, :].unsqueeze(1).broadcast_to([P, 2, HALF]), ALU.mult))
                then(dve.tensor_tensor(scored[:, :, :, :], hot_e[:, :, :, :],
                                       topg[:, :, :].unsqueeze(3).broadcast_to(spread2), ALU.mult))
                dve.tensor_tensor(xn2[:, half * HALF:(half + 1) * HALF, C:], scored[:, 0, :, :], scored[:, 1, :, :],
                                  ALU.add).then_inc(scores_ready, 1)

            def route_ranks(half):
                dve.wait_ge(rank_ready, half + 1)
                bank = banks[:, RANK_BANK[half], 0:2 * E * HALF]
                if half:
                    dve.wait_ge(hot_r_ready, HALF)
                then(dve.tensor_tensor_scan(incl[:, :, :].rearrange("p e i -> p (e i)"),
                                            seg[:, :, :].rearrange("p e i -> p (e i)"), bank[:, E * HALF:],
                                            0.0, ALU.mult, ALU.add))
                then(dve.tensor_tensor(incl[:, :, :], incl[:, :, :], run[half][:, :].unsqueeze(2)
                                       .broadcast_to([P, E, HALF]), ALU.add))
                dve.tensor_copy(run[half + 1][:, :], incl[:, :, HALF - 1]).then_inc(dve_step, 1)
                steps[0] += 1
                dve.tensor_tensor(rank[:, :, :], incl[:, :, :], bank[:, 0:E * HALF].rearrange("p (e i) -> p e i", e=E),
                                  ALU.add).then_inc(rank_taken, 1)
                dve.wait_ge(rank_taken, half + 1)
                then(dve.tensor_tensor(pos3[:, :, :, :], hot_e[:, :, :, :],
                                       rank[:, :, :].rearrange("p e i -> p i e").unsqueeze(1).broadcast_to(spread2),
                                       ALU.mult))
                then(dve.tensor_reduce(posf[:, :, :], pos3[:, :, :, :], AX.X, ALU.add))
                then(dve.tensor_copy(posi[:, :, :], posf[:, :, :]))
                then(dve.tensor_scalar(qi[:, :, :], posi[:, :, :], 7, None, ALU.logical_shift_right))
                then(dve.tensor_scalar(ri[:, :, :], posi[:, :, :], P - 1, None, ALU.bitwise_and))
                then(dve.tensor_copy(qf[:, :, :], qi[:, :, :]))
                dve.tensor_copy(rf[:, :, :], ri[:, :, :]).then_inc(rq_ready, 1)

            def column_hots(half):
                dve.wait_ge(rq_ready, half + 1)
                if half:
                    dve.wait_ge(inv_ready, half)
                for k in (1, 0):
                    for i in range(HALF):
                        b = half * HALF + i
                        if k == 1:
                            dve.tensor_scalar(hot_r[:, 1, i, :], iota_r[:, :], rf[:, 1, i:i + 1], None, ALU.is_equal
                                              ).then_inc(dve_step, 1)
                            steps[0] += 1
                        dve.tensor_scalar(hot_q[:, k, i, :], iota_r[:, :], qf[:, k, i:i + 1], token_id[:, b:b + 1],
                                          ALU.is_equal, ALU.mult).then_inc(hot_q_ready, 1)

            dve.wait_ge(xtok_loaded, 16)
            dve.wait_ge(y_added, 16)
            def context_low(g):
                dve.wait_ge(ctx_hi_done, g + 1)
                dve.tensor_tensor(ctx_lo[:, :], banks[:, CTX_BANK[g], :], ctx_hi[:, :].bitcast(F32),
                                  ALU.subtract).then_inc(ctx_split, 1)

            for step in range(NBLK + 1):
                if step < NBLK:
                    row_max(step)
                if step:
                    pt_low(step - 1, 0)
                    pt_low(step - 1, 1)
                if step in (8, 12, 16):
                    context_low(step // 4 - 2)
                if step in (9, 10, 13, 14):
                    out_rows(step // 4 - 2, step % 4 - 1)
                if step in (10, 14):
                    guess_std(step // 4 - 2)
            out_rows(2, 0)
            out_rows(2, 1)
            guess_std(2)
            context_low(3)
            out_rows(3, 0)
            out_rows(3, 1)
            guess_std(3)
            for half in range(2):
                route_gates(half)
                route_ranks(half)
                column_hots(half)

            then(dve.scalar_tensor_tensor(blocks_i[:, 0, :], run[2][:, :], float(P - 1), run[0][:, :],
                                          ALU.add, ALU.subtract))
            then(dve.tensor_scalar(blocks_i[:, 1, :], blocks_i[:, 0, :], 7, None, ALU.logical_shift_right))
            then(dve.tensor_scalar(parts_i[:, 2, :], blocks_i[:, 1, :], float(LEAST), None, ALU.max))
            dve.tensor_scalar(parts_i[:, 0, :], parts_i[:, 2, :], 1, None, ALU.logical_shift_right
                              ).then_inc(dve_step, 1)
            steps[0] += 1
            then(dve.tensor_scalar(parts_i[:, 1, :], parts_i[:, 2, :], 1, None, ALU.bitwise_and))
            then(dve.tensor_copy(parts[:, :, 1:], parts_i[:, :, :]))
            then(dve.tensor_tensor_scan(before[:, :, :].rearrange("p a e -> p (a e)"),
                                        seg2[:, :, :].rearrange("p a e -> p (a e)"),
                                        parts[:, 0:2, :].rearrange("p a e -> p (a e)"), 0.0, ALU.mult, ALU.add))
            dve.scalar_tensor_tensor(scrap[:, 0, :], before[:, 0, 0:E], float(WIDE), own[:, :], ALU.mult, ALU.mult,
                                     accum_out=col_a[:, :]).then_inc(dve_step, 1)
            steps[0] += 1
            then(dve.tensor_tensor(odd_m[:, :], parts[:, 1, 1:], parts[:, 2, 1:], ALU.mult))
            then(dve.scalar_tensor_tensor(scrap[:, 1, :], odd_m[:, :], 1.0, own[:, :], ALU.mult, ALU.mult,
                                          accum_out=col_z[:, :]))
            then(dve.tensor_scalar(col_z[:, :], col_z[:, :], k_one[:, :], k_move[:, :], ALU.is_equal, ALU.mult))
            then(dve.tensor_scalar(col_q[:, :], col_z[:, :], col_a[:, :], k_col[:, :], ALU.add, ALU.add))
            dve.tensor_scalar(place[:, :], iota_r[:, 0:SLOTS], col_q[:, :], None, ALU.is_equal
                              ).then_inc(place_ready, 1)
            dve.tensor_copy(starts[0:1, 2, 0:E], parts_i[0:1, 1, :]).then_inc(dve_step, 1)
            dve.tensor_scalar(starts[0:1, 3, 0:E], parts_i[0:1, 0, :], 1.0, None, ALU.is_gt).then_inc(dve_step, 1)
            steps[0] += 2
            dve.wait_ge(dve_step, steps[0])
            dve.tensor_copy(starts[0:1, 0:2, :], before[0:1, :, :]).then_inc(starts_ready, 1)
            dve.wait_ge(table_ready, 1)
            table = banks[:, TABLE_BANK, 0:SLOTS].rearrange("p (t w) -> p t w", w=WIDE)
            dve.tensor_scalar(row_in[:, :, :], table, -1.0, 0.0, ALU.add, ALU.max).then_inc(slots_ready, 1)
            then(dve.scalar_tensor_tensor(empty[:, :, :], table, 0.0, spare_row[:, :, :], ALU.is_equal, ALU.mult))
            dve.scalar_tensor_tensor(row_out[:, :, :], table, -1.0, empty[:, :, :], ALU.add, ALU.add
                                     ).then_inc(slots_ready, 1)
            dve.wait_ge(starts_ready, 1)

            def x_low(n):
                dve.wait_ge(xhi_done, n + 1)
                dve.tensor_tensor(x_lo[:, :, :], banks[:, 6:8, 0:TILE], x_hi[:, :, :].bitcast(F32),
                                  ALU.subtract).then_inc(x_split, 1)

            def tile(t, e, width, split):
                w = width * P
                for j in range(HJ):
                    dve.wait_ge(gelu_done, t * HJ + (j + 1 + RING))
                    dve.wait_ge(l2_done, t * HJ + (j + 1))
                    dve.tensor_tensor(h_lo[:, j, 0:w], h_raw[j % RING][:, 0:w], h_hi[:, j, 0:w].bitcast(F32),
                                      ALU.subtract).then_inc(h_split, 1)
                    if split and e + 1 < E:
                        c = slice(j * PIECE, (j + 1) * PIECE)
                        dve.wait_ge(whi_done, HJ * (e + 1) + j + 1)
                        dve.tensor_tensor(w_lo[(e + 1) % 2][:, c], w_raw[(e + 1) % 2][:, c],
                                          w_hi[(e + 1) % 2][:, c].bitcast(F32), ALU.subtract).then_inc(w_split, 1)
                x_low(t + 1)
                dve.wait_ge(l2_done, t * HJ + 2 * HJ)
                dve.wait_ge(y_weighted, t + 1)
                for i in range(width):
                    ins = dve.tensor_tensor(y_sum[:, i, :], banks[:, 4 + i % 2, i // 2 * C:(i // 2 + 1) * C],
                                            b2b[:, e * C:(e + 1) * C], ALU.add)
                ins.then_inc(y_taken, 1)

            dve.sem_inc(h_split, RING)
            dve.sem_inc(y_taken, 1)
            x_low(0)
            dve.wait_ge(bias_loaded, 32)
            for e in range(E):
                t0, t1, odd, more = expert_range(dve, e)
                with dve.If(odd):
                    tile(t0, e, WIDE, True)
                with dve.Else():
                    tile(t0, e, 2, True)
                with dve.If(more):
                    with dve.Fori(t0 + 1, t1) as t:
                        tile(t, e, 2, False)

        @block.tensor
        def _(pe):
            def product3(out, a_hi, a_lo, b_hi, b_lo, start, stop):
                pe.matmul(out, a_hi, b_hi, start=start, stop=False)
                pe.matmul(out, a_hi, b_lo, start=False, stop=False)
                return pe.matmul(out, a_lo, b_hi, start=False, stop=stop)

            pe.wait_ge(ones_made, 1)
            for _ in range(9):
                pe.matmul(banks[:, 7, 0:P], ones[:, :], ones[:, :], start=True, stop=True)
            pe.wait_ge(consts_made, 15)

            def mean(u):
                pe.wait_ge(x_loaded[u], 16)
                for k in range(KC):
                    ins = pe.matmul(banks[:, u, :], avg[:, :], x_cn[:, k, u * UNIT:(u + 1) * UNIT],
                                    start=k == 0, stop=k == KC - 1)
                ins.then_inc(mean_ready, 1)

            def variance(u):
                pe.wait_ge(sq_ready, u + 1)
                pe.wait_ge(centred, u + 1)
                for j in range(BLKU):
                    for k in range(KC):
                        ins = pe.matmul(banks[:, u, j:j + 1], sq[u % 2][:, k, j * P:(j + 1) * P], avg[:, 0:1],
                                        start=k == 0, stop=k == KC - 1)
                ins.then_inc(var_ready, 1)

            def spread_rstd(u):
                pe.wait_ge(diag_ready, u + 1)
                pe.matmul(banks[:, 4 + u, :], ones[:, :], diag[u % 2][:, :, :].rearrange("p j n -> p (j n)"),
                          start=True, stop=True).then_inc(rstd_ready, 1)

            def project(kind, u):
                n = AT[kind, u]
                if n >= 4:
                    pe.wait_ge(proj_out, n - 3)
                out = banks[:, n % 4, :]
                if kind in ("q2", "k2"):
                    src, w = (q1r, w_q2) if kind == "q2" else (k1r, w_k2)
                    pe.wait_ge(proj_out, AT[kind[0] + "1", u] + 1)
                    ins = pe.matmul(out, w[:, :], src[u % 2][:, :], start=True, stop=True)
                else:
                    w = {"q1": w_q1[:, :, :], "k1": w_k1[:, KC:, :], "v": w_v[:, KC:, :]}[kind]
                    pe.wait_ge(normed, u + 1)
                    for k in range(KC):
                        ins = pe.matmul(out, w[:, k, :], x_cn[:, k, u * UNIT:(u + 1) * UNIT],
                                        start=k == 0, stop=k == KC - 1)
                ins.then_inc(proj_ready, 1)

            def project_global(b):
                pe.wait_ge(gvec_ready, b + 1)
                if b:
                    pe.wait_ge(gbias_ready, b)
                for i, w in enumerate((w_k1, w_v)):
                    for k in range(KC):
                        ins = pe.matmul(banks[:, 4, 2 * b + i:2 * b + i + 1], w[:, k, :], gvec[:, b, k:k + 1],
                                        start=k == 0, stop=k == KC - 1)
                ins.then_inc(gproj_ready, 1)

            def turn_v(u):
                pe.wait_ge(proj_out, AT["v", u] + 1)
                if u >= 2:
                    pe.wait_ge(vt_split, u - 1)
                else:
                    pe.wait_ge(normed, UNITS)
                for i in range(BLKU):
                    ins = pe.transpose(banks[:, 5 + u % 2, i * P:(i + 1) * P], vr[u % 2][:, i * P:(i + 1) * P],
                                       ident[:, :])
                ins.then_inc(vt_ready, 1)

            mean(0)
            mean(1)
            mean(2)
            variance(0)
            mean(3)
            variance(1)
            spread_rstd(0)
            spread_rstd(1)
            pe.wait_ge(conv_loaded, 16 * 10)
            pe.wait_ge(std_ready, 2)
            project("q1", 0)
            variance(2)
            project("q1", 1)
            variance(3)
            spread_rstd(2)
            spread_rstd(3)
            pe.wait_ge(std_ready, UNITS)
            for item in PROJ[2:2 * UNITS]:
                project(*item)
            for b in range(B):
                u, w = 2 * b, 2 * b + 1
                project("k1", u)
                project("v", u)
                if b == 0:
                    project_global(0)
                project("k1", w)
                project("v", w)
                if b == 0:
                    project_global(1)
                turn_v(u)
                project("k2", u)
                turn_v(w)
                project("k2", w)

            def scores(r):
                b, i = divmod(r, N // P)
                if r >= 2:
                    pe.wait_ge(exp_done, r - 1)
                if i == 0:
                    pe.wait_ge(q_split, 2 * b + 2)
                    pe.wait_ge(k_split, 2 * b + 2)
                q_hi, q_lo, k_hi, k_lo = qk[b]
                qc = slice(i * P, (i + 1) * P)
                for h in range(2):
                    kc = slice(h * UNIT, (h + 1) * UNIT)
                    ins = product3(banks[:, 2 * (r % 2) + h, :], q_hi[:, qc], q_lo[:, qc], k_hi[:, kc], k_lo[:, kc],
                                   True, True)
                ins.then_inc(s_ready, 1)

            def turn(r):
                pe.wait_ge(exp_done, r + 1)
                for h in range(2):
                    if r:
                        pe.wait_ge(pt_split, 2 * (r - 1) + h + 1)
                    for m in range(4):
                        ins = pe.transpose(banks[:, 4 + h, m * P:(m + 1) * P],
                                           prob[r % 2][:, (4 * h + m) * P:(4 * h + m + 1) * P], ident[:, :])
                    ins.then_inc(t_ready, 1)

            def context(g, quarter):
                if quarter % 2 == 0:
                    pe.wait_ge(pt_split, 2 * BLKU * (g + 1) - 1 + quarter // 2)
                if quarter == 0:
                    if g == 3:
                        pe.wait_ge(exp_done, NBLK - 1)
                    elif g:
                        pe.wait_ge(ctx_split, g)
                v_hi, v_lo = vt[g // 2]
                for m in (2 * quarter, 2 * quarter + 1):
                    ins = product3(banks[:, CTX_BANK[g], :], v_hi[:, m, :], v_lo[:, m, :],
                                   pt_hi[g % 2][:, m, :], pt_lo[g % 2][:, m, :], m == 0, m == 7)
                if quarter == 3:
                    ins.then_inc(pv_ready, 1)

            def out_conv(g, pair):
                n = 2 * g + pair
                pe.wait_ge(ctx_split, g + 1)
                if n in (1, 3):
                    pe.wait_ge(o_taken, n)
                elif n in (2, 4):
                    pe.wait_ge(xt_copied, n)
                elif n >= 5:
                    pe.wait_ge(exp_done, NBLK)
                for i in range(2):
                    c = slice((2 * pair + i) * P, (2 * pair + i + 1) * P)
                    ins = product3(banks[:, O_BANK[n], i * C:(i + 1) * C], ctx_hi[:, c], ctx_lo[:, c],
                                   wo_hi[:, :], wo_lo[:, :], True, True)
                ins.then_inc(o_ready, 1)

            def turn_tokens(i):
                pe.wait_ge(xn2_ready, 2 * i + 2)
                if i in (0, 2):
                    pe.wait_ge(o_taken, i + 2)
                elif i in (1, 3):
                    pe.wait_ge(xt_copied, i)
                elif i == 4:
                    pe.wait_ge(pt_split, 2 * NBLK)
                elif i == 5:
                    pe.wait_ge(ctx_split, 3)
                elif i == 6:
                    pe.wait_ge(ctx_split, 4)
                else:
                    pe.wait_ge(o_taken, 6)
                for j in range(2):
                    for k in range(KC):
                        ins = pe.transpose(banks[:, XT_BANK[i], (KC * j + k) * P:(KC * j + k + 1) * P],
                                           xn2[:, 2 * i + j, k * P:(k + 1) * P], ident[:, :])
                ins.then_inc(xt_ready, 1)

            def logits(n):
                pe.wait_ge(xt_copied, n + 1)
                if n == 0:
                    pe.wait_ge(pt_split, 2 * NBLK)
                elif n == 4:
                    pe.wait_ge(o_taken, 7)
                half = n // (HALF // 2)
                for i in (2 * n, 2 * n + 1):
                    c = i % HALF * E
                    for k in range(KC):
                        ins = pe.matmul(banks[:, LG_BANK[half], c:c + E], xt2[:, i, k, :], w_g[:, k, :], start=k == 0,
                                        stop=k == KC - 1)
                ins.then_inc(lg_ready, 1)

            def ranks(half):
                pe.wait_ge(sel_ready, half + 1)
                chosen = sel[:, :, :].rearrange("p e i -> p (e i)")
                if half == 0:
                    pe.wait_ge(o_taken, 8)
                bank = banks[:, RANK_BANK[half], :]
                pe.matmul(bank[:, 0:E * HALF], below[:, :], chosen, start=True, stop=True)
                pe.matmul(bank[:, E * HALF:2 * E * HALF], ones[:, :], chosen, start=True, stop=True
                          ).then_inc(rank_ready, 1)

            def inverse(half):
                if half == 0:
                    pe.wait_ge(o_taken, 5)
                for m in range(2 * HALF):
                    k, i = divmod(m, HALF)
                    k = 1 - k
                    pe.wait_ge(hot_q_ready, 2 * HALF * half + m + 1)
                    if k == 0:
                        pe.wait_ge(hot_r_ready, HALF * half + i + 1)
                    ins = pe.matmul(banks[:, INV_BANK, 0:P], hot_q[:, k, i, :], hot_r[:, k, i, :],
                                    start=half == 0 and m == 0, stop=half == 1 and m == 2 * HALF - 1)
                ins.then_inc(inv_ready, 1)

            pe.wait_ge(proj_out, len(PROJ))
            pe.wait_ge(gbias_ready, B)
            pe.wait_ge(vt_split, UNITS)
            pe.wait_ge(wo_split, 1)
            for step in range(NBLK + 1):
                if step < NBLK:
                    scores(step)
                if step:
                    turn(step - 1)
                if step in (12, 16):
                    turn_tokens(step // 2 - 6)
                if step >= 5:
                    context((step - 5) // 4, (step - 5) % 4)
                if step in (9, 10, 13, 14):
                    out_conv(step // 4 - 2, step % 4 - 1)
                if step in (12, 16):
                    turn_tokens(step // 2 - 5)
            context(3, 0)
            context(3, 1)
            out_conv(2, 0)
            out_conv(2, 1)
            context(3, 2)
            context(3, 3)
            logits(0)
            out_conv(3, 0)
            out_conv(3, 1)
            for n in range(1, 4):
                logits(n)
            turn_tokens(4)
            turn_tokens(5)
            ranks(0)
            logits(4)
            logits(5)
            turn_tokens(6)
            turn_tokens(7)
            logits(6)
            logits(7)
            inverse(0)
            ranks(1)
            inverse(1)
            pe.wait_ge(inv_taken, 1)
            pe.wait_ge(place_ready, 1)
            pe.matmul(banks[:, TABLE_BANK, 0:SLOTS], slot_t[:, :], place[:, :], start=True, stop=True
                      ).then_inc(table_ready, 1)

            def turn_x(n):
                pe.wait_ge(x_gathered, (n + 1) * (16 * WIDE))
                for i in range(WIDE):
                    for k in range(KC):
                        ins = pe.transpose(banks[:, 6 + k, i * P:(i + 1) * P], xg[:, i, k * P:(k + 1) * P],
                                           ident[:, :])
                ins.then_inc(xg_turned, 1)

            def layer1(t, e, j, width):
                pe.wait_ge(gelu_done, t * HJ + (j + 1))
                w = width * P
                for k in range(KC):
                    c = slice(k * H + j * P, k * H + (j + 1) * P)
                    ins = product3(banks[:, j % RING, 0:w], w_hi[e % 2][:, c], w_lo[e % 2][:, c], x_hi[:, k, 0:w],
                                   x_lo[:, k, 0:w], k == 0, k == KC - 1)
                ins.then_inc(l1_ready, 1)

            def layer2(t, e, j, width):
                pe.wait_ge(h_split, t * HJ + (j + 1 + RING))
                if j == 0:
                    pe.wait_ge(y_taken, t + 1)
                c = slice(KC * H + j * C, KC * H + (j + 1) * C)
                for i in range(width):
                    r = slice(i * P, (i + 1) * P)
                    out = banks[:, 4 + i % 2, i // 2 * C:(i // 2 + 1) * C]
                    pe.matmul(out, h_hi[:, j, r], w_hi[e % 2][:, c], start=j == 0 and i < 2, stop=False,
                              skip_group_check=width == WIDE)
                    pe.matmul(out, h_hi[:, j, r], w_lo[e % 2][:, c], start=False, stop=False,
                              skip_group_check=width == WIDE)
                    ins = pe.matmul(out, h_lo[:, j, r], w_hi[e % 2][:, c], start=False, stop=j == HJ - 1,
                                    skip_group_check=width == WIDE)
                ins.then_inc(l2_done, 1)

            def tile(t, e, width):
                pe.wait_ge(x_split, t + 1)
                for j in range(RING):
                    layer1(t, e, j, width)
                for j in range(RING, HJ):
                    layer2(t, e, j - RING, width)
                    layer1(t, e, j, width)
                turn_x(t + 1)
                for j in range(HJ - RING, HJ):
                    layer2(t, e, j, width)

            pe.sem_inc(l2_done, HJ)
            pe.wait_ge(slots_ready, 2)
            turn_x(0)
            pe.wait_ge(starts_ready, 1)
            for e in range(E):
                t0, t1, odd, more = expert_range(pe, e)
                pe.wait_ge(w_split, HJ * (e + 1))
                with pe.If(odd):
                    tile(t0, e, WIDE)
                with pe.Else():
                    tile(t0, e, 2)
                with pe.If(more):
                    with pe.Fori(t0 + 1, t1) as t:
                        tile(t, e, 2)


def kernel(**inputs):
    import numpy as np
    import concourse.bacc as bacc
    from concourse.bass_utils import run_bass_kernel_spmd

    a = {k.replace("L0_conv_", "").replace("L0_ffn_", ""): np.asarray(v) for k, v in inputs.items()}
    x = a["x"]
    shape = x.shape
    cn = np.ascontiguousarray(x.reshape(B, C, N))
    tok = np.ascontiguousarray(cn.transpose(0, 2, 1).reshape(TOK, C))
    aff = np.stack([a[n] for n in ("q_g1", "q_b1", "q_g2", "q_b2", "k_g1", "k_b1", "k_g2", "k_b2", "v_g", "v_b")],
                   axis=1)
    arrays = dict(
        x_cn=cn, x_tok=tok, q1=a["q_w1"].T, q2=a["q_w2"].T, k1=a["k_w1"].T, k2=a["k_w2"].T, v=a["v_w"].T,
        o=a["o_w"].T, aff=aff, og=a["o_g"], ob=a["o_b"], wg=a["Wg"], w1=a["W1"],
        b1=a["b1"].reshape(E, HJ, P).transpose(2, 0, 1).reshape(P, E * HJ), w2=a["W2"],
        b2=a["b2"].reshape(E * C))
    arrays = {f"in_{k}": np.ascontiguousarray(v) for k, v in arrays.items()}
    nc = bacc.Bacc("TRN2", target_bir_lowering=False, num_devices=1)
    args = [nc.dram_tensor(k, v.shape, mybir.dt.from_np(v.dtype), kind="ExternalInput").ap()
            for k, v in arrays.items()]
    out = nc.dram_tensor("out_rows", (TOK + TILE, C), F32, kind="ExternalOutput").ap()
    metaformer_kernel(nc, *args, out)
    rows = run_bass_kernel_spmd(nc, [arrays], core_ids=[0]).results[0]["out_rows"][:TOK]
    return np.ascontiguousarray(rows.reshape(B, N, C).transpose(0, 2, 1)).reshape(shape)
```

```python
from contextlib import ExitStack

import concourse.bass as bass
from concourse import mybir

F32 = mybir.dt.float32
F32R = mybir.dt.float32r
I32 = mybir.dt.int32
U32 = mybir.dt.uint32
ALU = mybir.AluOpType
ACT = mybir.ActivationFunctionType
AX = mybir.AxisListType

P = 128
B, C, N = 2, 256, 1024
TC = 128
KC = C // P
TOK = B * N
NBLK = TOK // P
UNIT = 512
UNITS = TOK // UNIT
BLKU = UNIT // P
E, H = 8, 1024
HJ = H // P
MBLK = TOK // P
LEAST = 2
BLOCKS = 2 * TOK // P + LEAST * E
TMAX = BLOCKS // 2
WIDE = 3
TILE = WIDE * P
TILES = TMAX + 3
SLOTS = TILES * WIDE
HALF = NBLK // 2
ROW = C + E
RING = 4
WCOLS = KC * H + HJ * C
PIECE = WCOLS // HJ
SCALE = float(TC) ** -0.5
CHAN_EPS, TOK_EPS, GATE_EPS = 1e-6, 1e-5, 1e-6


def metaformer_kernel(nc, x_cn_d, x_tok_d, q1_d, q2_d, k1_d, k2_d, v_d, o_d, aff_d, og_d, ob_d,
                      wg_d, w1_d, b1_d, w2_d, b2_d, out_d):
    ctx = ExitStack()
    with ctx:
        def sb(name, shape, dt=F32, stack=ctx):
            return stack.enter_context(nc.sbuf_tensor(name, shape, dt))

        def sem(name):
            return ctx.enter_context(nc.semaphore(name))

        xs_d = nc.dram_tensor("xn_rows", (TOK, ROW), F32, kind="Internal").ap()

        ident = sb("ident", [P, P])
        avg = sb("avg", [P, P])
        ones = sb("ones", [P, P])
        iota_r = sb("iota_r", [P, P])
        below = sb("below", [P, P])
        iota_e = sb("iota_e", [P, E])
        own = sb("own", [P, E])
        q_i = sb("q_i", [P, 1], I32)
        k_i = sb("k_i", [P, 2], I32)
        k_f = sb("k_f", [P, 2])
        k_one = sb("k_one", [P, 1])
        k_col = sb("k_col", [P, 1])
        k_move = sb("k_move", [P, 1])
        seg2 = sb("seg2", [P, 2, E + 1])
        seg = sb("seg", [P, E, HALF])
        token_id = sb("token_id", [P, NBLK])
        spare_row = sb("spare_row", [P, TILES, WIDE])
        eps_c = sb("eps_c", [P, 1])
        std = sb("std", [P, UNITS, BLKU])
        warm = sb("warm", [P, 1])
        aff = sb("aff", [P, 10])
        w_g = sb("w_g", [P, KC, E])
        b1t = sb("b1t", [P, E * HJ])
        x1 = sb("x1", [P, NBLK, C])
        xn2 = sb("xn2", [P, NBLK, ROW])
        w_raw0 = sb("w_raw0", [P, WCOLS])
        with ExitStack() as s:
            xt2 = sb("xt2", [P, NBLK, KC, P], stack=s)
        w_raw = [w_raw0, sb("w_raw1", [P, WCOLS])]

        with ExitStack() as s:
            x_cn = sb("x_cn", [P, KC, TOK], stack=s)
            sq = [sb(f"sq{i}", [P, KC, UNIT], stack=s) for i in range(2)]
            diag = [sb(f"diag{i}", [P, BLKU, P], stack=s) for i in range(2)]
            q1r = [sb(f"q1r{i}", [P, UNIT], stack=s) for i in range(2)]
            k1r = [sb(f"k1r{i}", [P, UNIT], stack=s) for i in range(2)]
            vr = [sb(f"vr{i}", [P, UNIT], stack=s) for i in range(2)]
            q2r = [sb(f"q2r{i}", [P, UNIT], stack=s) for i in range(2)]
            k2r = [sb(f"k2r{i}", [P, UNIT], stack=s) for i in range(2)]
            w_q1 = sb("w_q1", [P, KC, TC], stack=s)
            w_q2 = sb("w_q2", [P, TC], stack=s)
            w_k1 = sb("w_k1", [P, 2 * KC, TC], stack=s)
            w_k2 = sb("w_k2", [P, TC], stack=s)
            w_v = sb("w_v", [P, 2 * KC, TC], stack=s)
            w_o = sb("w_o", [P, C], stack=s)
            og = sb("og", [P, C], stack=s)
            w_og = sb("w_og", [P, C], stack=s)
        with ExitStack() as s:
            pt_hi = [sb(f"pt_hi{i}", [P, N // P, UNIT], F32R, s) for i in range(2)]
            pt_lo = [sb(f"pt_lo{i}", [P, N // P, UNIT], F32R, s) for i in range(2)]
        s_w = ctx.enter_context(ExitStack())
        w_hi = [sb(f"w_hi{i}", [P, WCOLS], F32R, s_w) for i in range(2)]
        w_lo = [sb(f"w_lo{i}", [P, WCOLS], F32R, s_w) for i in range(2)]

        with ExitStack() as s:
            qk = [[sb(f"{n}{b}", [P, N], F32R, s) for n in ("q_hi", "q_lo", "k_hi", "k_lo")] for b in range(B)]
            vt = [[sb(f"{n}{b}", [P, N // P, TC], F32R, s) for n in ("vt_hi", "vt_lo")] for b in range(B)]
            prob = [sb(f"prob{i}", [P, N], stack=s) for i in range(2)]
        with ExitStack() as s:
            hot_r = sb("hot_r", [P, 2, HALF, P], F32R, s)
            hot_q = sb("hot_q", [P, 2, HALF, P], F32R, s)
        s_t = ctx.enter_context(ExitStack())
        h_raw = [sb(f"h_raw{i}", [P, TILE], stack=s_t) for i in range(RING)]
        h_hi = sb("h_hi", [P, HJ, TILE], F32R, s_t)
        h_lo = sb("h_lo", [P, HJ, TILE], F32R, s_t)
        x_hi = sb("x_hi", [P, KC, TILE], F32R, s_t)
        x_lo = sb("x_lo", [P, KC, TILE], F32R, s_t)
        b2b = sb("b2b", [P, E * C], stack=s_t)
        sb("pad", [P, 4 * TOK + 2 * NBLK * TC + 2 * N - (RING + 2 * HJ + 2 * KC) * TILE - E * C], stack=s_t)
        score_next = sb("score_next", [P, WIDE, E])
        score = sb("score", [P, WIDE, E])
        s_y = ExitStack()
        with s_y:
            ctx_hi = sb("ctx_hi", [P, UNIT], F32R, s_y)
            ctx_lo = sb("ctx_lo", [P, UNIT], F32R, s_y)
            o_tmp = sb("o_tmp", [P, 2, C], stack=s_y)
            wo_hi = sb("wo_hi", [P, C], F32R, s_y)
            wo_lo = sb("wo_lo", [P, C], F32R, s_y)
            ob = sb("ob", [P, C], stack=s_y)
        s_y2 = ctx.enter_context(ExitStack())
        y_sum = sb("y_sum", [P, WIDE, C], stack=s_y2)
        y_out = sb("y_out", [P, WIDE, C], stack=s_y2)
        xg = sb("xg", [P, WIDE, ROW], stack=s_y2)
        gmax = sb("gmax", [P, B, KC])
        gsum = sb("gsum", [P, B, KC])
        gdot = sb("gdot", [P, B, KC])
        gvec = sb("gvec", [P, B, KC])
        kbias = sb("kbias", [P, B])
        vbias = sb("vbias", [P, B])
        rmax = sb("rmax", [P, NBLK])
        rneg = sb("rneg", [P, NBLK])
        rsum = sb("rsum", [P, NBLK])
        rinv = sb("rinv", [P, NBLK])
        bst = sb("bst", [P, NBLK, 6])
        mv = sb("mv", [P, NBLK, 2])
        rv = sb("rv", [P, NBLK])
        rhv = sb("rhv", [P, NBLK])
        ri0 = sb("ri0", [P, NBLK], I32)
        rstd_i = sb("rstd_i", [P, NBLK], I32)
        rt = sb("rt", [P, NBLK])
        nmean = sb("nmean", [P, NBLK])
        nmr = sb("nmr", [P, NBLK])
        lg = sb("lg", [P, HALF, E])
        low = sb("low", [P, HALF, E + 2])
        gate = sb("gate", [P, HALF, E + 2])
        topp = sb("topp", [P, HALF, 2])
        g1 = sb("g1", [P, HALF])
        g2 = sb("g2", [P, HALF])
        top8 = sb("top8", [P, HALF, E])
        idx8 = sb("idx8", [P, HALF, E], U32)
        idxf = sb("idxf", [P, 2, HALF])
        topg = sb("topg", [P, 2, HALF])
        hot_e = sb("hot_e", [P, 2, HALF, E])
        scored = sb("scored", [P, 2, HALF, E])
        sel = sb("sel", [P, E, HALF])
        incl = sb("incl", [P, E, HALF])
        rank = sb("rank", [P, E, HALF])
        run = [sb(f"run{i}", [P, E]) for i in range(3)]
        blocks_i = sb("blocks_i", [P, 2, E], I32)
        parts_i = sb("parts_i", [P, 3, E], I32)
        parts = sb("parts", [P, 3, E + 1])
        before = sb("before", [P, 2, E + 1])
        odd_m = sb("odd_m", [P, E])
        scrap = sb("scrap", [P, 2, E])
        col_a = sb("col_a", [P, 1])
        col_z = sb("col_z", [P, 1])
        col_q = sb("col_q", [P, 1])
        place = sb("place", [P, SLOTS])
        many = sb("many", [1, E])
        flags = sb("flags", [1, E])
        bounds = sb("bounds", [1, 2, E], I32)
        pos3 = sb("pos3", [P, 2, HALF, E])
        posf = sb("posf", [P, 2, HALF])
        posi = sb("posi", [P, 2, HALF], I32)
        qi = sb("qi", [P, 2, HALF], I32)
        ri = sb("ri", [P, 2, HALF], I32)
        qf = sb("qf", [P, 2, HALF])
        rf = sb("rf", [P, 2, HALF])
        r_neg = sb("r_neg", [P, HALF])
        apart = sb("apart", [P, 2, P])
        slot_t = sb("slot_t", [P, P])
        empty = sb("empty", [P, TILES, WIDE])
        row_in = sb("row_in", [P, TILES, WIDE], U32)
        row_out = sb("row_out", [P, TILES, WIDE], U32)
        idx_in = sb("idx_in", [P, WIDE], U32)
        idx_out = sb("idx_out", [P, WIDE], U32)

        banks = ctx.enter_context(nc.psum_tensor("banks", [P, 8, 512], F32))

        x_loaded = [sem(f"x_loaded{u}") for u in range(UNITS)]
        conv_loaded = sem("conv_loaded")
        xtok_loaded = sem("xtok_loaded")
        bias_loaded = sem("bias_loaded")
        w_loaded = [sem(f"w_loaded{i}") for i in range(2)]
        consts_made = sem("consts_made")
        ones_made = sem("ones_made")
        pool_step = sem("pool_step")
        newton_step = sem("newton_step")
        guess_ready = sem("guess_ready")
        rq_ready = sem("rq_ready")
        dve_step = sem("dve_step")
        mean_ready = sem("mean_ready")
        centred = sem("centred")
        sq_ready = sem("sq_ready")
        var_ready = sem("var_ready")
        std_ready = sem("std_ready")
        diag_ready = sem("diag_ready")
        rstd_ready = sem("rstd_ready")
        normed = sem("normed")
        gmax_ready = sem("gmax_ready")
        gexp_ready = sem("gexp_ready")
        gvec_ready = sem("gvec_ready")
        gproj_ready = sem("gproj_ready")
        gbias_ready = sem("gbias_ready")
        proj_ready = sem("proj_ready")
        proj_out = sem("proj_out")
        q_split = sem("q_split")
        k_split = sem("k_split")
        vt_ready = sem("vt_ready")
        vt_hi_done = sem("vt_hi_done")
        vt_split = sem("vt_split")
        wo_split = sem("wo_split")
        s_ready = sem("s_ready")
        rmax_ready = sem("rmax_ready")
        exp_done = sem("exp_done")
        t_ready = sem("t_ready")
        pt_hi_done = sem("pt_hi_done")
        pt_split = sem("pt_split")
        pv_ready = sem("pv_ready")
        ctx_hi_done = sem("ctx_hi_done")
        ctx_split = sem("ctx_split")
        o_ready = sem("o_ready")
        o_taken = sem("o_taken")
        x1_ready = sem("x1_ready")
        nmr_ready = sem("nmr_ready")
        xn2_ready = sem("xn2_ready")
        xn2_more = sem("xn2_more")
        xt_ready = sem("xt_ready")
        xt_copied = sem("xt_copied")
        lg_ready = sem("lg_ready")
        shifted = sem("shifted")
        expd = sem("expd")
        norm_ready = sem("norm_ready")
        scores_ready = sem("scores_ready")
        sel_ready = sem("sel_ready")
        rank_ready = sem("rank_ready")
        rank_taken = sem("rank_taken")
        hot_r_ready = sem("hot_r_ready")
        hot_r_more = sem("hot_r_more")
        hot_r_rest = sem("hot_r_rest")
        r_neg_ready = sem("r_neg_ready")
        r_apart = sem("r_apart")
        hot_q_ready = sem("hot_q_ready")
        inv_ready = sem("inv_ready")
        inv_taken = sem("inv_taken")
        place_ready = sem("place_ready")
        table_ready = sem("table_ready")
        bounds_ready = sem("bounds_ready")
        slots_ready = sem("slots_ready")
        xs_stored = sem("xs_stored")
        x1_stored = sem("x1_stored")
        x_gathered = sem("x_gathered")
        idx_in_set = sem("idx_in_set")
        idx_out_set = sem("idx_out_set")
        xg_turned = sem("xg_turned")
        xhi_done = sem("xhi_done")
        x_split = sem("x_split")
        l1_ready = sem("l1_ready")
        gelu_done = sem("gelu_done")
        h_split = sem("h_split")
        l2_done = sem("l2_done")
        y_taken = sem("y_taken")
        y_weighted = sem("y_weighted")
        y_free = sem("y_free")
        scores_kept = sem("scores_kept")
        y_added = sem("y_added")
        gathers_begun = sem("gathers_begun")
        scores_begun = sem("scores_begun")
        scores_moved = sem("scores_moved")
        adds_begun = sem("adds_begun")
        whi_done = sem("whi_done")
        w_split = sem("w_split")

        block = ctx.enter_context(nc.Block())

        PROJ = ([(kind, b + i) for b in (0, 2) for kind in ("q1", "q2") for i in range(2)]
                + [(kind, b + i) for b in (0, 2) for kind, i in
                   (("k1", 0), ("v", 0), ("k1", 1), ("v", 1), ("k2", 0), ("k2", 1))])
        AT = {item: n for n, item in enumerate(PROJ)}
        GROUPS = NBLK // BLKU
        CTX_BANK = [6, 6, 6, 0]
        O_BANK = [7, 7, 7, 7, 1, 2, 3, 1]
        XT_BANK = [7, 7, 7, 5, 6, 7, 0, 5]
        LG_BANK, RANK_BANK, INV_BANK, TABLE_BANK = (4, 3), (2, 1), 6, 7
        POOL_HOTS = 6
        O_STEP = [9, 10, 14, 15]

        def expert_bounds(eng, e):
            word = eng.value_load(bounds[0:1, 0, e:e + 1], min_val=4, max_val=4 * TMAX + 3)
            return word // 4, word % 4 // 2, word % 2

        def load_expert(sp, e):
            raw = w_raw[e % 2]
            sp.dma_start(raw[:, 0:KC * H].rearrange("p (k h) -> p k h", k=KC),
                         w1_d[e].rearrange("(k p) h -> p k h", p=P)).then_inc(w_loaded[e % 2], 16)
            sp.dma_start(raw[:, KC * H:].rearrange("p (j d) -> p j d", j=HJ),
                         w2_d[e].rearrange("(j p) d -> p j d", p=P)).then_inc(w_loaded[e % 2], 16)

        @block.sync
        def _(sp):
            for u in range(UNITS):
                b, h = divmod(u, 2)
                sp.dma_start(x_cn[:, :, u * UNIT:(u + 1) * UNIT],
                             x_cn_d[b, :, h * UNIT:(h + 1) * UNIT].rearrange("(k p) n -> p k n", p=P)
                             ).then_inc(x_loaded[u], 16)
            for dst, src in ((w_q1, q1_d), (w_k1, k1_d), (w_v, v_d), (w_g, wg_d)):
                sp.dma_start(dst[:, :, :], src.rearrange("(k p) o -> p k o", p=P)).then_inc(conv_loaded, 16)
            for dst, src in ((w_q2, q2_d), (w_k2, k2_d), (w_o, o_d), (aff, aff_d),
                             (og, og_d.partition_broadcast(P)), (ob, ob_d.partition_broadcast(P))):
                sp.dma_start(dst[:, :], src).then_inc(conv_loaded, 16)
            sp.dma_start(x1[:, :, :], x_tok_d.rearrange("(i p) c -> p i c", p=P)).then_inc(xtok_loaded, 16)
            sp.dma_start(b1t[:, :], b1_d).then_inc(bias_loaded, 16)
            load_expert(sp, 0)
            sp.wait_ge(pv_ready, GROUPS)
            sp.dma_start(b2b[:, :], b2_d.partition_broadcast(P)).then_inc(bias_loaded, 16)
            def store_rows(half):
                sp.wait_ge(xn2_ready, (4, 12)[half])
                sp.wait_ge(xn2_more, 4)
                sp.wait_ge(scores_ready, half + 1)
                sp.dma_start(xs_d[half * HALF * P:(half + 1) * HALF * P, :].rearrange("(i p) c -> p i c", p=P),
                             xn2[:, half * HALF:(half + 1) * HALF, :]).then_inc(xs_stored, 16)

            store_rows(0)
            sp.wait_ge(x1_ready, NBLK)
            sp.dma_start(out_d[0:TOK, :].rearrange("(i p) c -> p i c", p=P), x1[:, :, :]).then_inc(x1_stored, 16)
            store_rows(1)
            sp.wait_ge(lg_ready, NBLK // 2)
            load_expert(sp, 1)
            for e in range(2, E):
                sp.wait_ge(w_split, HJ * (e - 1))
                if e == 2:
                    sp.wait_ge(x_gathered, 16 * WIDE)
                load_expert(sp, e)

        @block.gpsimd
        def _(pool):
            pool.memset(ident[:, :], 0.0).then_inc(pool_step, 1)
            pool.memset(below[:, :], -1.0).then_inc(pool_step, 1)
            pool.memset(avg[:, :], 1.0 / C).then_inc(consts_made, 1)
            pool.memset(eps_c[:, :], CHAN_EPS).then_inc(consts_made, 1)
            pool.wait_ge(pool_step, 2)
            pool.affine_select(out=ident[:, :], in_=ident[:, :], compare_op=ALU.not_equal, fill=1.0, base=0,
                               pattern=[[-1, P]], channel_multiplier=1).then_inc(consts_made, 1)
            pool.affine_select(out=below[:, :], in_=below[:, :], compare_op=ALU.is_ge, fill=0.0, base=0,
                               pattern=[[-1, P]], channel_multiplier=1).then_inc(consts_made, 1)
            io = dict(allow_small_or_imprecise_dtypes=True)
            pool.iota(iota_r[:, :], [[1, P]], base=0, channel_multiplier=0, **io).then_inc(consts_made, 1)
            pool.iota(iota_e[:, :], [[1, E]], base=0, channel_multiplier=0, **io).then_inc(consts_made, 1)
            pool.iota(q_i[:, :], [[0, 1]], base=0, channel_multiplier=1).then_inc(consts_made, 1)
            pool.memset(seg[:, :, :], 1.0).then_inc(pool_step, 1)
            pool.memset(seg2[:, :, :], 1.0).then_inc(pool_step, 1)
            pool.memset(own[:, :], 1.0).then_inc(pool_step, 1)
            pool.wait_ge(pool_step, 5)
            pool.memset(seg[:, :, 0:1], 0.0).then_inc(consts_made, 1)
            pool.memset(seg2[:, :, 0:1], 0.0).then_inc(consts_made, 1)
            pool.memset(parts[:, :, 0:1], 0.0).then_inc(consts_made, 1)
            pool.affine_select(out=own[:, :], in_=own[:, :], compare_op=ALU.is_ge, fill=0.0, base=0,
                               pattern=[[-MBLK, E]], channel_multiplier=1).then_inc(pool_step, 1)
            pool.wait_ge(pool_step, 6)
            pool.affine_select(out=own[:, :], in_=own[:, :], compare_op=ALU.is_ge, fill=0.0, base=MBLK - 1,
                               pattern=[[MBLK, E]], channel_multiplier=-1).then_inc(consts_made, 1)
            pool.iota(run[0][:, :], [[TOK, E]], base=0, channel_multiplier=0, **io).then_inc(consts_made, 1)
            pool.iota(token_id[:, :], [[P, NBLK]], base=1, channel_multiplier=1, **io).then_inc(consts_made, 1)
            pool.iota(spare_row[:, :, :],
                      [[0, TILES], [P, WIDE]], base=TOK + 1, channel_multiplier=1, **io).then_inc(consts_made, 1)
            pool.wait_ge(xtok_loaded, 16)
            pool.dma_start(out_d[TOK:TOK + TILE, :].rearrange("(i p) c -> p i c", p=P),
                           x1[:, 0:WIDE, :]).then_inc(y_added, 16)
            steps = [0]

            def then(ins):
                steps[0] += 1
                ins.then_inc(newton_step, 1)
                pool.wait_ge(newton_step, steps[0])

            def inverse_std(g):
                c = slice(g * BLKU, (g + 1) * BLKU)
                y = rstd_i[:, c].bitcast(F32)
                pool.wait_ge(guess_ready, g + 1)
                for _ in range(3):
                    then(pool.tensor_tensor(rt[:, c], y, rhv[:, c], ALU.mult))
                    then(pool.tensor_tensor(rt[:, c], rt[:, c], y, ALU.mult))
                    then(pool.tensor_scalar(rt[:, c], rt[:, c], 1.5, None, ALU.add))
                    then(pool.tensor_tensor(y, rt[:, c], y, ALU.mult))
                pool.tensor_tensor(nmr[:, c], nmean[:, c], y, ALU.mult).then_inc(nmr_ready, 1)

            def token_norm(g):
                pool.wait_ge(nmr_ready, g + 1)
                for i in range(g * BLKU + 2, (g + 1) * BLKU):
                    pool.tensor_scalar(xn2[:, i, 0:C], x1[:, i, :], rstd_i[:, i:i + 1].bitcast(F32), nmr[:, i:i + 1],
                                       ALU.mult, ALU.add).then_inc(xn2_more, 1)

            def expert_scores(half):
                pool.wait_ge(norm_ready, half + 1)
                then(pool.tensor_tensor(topg[:, :, :], topp[:, :, :].rearrange("p i k -> p k i"),
                                        g2[:, :].unsqueeze(1).broadcast_to([P, 2, HALF]), ALU.mult))
                then(pool.tensor_tensor(scored[:, :, :, :], hot_e[:, :, :, :],
                                        topg[:, :, :].unsqueeze(3).broadcast_to([P, 2, HALF, E]), ALU.mult))
                pool.tensor_tensor(xn2[:, half * HALF:(half + 1) * HALF, C:], scored[:, 0, :, :], scored[:, 1, :, :],
                                   ALU.add).then_inc(scores_ready, 1)

            def w_low(k):
                c = slice(k * PIECE, (k + 1) * PIECE)
                pool.wait_ge(whi_done, k + 1)
                pool.tensor_tensor(w_lo[0][:, c], w_raw[0][:, c], w_hi[0][:, c].bitcast(F32),
                                   ALU.subtract).then_inc(w_split, 1)

            def row_hots(half):
                pool.wait_ge(rq_ready, half + 1)
                if half:
                    pool.wait_ge(inv_ready, half)
                for i in range(POOL_HOTS):
                    pool.tensor_scalar(hot_r[:, 0, i, :], iota_r[:, :], rf[:, 0, i:i + 1], None, ALU.is_equal
                                       ).then_inc(hot_r_ready, 1)

            for g in range(GROUPS):
                inverse_std(g)
                if g < 2:
                    token_norm(g)
            for k in range(2):
                w_low(k)
            expert_scores(0)
            row_hots(0)
            for k in range(2, 5):
                w_low(k)
            expert_scores(1)
            row_hots(1)
            for k in range(5, HJ):
                w_low(k)

            def gather(n):
                pool.tensor_copy(idx_in[:, :], row_in[:, bass.ds(n, 1), :].rearrange("p a w -> p (a w)")
                                 ).then_inc(idx_in_set, 1)
                pool.wait_ge(idx_in_set, n + 1)
                pool.sem_inc(gathers_begun, 1)
                for i in range(WIDE):
                    pool.indirect_dma_start(xg[:, i, :], None, xs_d,
                                            bass.IndirectOffsetOnAxis(ap=idx_in[:, i:i + 1], axis=0)
                                            ).then_inc(x_gathered, 16)

            def keep_scores(n):
                pool.wait_ge(x_gathered, (n + 1) * (16 * WIDE))
                pool.sem_inc(scores_begun, 1)
                pool.tensor_copy(score_next[:, :, :], xg[:, :, C:]).then_inc(scores_kept, 1)

            def move_scores(n):
                pool.wait_ge(scores_kept, n + 1)
                pool.sem_inc(scores_begun, 1)
                pool.tensor_copy(score[:, :, :], score_next[:, :, :]).then_inc(scores_moved, 1)

            pool.wait_ge(slots_ready, 1)
            pool.wait_ge(xs_stored, 32)
            gather(0)
            pool.wait_ge(bounds_ready, 2)
            t0, odd0 = 0, 0
            keep_scores(0)
            move_scores(0)
            pool.wait_ge(xg_turned, 1)
            gather(1)
            pool.wait_ge(slots_ready, 2)
            pool.wait_ge(x1_stored, 16)

            def tile(t, e, block, width):
                pool.wait_ge(scores_moved, t + 1)
                keep_scores(t + 1)
                pool.wait_ge(scores_kept, t + 2)
                pool.wait_ge(xg_turned, t + 2)
                gather(t + 2)
                pool.wait_ge(y_added, block * 16 + 16)
                pool.tensor_copy(idx_out[:, :], row_out[:, bass.ds(t, 1), :].rearrange("p a w -> p (a w)")
                                 ).then_inc(idx_out_set, 1)
                pool.wait_ge(idx_out_set, t + 1)
                pool.sem_inc(y_free, 1)
                pool.wait_ge(y_weighted, t + 2)
                pool.sem_inc(adds_begun, 1)
                for i in range(width):
                    pool.indirect_dma_start(out_d, bass.IndirectOffsetOnAxis(ap=idx_out[:, i:i + 1], axis=0),
                                            y_out[:, i, :], None, compute_op=ALU.add).then_inc(y_added, 16)
                move_scores(t + 1)

            for e in range(E):
                t1, odd, more = expert_bounds(pool, e)
                odd1 = pool.value_load(bounds[0:1, 1, e:e + 1], min_val=0, max_val=E)
                with pool.If(odd):
                    tile(t0, e, t0 * 2 + odd0, WIDE)
                with pool.Else():
                    tile(t0, e, t0 * 2 + odd0, 2)
                with pool.If(more):
                    with pool.Fori(t0 + 1, t1) as t:
                        tile(t, e, t * 2 + odd1, 2)
                t0 = t1
                odd0 = odd1
            pool.wait_ge(y_added, t1 * 32 + odd1 * 16 + 16)
            pool.wait_ge(x_gathered, (t1 + 2) * (16 * WIDE))

        @block.scalar
        def _(act):
            act.wait_ge(consts_made, 14)
            act.activation(warm[:, :], eps_c[:, :], ACT.Sqrt)

            def square(u):
                act.wait_ge(centred, u + 1)
                if u >= 2:
                    act.wait_ge(var_ready, u - 1)
                act.activation(sq[u % 2][:, :, :], x_cn[:, :, u * UNIT:(u + 1) * UNIT], ACT.Square
                               ).then_inc(sq_ready, 1)

            def root(u):
                act.wait_ge(var_ready, u + 1)
                act.activation(std[:, u, :], banks[:, u, 0:BLKU], ACT.Sqrt, bias=eps_c[:, :]).then_inc(std_ready, 1)

            square(0)
            square(1)
            root(0)
            square(2)
            root(1)
            square(3)
            root(2)
            root(3)
            act.wait_ge(conv_loaded, 16 * 10)

            def take(kind, u):
                n = AT[kind, u]
                b = u // 2
                act.wait_ge(proj_ready, n + 1)
                if u >= 2:
                    if kind in ("q1", "k1"):
                        act.wait_ge(proj_ready, AT[kind[0] + "2", u - 2] + 1)
                    elif kind == "v":
                        act.wait_ge(vt_ready, u - 1)
                    else:
                        act.wait_ge(q_split if kind == "q2" else k_split, u - 1)
                dst = {"q1": q1r, "q2": q2r, "k1": k1r, "k2": k2r, "v": vr}[kind][u % 2]
                g = {"q1": 0, "q2": 2, "k1": 4, "k2": 6, "v": 8}[kind]
                bias = {"k1": kbias[:, b:b + 1], "v": vbias[:, b:b + 1]}.get(kind, aff[:, g + 1:g + 2])
                act.activation(dst[:, :], banks[:, n % 4, :], ACT.Relu, bias=bias, scale=aff[:, g:g + 1]
                               ).then_inc(proj_out, 1)

            def vt_high(u):
                act.wait_ge(vt_ready, u + 1)
                act.activation(vt[u // 2][0][:, u % 2 * BLKU:(u % 2 + 1) * BLKU, :],
                               banks[:, 5 + u % 2, :].rearrange("p (i c) -> p i c", i=BLKU), ACT.Copy
                               ).then_inc(vt_hi_done, 1)

            def global_exp(b):
                act.wait_ge(gmax_ready, b + 1)
                for k in range(KC):
                    if b == 0:
                        act.wait_ge(var_ready, UNITS)
                    else:
                        act.wait_ge(gvec_ready, b)
                    act.activation(sq[k][:, :, :].rearrange("p h n -> p (h n)"), x_cn[:, k, b * N:(b + 1) * N],
                                   ACT.Exp, bias=gmax[:, b, k:k + 1], accum_out=gsum[:, b, k:k + 1]
                                   ).then_inc(gexp_ready, 1)

            for b in range(B):
                for item in (("q1", 2 * b), ("q1", 2 * b + 1), ("q2", 2 * b), ("q2", 2 * b + 1)):
                    take(*item)
                global_exp(b)
            for b in range(B):
                u, w = 2 * b, 2 * b + 1
                act.wait_ge(gbias_ready, b + 1)
                for item in (("k1", u), ("v", u), ("k1", w), ("v", w)):
                    take(*item)
                vt_high(u)
                take("k2", u)
                vt_high(w)
                take("k2", w)

            def exp_row(r):
                act.wait_ge(rmax_ready, r + 1)
                if r >= 2:
                    act.wait_ge(t_ready, 2 * (r - 1))
                act.activation(prob[r % 2][:, :].rearrange("p (h m) -> p h m", h=2),
                               banks[:, 2 * (r % 2):2 * (r % 2) + 2, :], ACT.Exp, bias=rneg[:, r:r + 1], scale=SCALE,
                               accum_out=rsum[:, r:r + 1]).then_inc(exp_done, 1)

            def pt_high(r, h):
                g, i = divmod(r, BLKU)
                act.wait_ge(t_ready, 2 * r + h + 1)
                if g >= 2:
                    act.wait_ge(pv_ready, g - 1)
                act.activation(pt_hi[g % 2][:, 4 * h:4 * h + 4, i * P:(i + 1) * P],
                               banks[:, 4 + h, :].rearrange("p (m n) -> p m n", m=4), ACT.Copy
                               ).then_inc(pt_hi_done, 1)

            act.wait_ge(k_split, UNITS)

            def ctx_high(g):
                act.wait_ge(pv_ready, g + 1)
                if g:
                    act.wait_ge(o_ready, 2 * g)
                act.activation(ctx_hi[:, :], banks[:, CTX_BANK[g], :], ACT.Copy).then_inc(ctx_hi_done, 1)

            def token_norm(g):
                act.wait_ge(nmr_ready, g + 1)
                for i in range(g * BLKU, (g + 1) * BLKU if g >= 2 else g * BLKU + 2):
                    act.activation(xn2[:, i, 0:C], x1[:, i, :], ACT.Identity, bias=nmr[:, i:i + 1],
                                   scale=rstd_i[:, i:i + 1].bitcast(F32)).then_inc(xn2_ready, 1)

            def xt_copy(i):
                act.wait_ge(xt_ready, i + 1)
                act.activation(xt2[:, 2 * i:2 * i + 2, :, :],
                               banks[:, XT_BANK[i], :].rearrange("p (i k n) -> p i k n", i=2, k=KC), ACT.Copy
                               ).then_inc(xt_copied, 1)

            def gate_exp(half):
                act.wait_ge(shifted, 2 * half + 2)
                if half:
                    act.wait_ge(norm_ready, half)
                act.activation(gate[:, :, :], low[:, :, :], ACT.Exp).then_inc(expd, 1)

            def w_high(k):
                act.wait_ge(pv_ready, GROUPS)
                act.wait_ge(w_loaded[0], 32)
                c = slice(k * PIECE, (k + 1) * PIECE)
                act.activation(w_hi[0][:, c], w_raw[0][:, c], ACT.Copy).then_inc(whi_done, 1)

            def row_hots(half):
                act.wait_ge(r_neg_ready, half + 1)
                if half:
                    act.wait_ge(inv_ready, half)
                for i in range(HALF):
                    n = half * HALF + i
                    if n >= 2:
                        act.wait_ge(hot_r_more, n - 1)
                    act.activation(apart[:, n % 2, :], iota_r[:, :], ACT.Abs, bias=r_neg[:, i:i + 1]
                                   ).then_inc(r_apart, 1)
                    if i:
                        act.wait_ge(r_apart, n)
                        act.activation(hot_r[:, 1, i - 1, :], apart[:, (n - 1) % 2, :], ACT.Relu, bias=ones[:, 0:1],
                                       scale=-1.0).then_inc(hot_r_more, 1)
                act.wait_ge(r_apart, (half + 1) * HALF)
                act.activation(hot_r[:, 1, HALF - 1, :], apart[:, (HALF - 1) % 2, :], ACT.Relu, bias=ones[:, 0:1],
                               scale=-1.0).then_inc(hot_r_more, 1)

            for step in range(NBLK + 1):
                if step:
                    pt_high(step - 1, 0)
                    pt_high(step - 1, 1)
                if step < NBLK:
                    exp_row(step)
                if step in (8, 12, 16):
                    ctx_high(step // 4 - 2)
                if step == 12:
                    token_norm(0)
                if step == 13:
                    xt_copy(0)
                    xt_copy(1)
            ctx_high(3)
            token_norm(1)
            xt_copy(2)
            xt_copy(3)
            token_norm(2)
            gate_exp(0)
            xt_copy(4)
            xt_copy(5)
            for k in range(2):
                w_high(k)
            token_norm(3)
            xt_copy(6)
            xt_copy(7)
            w_high(2)
            row_hots(0)
            gate_exp(1)
            for k in range(3, HJ):
                w_high(k)
            row_hots(1)
            act.wait_ge(inv_ready, 2)
            act.activation(slot_t[:, :], banks[:, INV_BANK, 0:P], ACT.Copy).then_inc(inv_taken, 1)
            act.activation(warm[:, :], eps_c[:, :], ACT.Gelu)

            def x_high(n):
                act.wait_ge(xg_turned, n + 1)
                act.activation(x_hi[:, :, :], banks[:, 6:8, 0:TILE], ACT.Copy
                               ).then_inc(xhi_done, 1)

            def tile(t, e, width, split):
                w = width * P
                for j in range(HJ):
                    act.wait_ge(l1_ready, t * HJ + (j + 1))
                    act.wait_ge(h_split, t * HJ + (j + 1))
                    bias = b1t[:, e * HJ + j:e * HJ + j + 1]
                    act.activation(h_raw[j % RING][:, 0:w], banks[:, j % RING, 0:w], ACT.Gelu, bias=bias)
                    act.wait_ge(l2_done, t * HJ + (j + 1))
                    act.activation(h_hi[:, j, 0:w], banks[:, j % RING, 0:w], ACT.Gelu, bias=bias
                                   ).then_inc(gelu_done, 1)
                    if split and e + 1 < E:
                        if j == 0:
                            act.wait_ge(w_loaded[(e + 1) % 2], 32 * ((e + 1) // 2 + 1))
                            act.wait_ge(l2_done, t * HJ + HJ)
                        c = slice(j * PIECE, (j + 1) * PIECE)
                        if j == HJ - 1:
                            x_high(t + 1)
                        act.activation(w_hi[(e + 1) % 2][:, c], w_raw[(e + 1) % 2][:, c], ACT.Copy
                                       ).then_inc(whi_done, 1)
                if not (split and e + 1 < E):
                    x_high(t + 1)

            act.sem_inc(gelu_done, RING)
            act.wait_ge(bounds_ready, 2)
            experts = [expert_bounds(act, e) for e in range(E)]
            t0 = 0
            x_high(0)
            act.wait_ge(bias_loaded, 32)
            for e in range(E):
                t1, odd, more = experts[e]
                with act.If(odd):
                    tile(t0, e, WIDE, True)
                with act.Else():
                    tile(t0, e, 2, True)
                with act.If(more):
                    with act.Fori(t0 + 1, t1) as t:
                        tile(t, e, 2, False)
                t0 = t1

        @block.vector
        def _(dve):
            steps = [0]

            def then(ins):
                steps[0] += 1
                ins.then_inc(dve_step, 1)
                dve.wait_ge(dve_step, steps[0])

            dve.memset(ones[:, :], 1.0).then_inc(ones_made, 1)
            dve.wait_ge(consts_made, 14)
            then(dve.tensor_scalar(k_i[:, 0:1], q_i[:, :], MBLK - 1, None, ALU.bitwise_and))
            then(dve.tensor_scalar(k_i[:, 1:2], k_i[:, 0:1], 1, None, ALU.logical_shift_right))
            then(dve.tensor_copy(k_f[:, :], k_i[:, :]))
            then(dve.tensor_tensor(k_col[:, :], k_f[:, 0:1], k_f[:, 1:2], ALU.add))
            dve.tensor_scalar(k_one[:, :], k_f[:, 0:1], 1.0, None, ALU.add).then_inc(dve_step, 1)
            steps[0] += 1
            then(dve.tensor_scalar(k_move[:, :], k_col[:, :], -1.0, 2.0, ALU.mult, ALU.add))
            for u in range(UNITS):
                c = x_cn[:, :, u * UNIT:(u + 1) * UNIT]
                dve.wait_ge(mean_ready, u + 1)
                dve.tensor_tensor(c, c, banks[:, u:u + 1, :].broadcast_to([P, KC, UNIT]), ALU.subtract
                                  ).then_inc(centred, 1)

            def spread_root(u):
                dve.wait_ge(std_ready, u + 1)
                if u >= 2:
                    dve.wait_ge(rstd_ready, u - 1)
                then(dve.reciprocal(std[:, u, :], std[:, u, :]))
                dve.tensor_tensor(diag[u % 2][:, :, :], ident[:, :].unsqueeze(1).broadcast_to([P, BLKU, P]),
                                  std[:, u, :].unsqueeze(2).broadcast_to([P, BLKU, P]), ALU.mult
                                  ).then_inc(diag_ready, 1)

            def norm(u):
                c = x_cn[:, :, u * UNIT:(u + 1) * UNIT]
                dve.wait_ge(rstd_ready, u + 1)
                dve.tensor_tensor(c, c, banks[:, 4 + u:5 + u, :].broadcast_to([P, KC, UNIT]), ALU.mult
                                  ).then_inc(normed, 1)

            def global_max(b):
                dve.wait_ge(normed, 2 * b + 2)
                then(dve.tensor_reduce(gmax[:, b, :], x_cn[:, :, b * N:(b + 1) * N], AX.X, ALU.max))
                dve.tensor_scalar(gmax[:, b, :], gmax[:, b, :], -1.0, None, ALU.mult).then_inc(gmax_ready, 1)

            def global_vector(b):
                dve.wait_ge(gexp_ready, KC * (b + 1))
                for k in range(KC):
                    e = sq[k][:, :, :].rearrange("p h n -> p (h n)")
                    then(dve.scalar_tensor_tensor(e, e, 1.0 / N, x_cn[:, k, b * N:(b + 1) * N],
                                                  ALU.mult, ALU.mult, accum_out=gdot[:, b, k:k + 1]))
                then(dve.reciprocal(gsum[:, b, :], gsum[:, b, :]))
                dve.tensor_tensor(gvec[:, b, :], gdot[:, b, :], gsum[:, b, :], ALU.mult).then_inc(gvec_ready, 1)

            def global_bias(b):
                dve.wait_ge(gproj_ready, b + 1)
                dve.tensor_scalar(kbias[:, b:b + 1], banks[:, 4, 2 * b:2 * b + 1], aff[:, 4:5], aff[:, 5:6],
                                  ALU.mult, ALU.add).then_inc(dve_step, 1)
                dve.tensor_scalar(vbias[:, b:b + 1], banks[:, 4, 2 * b + 1:2 * b + 2], aff[:, 8:9], aff[:, 9:10],
                                  ALU.mult, ALU.add).then_inc(gbias_ready, 1)
                steps[0] += 1

            def split(kind, u, raw, done):
                hi, lo = qk[u // 2][0:2] if kind == "q2" else qk[u // 2][2:4]
                dve.wait_ge(proj_out, AT[kind, u] + 1)
                c = slice(u % 2 * UNIT, (u % 2 + 1) * UNIT)
                then(dve.tensor_copy(hi[:, c], raw[u % 2][:, :]))
                dve.tensor_tensor(lo[:, c], raw[u % 2][:, :], hi[:, c].bitcast(F32), ALU.subtract).then_inc(done, 1)

            def vt_low(u):
                dve.wait_ge(vt_hi_done, u + 1)
                c = slice(u % 2 * BLKU, (u % 2 + 1) * BLKU)
                hi, lo = vt[u // 2]
                dve.tensor_tensor(lo[:, c, :], banks[:, 5 + u % 2, :].rearrange("p (i c) -> p i c", i=BLKU),
                                  hi[:, c, :].bitcast(F32), ALU.subtract).then_inc(vt_split, 1)

            def row_max(r):
                dve.wait_ge(s_ready, r + 1)
                then(dve.tensor_reduce(rmax[:, r:r + 1], banks[:, 2 * (r % 2):2 * (r % 2) + 2, :], AX.XY, ALU.max))
                dve.tensor_scalar(rneg[:, r:r + 1], rmax[:, r:r + 1], -SCALE, None, ALU.mult).then_inc(rmax_ready, 1)

            spread_root(0)
            spread_root(1)
            norm(0)
            norm(1)
            spread_root(2)
            spread_root(3)
            global_max(0)
            norm(2)
            norm(3)
            split("q2", 0, q2r, q_split)
            split("q2", 1, q2r, q_split)
            global_vector(0)
            global_max(1)
            split("q2", 2, q2r, q_split)
            split("q2", 3, q2r, q_split)
            global_bias(0)
            global_vector(1)
            dve.wait_ge(conv_loaded, 16 * 10)
            then(dve.tensor_tensor(w_og[:, :], w_o[:, :], og[:, :], ALU.mult))
            then(dve.tensor_copy(wo_hi[:, :], w_og[:, :]))
            dve.tensor_tensor(wo_lo[:, :], w_og[:, :], wo_hi[:, :].bitcast(F32), ALU.subtract).then_inc(wo_split, 1)
            global_bias(1)
            for b in range(B):
                for u in (2 * b, 2 * b + 1):
                    vt_low(u)
                    split("k2", u, k2r, k_split)

            def pt_low(r, h):
                g, i = divmod(r, BLKU)
                dve.wait_ge(pt_hi_done, 2 * r + h + 1)
                c = pt_hi[g % 2][:, 4 * h:4 * h + 4, i * P:(i + 1) * P]
                dve.tensor_tensor(pt_lo[g % 2][:, 4 * h:4 * h + 4, i * P:(i + 1) * P],
                                  banks[:, 4 + h, :].rearrange("p (m n) -> p m n", m=4), c.bitcast(F32),
                                  ALU.subtract).then_inc(pt_split, 1)

            def out_taken(n):
                g = n // 2
                if n % 2 == 0:
                    dve.wait_ge(exp_done, BLKU * (g + 1))
                    then(dve.reciprocal(rinv[:, g * BLKU:(g + 1) * BLKU], rsum[:, g * BLKU:(g + 1) * BLKU]))
                dve.wait_ge(o_ready, n + 1)
                for i in range(2):
                    k = 2 * n + i
                    ins = dve.scalar_tensor_tensor(o_tmp[:, i, :], banks[:, O_BANK[n], i * C:(i + 1) * C],
                                                   rinv[:, k:k + 1], ob[:, :], ALU.mult, ALU.add)
                    if i == 0:
                        ins.then_inc(dve_step, 1)
                        steps[0] += 1
                    else:
                        ins.then_inc(o_taken, 1)

            def out_rows(n):
                dve.wait_ge(o_taken, n + 1)
                dve.wait_ge(dve_step, steps[0])
                for k in (2 * n, 2 * n + 1):
                    dve.scalar_tensor_tensor(x1[:, k, :], o_tmp[:, k % 2, :], 0.0, x1[:, k, :], ALU.max, ALU.add
                                             ).then_inc(x1_ready, 1)
                for k in (2 * n, 2 * n + 1):
                    dve.wait_ge(x1_ready, k + 1)
                    dve.bn_stats(bst[:, k, :], x1[:, k, :]).then_inc(dve_step, 1)
                steps[0] += 2
                dve.wait_ge(dve_step, steps[0])
                for k in (2 * n, 2 * n + 1):
                    dve.bn_aggr(mv[:, k, :], bst[:, k, :]).then_inc(dve_step, 1)
                steps[0] += 2
                if n % 2:
                    dve.wait_ge(dve_step, steps[0])
                    guess_std(n // 2)

            def guess_std(g):
                c = slice(g * BLKU, (g + 1) * BLKU)
                dve.tensor_scalar(nmean[:, c], mv[:, c, 0], -1.0, None, ALU.mult).then_inc(dve_step, 1)
                steps[0] += 1
                then(dve.tensor_scalar(rv[:, c], mv[:, c, 1], TOK_EPS, None, ALU.add))
                dve.tensor_scalar(rhv[:, c], rv[:, c], -0.5, None, ALU.mult).then_inc(dve_step, 1)
                steps[0] += 1
                then(dve.tensor_scalar(ri0[:, c], rv[:, c].bitcast(I32), 1, None, ALU.logical_shift_right))
                dve.tensor_scalar(rstd_i[:, c], ri0[:, c], -1.0, float(0x5F3759DF), ALU.mult, ALU.add
                                  ).then_inc(guess_ready, 1)

            spread = [P, HALF, E]
            spread2 = [P, 2, HALF, E]

            def route_gates(half):
                dve.wait_ge(lg_ready, HALF // 2 * (half + 1))
                if half:
                    dve.wait_ge(scores_ready, half)
                then(dve.tensor_copy(lg[:, :, :], banks[:, LG_BANK[half], 0:HALF * E]
                                     .rearrange("p (i e) -> p i e", e=E)))
                for i in range(HALF):
                    dve.max(top8[:, i, :], lg[:, i, :]).then_inc(dve_step, 1)
                steps[0] += HALF
                dve.wait_ge(dve_step, steps[0])
                top = top8[:, :, 0:1]
                dve.tensor_tensor(low[:, :, 0:E], lg[:, :, :], top.broadcast_to(spread), ALU.subtract
                                  ).then_inc(shifted, 1)
                dve.tensor_tensor(low[:, :, E:], top8[:, :, 0:2], top.broadcast_to([P, HALF, 2]), ALU.subtract
                                  ).then_inc(shifted, 1)
                for i in range(HALF):
                    dve.max_index(idx8[:, i, :], top8[:, i, :], lg[:, i, :]).then_inc(dve_step, 1)
                steps[0] += HALF
                dve.wait_ge(dve_step, steps[0])
                then(dve.tensor_copy(idxf[:, :, :], idx8[:, :, 0:2].rearrange("p i k -> p k i")))
                then(dve.tensor_tensor(hot_e[:, :, :, :], iota_e[:, :].unsqueeze(1).unsqueeze(1).broadcast_to(spread2),
                                       idxf[:, :, :].unsqueeze(3).broadcast_to(spread2), ALU.is_equal))
                dve.tensor_tensor(sel[:, :, :].rearrange("p e i -> p i e"), hot_e[:, 0, :, :], hot_e[:, 1, :, :],
                                  ALU.add).then_inc(sel_ready, 1)
                dve.wait_ge(expd, half + 1)
                then(dve.tensor_reduce(g1[:, :], gate[:, :, 0:E], AX.X, ALU.add))
                then(dve.reciprocal(g1[:, :], g1[:, :]))
                then(dve.tensor_tensor(topp[:, :, :], gate[:, :, E:], g1[:, :].unsqueeze(2).broadcast_to([P, HALF, 2]),
                                       ALU.mult))
                then(dve.scalar_tensor_tensor(g2[:, :], topp[:, :, 0], GATE_EPS, topp[:, :, 1], ALU.add, ALU.add))
                dve.reciprocal(g2[:, :], g2[:, :]).then_inc(norm_ready, 1)

            def route_ranks(half):
                dve.wait_ge(rank_ready, half + 1)
                bank = banks[:, RANK_BANK[half], 0:2 * E * HALF]
                if half:
                    dve.wait_ge(hot_r_ready, POOL_HOTS)
                    dve.wait_ge(r_apart, HALF)
                then(dve.tensor_tensor_scan(incl[:, :, :].rearrange("p e i -> p (e i)"),
                                            seg[:, :, :].rearrange("p e i -> p (e i)"), bank[:, E * HALF:],
                                            0.0, ALU.mult, ALU.add))
                then(dve.tensor_tensor(incl[:, :, :], incl[:, :, :], run[half][:, :].unsqueeze(2)
                                       .broadcast_to([P, E, HALF]), ALU.add))
                dve.tensor_copy(run[half + 1][:, :], incl[:, :, HALF - 1]).then_inc(dve_step, 1)
                steps[0] += 1
                dve.tensor_tensor(rank[:, :, :], incl[:, :, :], bank[:, 0:E * HALF].rearrange("p (e i) -> p e i", e=E),
                                  ALU.add).then_inc(rank_taken, 1)
                dve.wait_ge(rank_taken, half + 1)
                then(dve.tensor_tensor(pos3[:, :, :, :], hot_e[:, :, :, :],
                                       rank[:, :, :].rearrange("p e i -> p i e").unsqueeze(1).broadcast_to(spread2),
                                       ALU.mult))
                then(dve.tensor_reduce(posf[:, :, :], pos3[:, :, :, :], AX.X, ALU.add))
                then(dve.tensor_copy(posi[:, :, :], posf[:, :, :]))
                then(dve.tensor_scalar(qi[:, :, :], posi[:, :, :], 7, None, ALU.logical_shift_right))
                then(dve.tensor_scalar(ri[:, :, :], posi[:, :, :], P - 1, None, ALU.bitwise_and))
                then(dve.tensor_copy(qf[:, :, :], qi[:, :, :]))
                dve.tensor_copy(rf[:, :, :], ri[:, :, :]).then_inc(rq_ready, 1)
                dve.wait_ge(rq_ready, half + 1)
                dve.tensor_scalar(r_neg[:, :], rf[:, 1, :], -1.0, None, ALU.mult).then_inc(r_neg_ready, 1)

            def column_hot(half, n):
                k, i = divmod(n, HALF)
                b = half * HALF + i
                dve.tensor_scalar(hot_q[:, k, i, :], iota_r[:, :], qf[:, k, i:i + 1], token_id[:, b:b + 1],
                                  ALU.is_equal, ALU.mult).then_inc(hot_q_ready, 1)

            def hots(half, last):
                dve.wait_ge(rq_ready, half + 1)
                if half:
                    dve.wait_ge(inv_ready, half)
                for i in range(POOL_HOTS, HALF):
                    dve.tensor_scalar(hot_r[:, 0, i, :], iota_r[:, :], rf[:, 0, i:i + 1], None, ALU.is_equal
                                      ).then_inc(hot_r_rest, 1)
                for n in range(last):
                    column_hot(half, n)

            def meanwhile(ins, n):
                steps[0] += 1
                ins.then_inc(dve_step, 1)
                column_hot(1, n)
                dve.wait_ge(dve_step, steps[0])

            dve.wait_ge(xtok_loaded, 16)
            dve.wait_ge(y_added, 16)
            def context_low(g):
                dve.wait_ge(ctx_hi_done, g + 1)
                dve.tensor_tensor(ctx_lo[:, :], banks[:, CTX_BANK[g], :], ctx_hi[:, :].bitcast(F32),
                                  ALU.subtract).then_inc(ctx_split, 1)

            for step in range(NBLK + 1):
                if step < NBLK:
                    row_max(step)
                if step - 1 in O_STEP[:3]:
                    out_rows(O_STEP.index(step - 1))
                if step:
                    pt_low(step - 1, 0)
                    pt_low(step - 1, 1)
                if step in (8, 12, 16):
                    context_low(step // 4 - 2)
                if step in O_STEP:
                    out_taken(O_STEP.index(step))
            out_rows(3)
            out_taken(4)
            out_rows(4)
            out_taken(5)
            context_low(3)
            out_rows(5)
            for n in (6, 7):
                out_taken(n)
                out_rows(n)
            for half in range(2):
                route_gates(half)
                route_ranks(half)
                hots(half, (2 * HALF, 6)[half])

            meanwhile(dve.scalar_tensor_tensor(blocks_i[:, 0, :], run[2][:, :], float(P - 1), run[0][:, :],
                                               ALU.add, ALU.subtract), 6)
            meanwhile(dve.tensor_scalar(blocks_i[:, 1, :], blocks_i[:, 0, :], 7, None, ALU.logical_shift_right), 7)
            meanwhile(dve.tensor_scalar(parts_i[:, 2, :], blocks_i[:, 1, :], float(LEAST), None, ALU.max), 8)
            dve.tensor_scalar(parts_i[:, 0, :], parts_i[:, 2, :], 1, None, ALU.logical_shift_right
                              ).then_inc(dve_step, 1)
            steps[0] += 1
            meanwhile(dve.tensor_scalar(parts_i[:, 1, :], parts_i[:, 2, :], 1, None, ALU.bitwise_and), 9)
            meanwhile(dve.tensor_copy(parts[:, :, 1:], parts_i[:, :, :]), 10)
            meanwhile(dve.tensor_tensor_scan(before[:, :, :].rearrange("p a e -> p (a e)"),
                                             seg2[:, :, :].rearrange("p a e -> p (a e)"),
                                             parts[:, 0:2, :].rearrange("p a e -> p (a e)"), 0.0, ALU.mult,
                                             ALU.add), 11)
            dve.scalar_tensor_tensor(scrap[:, 0, :], before[:, 0, 0:E], float(WIDE), own[:, :], ALU.mult, ALU.mult,
                                     accum_out=col_a[:, :]).then_inc(dve_step, 1)
            steps[0] += 1
            meanwhile(dve.tensor_tensor(odd_m[:, :], parts[:, 1, 1:], parts[:, 2, 1:], ALU.mult), 12)
            meanwhile(dve.scalar_tensor_tensor(scrap[:, 1, :], odd_m[:, :], 1.0, own[:, :], ALU.mult, ALU.mult,
                                               accum_out=col_z[:, :]), 13)
            meanwhile(dve.tensor_scalar(col_z[:, :], col_z[:, :], k_one[:, :], k_move[:, :], ALU.is_equal,
                                        ALU.mult), 14)
            meanwhile(dve.tensor_scalar(col_q[:, :], col_z[:, :], col_a[:, :], k_col[:, :], ALU.add, ALU.add), 15)
            dve.tensor_scalar(place[:, :], iota_r[:, 0:SLOTS], col_q[:, :], None, ALU.is_equal
                              ).then_inc(place_ready, 1)
            then(dve.tensor_scalar(many[:, :], parts[0:1, 0, 1:], 1.0, None, ALU.is_gt))
            then(dve.scalar_tensor_tensor(flags[:, :], parts[0:1, 1, 1:], 2.0, many[:, :], ALU.mult, ALU.add))
            dve.scalar_tensor_tensor(bounds[:, 0, :], before[0:1, 0, 1:], 4.0, flags[:, :], ALU.mult, ALU.add
                                     ).then_inc(bounds_ready, 1)
            dve.tensor_copy(bounds[:, 1, :], before[0:1, 1, 1:]).then_inc(bounds_ready, 1)
            dve.wait_ge(table_ready, 1)
            table = banks[:, TABLE_BANK, 0:SLOTS].rearrange("p (t w) -> p t w", w=WIDE)
            dve.tensor_scalar(row_in[:, :, :], table, -1.0, 0.0, ALU.add, ALU.max).then_inc(slots_ready, 1)
            then(dve.scalar_tensor_tensor(empty[:, :, :], table, 0.0, spare_row[:, :, :], ALU.is_equal, ALU.mult))
            dve.scalar_tensor_tensor(row_out[:, :, :], table, -1.0, empty[:, :, :], ALU.add, ALU.add
                                     ).then_inc(slots_ready, 1)
            dve.wait_ge(bounds_ready, 2)
            experts = [expert_bounds(dve, e) for e in range(E)]

            def x_low(n):
                dve.wait_ge(xhi_done, n + 1)
                dve.tensor_tensor(x_lo[:, :, :], banks[:, 6:8, 0:TILE], x_hi[:, :, :].bitcast(F32),
                                  ALU.subtract).then_inc(x_split, 1)

            def tile(t, e, width, split):
                w = width * P
                for j in range(HJ):
                    dve.wait_ge(gelu_done, t * HJ + (j + 1 + RING))
                    dve.wait_ge(l2_done, t * HJ + (j + 1))
                    dve.tensor_tensor(h_lo[:, j, 0:w], h_raw[j % RING][:, 0:w], h_hi[:, j, 0:w].bitcast(F32),
                                      ALU.subtract).then_inc(h_split, 1)
                    if split and e + 1 < E:
                        c = slice(j * PIECE, (j + 1) * PIECE)
                        if j == HJ - 1:
                            x_low(t + 1)
                        dve.wait_ge(whi_done, HJ * (e + 1) + j + 1)
                        dve.tensor_tensor(w_lo[(e + 1) % 2][:, c], w_raw[(e + 1) % 2][:, c],
                                          w_hi[(e + 1) % 2][:, c].bitcast(F32), ALU.subtract).then_inc(w_split, 1)
                if not (split and e + 1 < E):
                    x_low(t + 1)
                dve.wait_ge(l2_done, t * HJ + 2 * HJ)
                dve.wait_ge(y_weighted, t + 1)
                for i in range(width):
                    ins = dve.tensor_tensor(y_sum[:, i, :], banks[:, 4 + i % 2, i // 2 * C:(i // 2 + 1) * C],
                                            b2b[:, e * C:(e + 1) * C], ALU.add)
                ins.then_inc(y_taken, 1)
                dve.wait_ge(y_free, t + 1)
                dve.wait_ge(scores_moved, t + 1)
                dve.wait_ge(y_taken, t + 2)
                for i in range(width):
                    ins = dve.tensor_scalar(y_out[:, i, :], y_sum[:, i, :], score[:, i, e:e + 1], None, ALU.mult)
                ins.then_inc(y_weighted, 1)

            dve.sem_inc(h_split, RING)
            dve.sem_inc(y_taken, 1)
            dve.sem_inc(y_weighted, 1)
            t0 = 0
            x_low(0)
            dve.wait_ge(bias_loaded, 32)
            for e in range(E):
                t1, odd, more = experts[e]
                with dve.If(odd):
                    tile(t0, e, WIDE, True)
                with dve.Else():
                    tile(t0, e, 2, True)
                with dve.If(more):
                    with dve.Fori(t0 + 1, t1) as t:
                        tile(t, e, 2, False)
                t0 = t1

        @block.tensor
        def _(pe):
            def product3(out, a_hi, a_lo, b_hi, b_lo, start, stop):
                pe.matmul(out, a_hi, b_hi, start=start, stop=False)
                pe.matmul(out, a_hi, b_lo, start=False, stop=False)
                return pe.matmul(out, a_lo, b_hi, start=False, stop=stop)

            pe.wait_ge(ones_made, 1)
            for _ in range(9):
                pe.matmul(banks[:, 7, 0:P], ones[:, :], ones[:, :], start=True, stop=True)
            pe.wait_ge(consts_made, 14)

            def mean(u):
                pe.wait_ge(x_loaded[u], 16)
                for k in range(KC):
                    ins = pe.matmul(banks[:, u, :], avg[:, :], x_cn[:, k, u * UNIT:(u + 1) * UNIT],
                                    start=k == 0, stop=k == KC - 1)
                ins.then_inc(mean_ready, 1)

            def variance(u):
                pe.wait_ge(sq_ready, u + 1)
                pe.wait_ge(centred, u + 1)
                for j in range(BLKU):
                    for k in range(KC):
                        ins = pe.matmul(banks[:, u, j:j + 1], sq[u % 2][:, k, j * P:(j + 1) * P], avg[:, 0:1],
                                        start=k == 0, stop=k == KC - 1)
                ins.then_inc(var_ready, 1)

            def spread_rstd(u):
                pe.wait_ge(diag_ready, u + 1)
                pe.matmul(banks[:, 4 + u, :], ones[:, :], diag[u % 2][:, :, :].rearrange("p j n -> p (j n)"),
                          start=True, stop=True).then_inc(rstd_ready, 1)

            def project(kind, u):
                n = AT[kind, u]
                if n >= 4:
                    pe.wait_ge(proj_out, n - 3)
                out = banks[:, n % 4, :]
                if kind in ("q2", "k2"):
                    src, w = (q1r, w_q2) if kind == "q2" else (k1r, w_k2)
                    pe.wait_ge(proj_out, AT[kind[0] + "1", u] + 1)
                    ins = pe.matmul(out, w[:, :], src[u % 2][:, :], start=True, stop=True)
                else:
                    w = {"q1": w_q1[:, :, :], "k1": w_k1[:, KC:, :], "v": w_v[:, KC:, :]}[kind]
                    pe.wait_ge(normed, u + 1)
                    for k in range(KC):
                        ins = pe.matmul(out, w[:, k, :], x_cn[:, k, u * UNIT:(u + 1) * UNIT],
                                        start=k == 0, stop=k == KC - 1)
                ins.then_inc(proj_ready, 1)

            def project_global(b):
                pe.wait_ge(gvec_ready, b + 1)
                if b:
                    pe.wait_ge(gbias_ready, b)
                for i, w in enumerate((w_k1, w_v)):
                    for k in range(KC):
                        ins = pe.matmul(banks[:, 4, 2 * b + i:2 * b + i + 1], w[:, k, :], gvec[:, b, k:k + 1],
                                        start=k == 0, stop=k == KC - 1)
                ins.then_inc(gproj_ready, 1)

            def turn_v(u):
                pe.wait_ge(proj_out, AT["v", u] + 1)
                if u >= 2:
                    pe.wait_ge(vt_split, u - 1)
                else:
                    pe.wait_ge(normed, UNITS)
                for i in range(BLKU):
                    ins = pe.transpose(banks[:, 5 + u % 2, i * P:(i + 1) * P], vr[u % 2][:, i * P:(i + 1) * P],
                                       ident[:, :])
                ins.then_inc(vt_ready, 1)

            mean(0)
            mean(1)
            mean(2)
            variance(0)
            mean(3)
            variance(1)
            spread_rstd(0)
            spread_rstd(1)
            pe.wait_ge(conv_loaded, 16 * 10)
            pe.wait_ge(std_ready, 2)
            project("q1", 0)
            variance(2)
            project("q1", 1)
            variance(3)
            spread_rstd(2)
            spread_rstd(3)
            pe.wait_ge(std_ready, UNITS)
            for item in PROJ[2:2 * UNITS]:
                project(*item)
            for b in range(B):
                u, w = 2 * b, 2 * b + 1
                project("k1", u)
                project("v", u)
                if b == 0:
                    project_global(0)
                project("k1", w)
                project("v", w)
                if b == 0:
                    project_global(1)
                turn_v(u)
                project("k2", u)
                turn_v(w)
                project("k2", w)

            def scores(r):
                b, i = divmod(r, N // P)
                if r >= 2:
                    pe.wait_ge(exp_done, r - 1)
                if i == 0:
                    pe.wait_ge(q_split, 2 * b + 2)
                    pe.wait_ge(k_split, 2 * b + 2)
                q_hi, q_lo, k_hi, k_lo = qk[b]
                qc = slice(i * P, (i + 1) * P)
                for h in range(2):
                    kc = slice(h * UNIT, (h + 1) * UNIT)
                    ins = product3(banks[:, 2 * (r % 2) + h, :], q_hi[:, qc], q_lo[:, qc], k_hi[:, kc], k_lo[:, kc],
                                   True, True)
                ins.then_inc(s_ready, 1)

            def turn(r):
                pe.wait_ge(exp_done, r + 1)
                for h in range(2):
                    if r:
                        pe.wait_ge(pt_split, 2 * (r - 1) + h + 1)
                    for m in range(4):
                        ins = pe.transpose(banks[:, 4 + h, m * P:(m + 1) * P],
                                           prob[r % 2][:, (4 * h + m) * P:(4 * h + m + 1) * P], ident[:, :])
                    ins.then_inc(t_ready, 1)

            def context(g, quarter):
                if quarter % 2 == 0:
                    pe.wait_ge(pt_split, 2 * BLKU * (g + 1) - 1 + quarter // 2)
                if quarter == 0:
                    if g == 3:
                        pe.wait_ge(exp_done, NBLK - 1)
                    elif g:
                        pe.wait_ge(ctx_split, g)
                v_hi, v_lo = vt[g // 2]
                for m in (2 * quarter, 2 * quarter + 1):
                    ins = product3(banks[:, CTX_BANK[g], :], v_hi[:, m, :], v_lo[:, m, :],
                                   pt_hi[g % 2][:, m, :], pt_lo[g % 2][:, m, :], m == 0, m == 7)
                if quarter == 3:
                    ins.then_inc(pv_ready, 1)

            def out_conv(g, pair):
                n = 2 * g + pair
                pe.wait_ge(ctx_split, g + 1)
                if n in (1, 3):
                    pe.wait_ge(o_taken, n)
                elif n == 2:
                    pe.wait_ge(xt_copied, 2)
                elif n == 7:
                    pe.wait_ge(o_taken, 5)
                elif n >= 4:
                    pe.wait_ge(exp_done, NBLK)
                for i in range(2):
                    c = slice((2 * pair + i) * P, (2 * pair + i + 1) * P)
                    ins = product3(banks[:, O_BANK[n], i * C:(i + 1) * C], ctx_hi[:, c], ctx_lo[:, c],
                                   wo_hi[:, :], wo_lo[:, :], True, True)
                ins.then_inc(o_ready, 1)

            def turn_tokens(i):
                if i in (1, 3):
                    pe.wait_ge(xn2_more, i + 1)
                else:
                    pe.wait_ge(xn2_ready, {0: 2, 2: 4}.get(i, 2 * i - 2))
                if i in (0, 2):
                    pe.wait_ge(o_taken, i + 2)
                elif i == 3:
                    pe.wait_ge(pt_split, 2 * NBLK)
                elif i in (4, 6):
                    pe.wait_ge(ctx_split, 3 + i // 6)
                else:
                    pe.wait_ge(xt_copied, {1: 1, 5: 3, 7: 4}[i])
                for j in range(2):
                    for k in range(KC):
                        ins = pe.transpose(banks[:, XT_BANK[i], (KC * j + k) * P:(KC * j + k + 1) * P],
                                           xn2[:, 2 * i + j, k * P:(k + 1) * P], ident[:, :])
                ins.then_inc(xt_ready, 1)

            def logits(n):
                pe.wait_ge(xt_copied, n + 1)
                if n == 0:
                    pe.wait_ge(pt_split, 2 * NBLK)
                elif n == 4:
                    pe.wait_ge(o_taken, 7)
                half = n // (HALF // 2)
                for i in (2 * n, 2 * n + 1):
                    c = i % HALF * E
                    for k in range(KC):
                        ins = pe.matmul(banks[:, LG_BANK[half], c:c + E], xt2[:, i, k, :], w_g[:, k, :], start=k == 0,
                                        stop=k == KC - 1)
                ins.then_inc(lg_ready, 1)

            def ranks(half):
                pe.wait_ge(sel_ready, half + 1)
                chosen = sel[:, :, :].rearrange("p e i -> p (e i)")
                pe.wait_ge(o_taken, 6 + 2 * half)
                bank = banks[:, RANK_BANK[half], :]
                pe.matmul(bank[:, 0:E * HALF], below[:, :], chosen, start=True, stop=True)
                pe.matmul(bank[:, E * HALF:2 * E * HALF], ones[:, :], chosen, start=True, stop=True
                          ).then_inc(rank_ready, 1)

            def inverse(half, k):
                pe.wait_ge(xt_copied, 5)
                for i in range(HALF):
                    m = HALF * k + i
                    pe.wait_ge(hot_q_ready, 2 * HALF * half + m + 1)
                    if k == 1:
                        pe.wait_ge(hot_r_more, HALF * half + i + 1)
                    elif i < POOL_HOTS:
                        pe.wait_ge(hot_r_ready, POOL_HOTS * half + i + 1)
                    else:
                        pe.wait_ge(hot_r_rest, (HALF - POOL_HOTS) * half + i - POOL_HOTS + 1)
                    ins = pe.matmul(banks[:, INV_BANK, 0:P], hot_q[:, k, i, :], hot_r[:, k, i, :],
                                    start=half == 0 and m == 0, stop=half == 1 and m == 2 * HALF - 1)
                if k == 1:
                    ins.then_inc(inv_ready, 1)

            pe.wait_ge(proj_out, len(PROJ) - 2)
            for step in range(NBLK + 1):
                if step == 1:
                    pe.wait_ge(proj_out, len(PROJ))
                if step < NBLK:
                    scores(step)
                if step == 1:
                    pe.wait_ge(gbias_ready, B)
                    pe.wait_ge(vt_split, UNITS)
                    pe.wait_ge(wo_split, 1)
                if step:
                    turn(step - 1)
                if step == 13:
                    turn_tokens(0)
                if step in (14, 15):
                    out_conv(1, step - 14)
                if step >= 5:
                    context((step - 5) // 4, (step - 5) % 4)
                if step in (9, 10):
                    out_conv(0, step - 9)
                if step == 13:
                    turn_tokens(1)
            context(3, 0)
            context(3, 1)
            out_conv(2, 0)
            out_conv(2, 1)
            context(3, 2)
            context(3, 3)
            logits(0)
            out_conv(3, 0)
            logits(1)
            out_conv(3, 1)
            turn_tokens(2)
            turn_tokens(3)
            logits(2)
            logits(3)
            turn_tokens(4)
            turn_tokens(5)
            logits(4)
            ranks(0)
            logits(5)
            turn_tokens(6)
            turn_tokens(7)
            logits(6)
            logits(7)
            inverse(0, 0)
            ranks(1)
            inverse(0, 1)
            inverse(1, 0)
            inverse(1, 1)
            pe.wait_ge(inv_taken, 1)
            pe.wait_ge(place_ready, 1)
            pe.matmul(banks[:, TABLE_BANK, 0:SLOTS], slot_t[:, :], place[:, :], start=True, stop=True
                      ).then_inc(table_ready, 1)

            def turn_x(n):
                pe.wait_ge(x_gathered, (n + 1) * (16 * WIDE))
                for i in range(WIDE):
                    for k in range(KC):
                        ins = pe.transpose(banks[:, 6 + k, i * P:(i + 1) * P], xg[:, i, k * P:(k + 1) * P],
                                           ident[:, :])
                ins.then_inc(xg_turned, 1)

            def layer1(t, e, j, width):
                pe.wait_ge(gelu_done, t * HJ + (j + 1))
                w = width * P
                for k in range(KC):
                    c = slice(k * H + j * P, k * H + (j + 1) * P)
                    ins = product3(banks[:, j % RING, 0:w], w_hi[e % 2][:, c], w_lo[e % 2][:, c], x_hi[:, k, 0:w],
                                   x_lo[:, k, 0:w], k == 0, k == KC - 1)
                ins.then_inc(l1_ready, 1)

            def layer2(t, e, j, width):
                pe.wait_ge(h_split, t * HJ + (j + 1 + RING))
                if j == 0:
                    pe.wait_ge(y_taken, t + 1)
                c = slice(KC * H + j * C, KC * H + (j + 1) * C)
                for i in range(width):
                    r = slice(i * P, (i + 1) * P)
                    out = banks[:, 4 + i % 2, i // 2 * C:(i // 2 + 1) * C]
                    pe.matmul(out, h_hi[:, j, r], w_hi[e % 2][:, c], start=j == 0 and i < 2, stop=False,
                              skip_group_check=width == WIDE)
                    pe.matmul(out, h_hi[:, j, r], w_lo[e % 2][:, c], start=False, stop=False,
                              skip_group_check=width == WIDE)
                    ins = pe.matmul(out, h_lo[:, j, r], w_hi[e % 2][:, c], start=False, stop=j == HJ - 1,
                                    skip_group_check=width == WIDE)
                ins.then_inc(l2_done, 1)

            def tile(t, e, width, new):
                pe.wait_ge(x_split, t + 1)
                if new:
                    pe.wait_ge(w_split, HJ * e + HJ // 2)
                for j in range(RING):
                    layer1(t, e, j, width)
                if new:
                    pe.wait_ge(w_split, HJ * (e + 1))
                for j in range(RING, HJ):
                    layer2(t, e, j - RING, width)
                    layer1(t, e, j, width)
                turn_x(t + 1)
                for j in range(HJ - RING, HJ):
                    layer2(t, e, j, width)

            pe.sem_inc(l2_done, HJ)
            pe.wait_ge(slots_ready, 2)
            for _ in range(10):
                pe.matmul(banks[:, 0, 0:P], ones[:, :], ones[:, :], start=True, stop=True)
            pe.wait_ge(bounds_ready, 2)
            t0 = 0
            turn_x(0)
            for _ in range(8):
                pe.matmul(banks[:, 0, 0:P], ones[:, :], ones[:, :], start=True, stop=True)
            for e in range(E):
                t1, odd, more = expert_bounds(pe, e)
                with pe.If(odd):
                    tile(t0, e, WIDE, True)
                with pe.Else():
                    tile(t0, e, 2, True)
                with pe.If(more):
                    with pe.Fori(t0 + 1, t1) as t:
                        tile(t, e, 2, False)
                t0 = t1


def kernel(**inputs):
    import numpy as np
    import concourse.bacc as bacc
    from concourse.bass_utils import run_bass_kernel_spmd

    a = {k.replace("L0_conv_", "").replace("L0_ffn_", ""): np.asarray(v) for k, v in inputs.items()}
    x = a["x"]
    shape = x.shape
    cn = np.ascontiguousarray(x.reshape(B, C, N))
    tok = np.ascontiguousarray(cn.transpose(0, 2, 1).reshape(TOK, C))
    aff = np.stack([a[n] for n in ("q_g1", "q_b1", "q_g2", "q_b2", "k_g1", "k_b1", "k_g2", "k_b2", "v_g", "v_b")],
                   axis=1)
    arrays = dict(
        x_cn=cn, x_tok=tok, q1=a["q_w1"].T, q2=a["q_w2"].T, k1=a["k_w1"].T, k2=a["k_w2"].T, v=a["v_w"].T,
        o=a["o_w"].T, aff=aff, og=a["o_g"], ob=a["o_b"], wg=a["Wg"], w1=a["W1"],
        b1=a["b1"].reshape(E, HJ, P).transpose(2, 0, 1).reshape(P, E * HJ), w2=a["W2"],
        b2=a["b2"].reshape(E * C))
    arrays = {f"in_{k}": np.ascontiguousarray(v) for k, v in arrays.items()}
    nc = bacc.Bacc("TRN2", target_bir_lowering=False, num_devices=1)
    args = [nc.dram_tensor(k, v.shape, mybir.dt.from_np(v.dtype), kind="ExternalInput").ap()
            for k, v in arrays.items()]
    out = nc.dram_tensor("out_rows", (TOK + TILE, C), F32, kind="ExternalOutput").ap()
    metaformer_kernel(nc, *args, out)
    rows = run_bass_kernel_spmd(nc, [arrays], core_ids=[0]).results[0]["out_rows"][:TOK]
    return np.ascontiguousarray(rows.reshape(B, N, C).transpose(0, 2, 1)).reshape(shape)
```
